# Optimizing a Trainium2 kernel written in Bass

```python
import numpy as np
import jax
import jax.numpy as jnp

def _softmax(x, axis=-1):
    return jax.nn.softmax(x, axis=axis)

def _gelu(x):
    return jax.nn.gelu(x, approximate=True)

def _silu(x):
    return jax.nn.silu(x)

def _sigmoid(x):
    return jax.nn.sigmoid(x)

def _layernorm(x, axis=-1, eps=1e-05):
    m = jnp.mean(x, axis=axis, keepdims=True)
    v = jnp.var(x, axis=axis, keepdims=True)
    return (x - m) / jnp.sqrt(v + eps)

def _scatter_add(tgt, idx, src, axis=0):
    return tgt.at[idx].add(src)

def _segment_sum(src, seg, n):
    return jax.ops.segment_sum(src, seg, n)
kernel_name = 'mk_flamingo_gated_d2_seqx_r8_e08ac3'

def setup_inputs(seed: int=0):
    np.random.seed(seed)
    _w = jnp.asarray

    def _rec_inputs():
        import jax
        import jax.numpy as jnp
        _rk = jax.random.key(seed)
        x = 7.22e-05 + 1 * jax.random.normal(jax.random.fold_in(_rk, 1), (16, 64, 256), jnp.float32)
        _lenS = 64 - jax.random.randint(jax.random.fold_in(_rk, 7), (16,), 0, max(1, 64 // 4) + 1, jnp.int32)
        _lenS2 = 64 - jax.random.randint(jax.random.fold_in(_rk, 8), (16,), 0, max(1, 64 // 4) + 1, jnp.int32)
        _ctx_2048P = jax.random.normal(jax.random.fold_in(_rk, 12), (16, 16, 256), jnp.float32)
        _ctx_2048c = jax.random.dirichlet(jax.random.fold_in(_rk, 512), 0.3 * jnp.ones((16,), jnp.float32), (16, 64))
        _ctx_2048t = jnp.einsum('bsk,bkd->bsd', _ctx_2048c, _ctx_2048P)
        _ctx_2048t = _ctx_2048t * jax.lax.rsqrt(jnp.mean(jnp.square(_ctx_2048t)) + 1e-12) * 0.953939
        ctx_2048 = 0.00424091 + 1.0017 * (_ctx_2048t + 0.3 * jax.random.normal(jax.random.fold_in(_rk, 612), (16, 64, 256), jnp.float32))
        _validS = jnp.arange(64)[None, :] < _lenS[:, None]
        _validS2 = jnp.arange(64)[None, :] < _lenS2[:, None]
        _causal = jnp.tril(jnp.ones((64, 64), dtype=bool))
        mask_Bx1xSxS_fk0 = jnp.where(jnp.broadcast_to(_validS[:, None, None, :], (16, 1, 64, 64)), -1000000000.0, 0.0).astype(jnp.float32)
        _g = jax.random.normal(jax.random.fold_in(_rk, 9001), (2, 2), jnp.float32)
        _g = jnp.sign(_g) * jnp.maximum(jnp.abs(_g), 1.0) + (_g == 0) * 1.0
        g_xattn = _g[0]
        g_ffn = _g[1]
        return (x, ctx_2048, mask_Bx1xSxS_fk0, g_xattn, g_ffn)
    x, ctx_2048, mask_Bx1xSxS_fk0, g_xattn, g_ffn = _rec_inputs()

    def _L0_xattn_setup():
        import jax, jax.numpy as jnp
        import numpy as np
        import math
        B, S, HID, H = (2, 256, 256, 32)
        D = HID // H
        AL = 10

        def _rope_tables(seq_len, dim, dtype):
            inv_freq = 1.0 / 10000.0 ** (np.arange(0, dim, 2, dtype=np.float32) / dim)
            t = np.arange(seq_len, dtype=np.float32)
            freqs = np.outer(t, inv_freq)
            emb = np.concatenate([freqs, freqs], -1)
            return (jnp.asarray(np.cos(emb), dtype), jnp.asarray(np.sin(emb), dtype))

        def _rotate_half(x):
            x1, x2 = jnp.split(x, 2, axis=-1)
            return jnp.concatenate([-x2, x1], axis=-1)
        key = jax.random.key(seed)
        ks = jax.random.split(key, 8)
        hidden_states = jax.random.normal(ks[0], (B, S, HID), dtype=jnp.float32)
        adapter = jax.random.normal(ks[1], (B, AL, HID), dtype=jnp.float32)
        causal = jnp.tril(jnp.ones((S, S), dtype=bool))
        attention_mask = jnp.broadcast_to(jnp.where(causal, 0.0, -1000000000.0).astype(jnp.float32)[None, None], (B, 1, S, S))
        scale = 0.02
        Wq = jax.random.normal(ks[2], (HID, HID), dtype=jnp.float32) * scale
        Wk = jax.random.normal(ks[3], (HID, HID), dtype=jnp.float32) * scale
        Wv = jax.random.normal(ks[4], (HID, HID), dtype=jnp.float32) * scale
        Wo = jax.random.normal(ks[5], (HID, HID), dtype=jnp.float32) * scale
        gate = jax.random.normal(ks[6], (1, H, 1, 1), dtype=jnp.float32) * 0.1
        return {'hidden_states': hidden_states, 'attention_mask': attention_mask, 'adapter': adapter, 'Wq': Wq, 'Wk': Wk, 'Wv': Wv, 'Wo': Wo, 'gate': gate}
    _L0_xattn_all = _L0_xattn_setup()
    _L0_xattn_in = {k: v for k, v in _L0_xattn_all.items() if k in ('Wq', 'Wk', 'Wv', 'Wo', 'gate')}
    del _L0_xattn_all

    def _L0_ffn_setup():
        import jax, jax.numpy as jnp
        import numpy as np
        B, S, H, E = (4, 256, 256, 8)
        key = jax.random.key(seed)
        k_x, k_wg, k_w, k_b = jax.random.split(key, 4)
        x = jax.random.normal(k_x, (B, S, H), dtype=jnp.float32)
        wg = jax.random.normal(k_wg, (H, E), dtype=jnp.float32) * (1.0 / np.sqrt(H))
        W = jax.random.normal(k_w, (E, H, H), dtype=jnp.float32) * (1.0 / np.sqrt(H))
        b = jax.random.normal(k_b, (E, H), dtype=jnp.float32) * 0.01
        return {'x': x, 'wg': wg, 'W': W, 'b': b}
    _L0_ffn_all = _L0_ffn_setup()
    _L0_ffn_in = {k: v for k, v in _L0_ffn_all.items() if k in ('wg', 'W', 'b')}
    del _L0_ffn_all

    def _L1_xattn_setup():
        import jax, jax.numpy as jnp
        import numpy as np
        B_DIM, T_DIM, C_DIM = (16, 128, 256)

        def _wkv(w, u, k, v):
            Bn, Tn, Cn = k.shape
            NEG_INF = jnp.float32(-1e+38)

            def step(carry, kv_t):
                p, q, o = carry
                kt, vt = kv_t
                no = jnp.maximum(o, u + kt)
                A = jnp.exp(o - no)
                E = jnp.exp(u + kt - no)
                y = (A * p + E * vt) / (A * q + E)
                no2 = jnp.maximum(w + o, kt)
                A2 = jnp.exp(w + o - no2)
                E2 = jnp.exp(kt - no2)
                return ((A2 * p + E2 * vt, A2 * q + E2, no2), y)
            init = (jnp.zeros((Bn, Cn), k.dtype), jnp.zeros((Bn, Cn), k.dtype), jnp.full((Bn, Cn), NEG_INF, k.dtype))
            kT = jnp.moveaxis(k, 1, 0)
            vT = jnp.moveaxis(v, 1, 0)
            _, yT = jax.lax.scan(step, init, (kT, vT))
            return jnp.moveaxis(yT, 0, 1)
        key = jax.random.key(seed)
        k1, k2, k3, k4 = jax.random.split(key, 4)
        w = -jnp.exp(jax.random.normal(k1, (C_DIM,), jnp.float32))
        u = jax.random.normal(k2, (C_DIM,), jnp.float32)
        k = jax.random.normal(k3, (B_DIM, T_DIM, C_DIM), jnp.float32)
        v = jax.random.normal(k4, (B_DIM, T_DIM, C_DIM), jnp.float32)
        return {'B': B_DIM, 'T': T_DIM, 'C': C_DIM, 'w': w, 'u': u, 'k': k, 'v': v}
    _L1_xattn_all = _L1_xattn_setup()
    _L1_xattn_in = {k: v for k, v in _L1_xattn_all.items() if k in ('w', 'u')}
    del _L1_xattn_all

    def _L1_ffn_setup():
        import jax, jax.numpy as jnp
        import numpy as np
        _Q_IN = 128
        _LUT_MIN = -128
        _Q_OUT = 1 << 16
        _TOP_K = 2
        _EXP_LUT = (jnp.exp(jnp.arange(_LUT_MIN, 1, dtype=jnp.float32) / _Q_IN) * _Q_OUT).astype(jnp.int32)

        def softmax_integer(logits):
            li = jnp.round(logits.astype(jnp.float32) * _Q_IN).astype(jnp.int32)
            shifted = jnp.clip(li - li.max(axis=-1, keepdims=True), _LUT_MIN, None)
            exp_vals = _EXP_LUT[shifted - _LUT_MIN]
            exp_sum = jnp.clip(exp_vals.sum(axis=-1, keepdims=True), 1, None)
            return exp_vals.astype(jnp.float32) / exp_sum.astype(jnp.float32)
        key = jax.random.key(seed)
        k0, k1, k2, k3, k4 = jax.random.split(key, 5)
        B, S, H, I, E = (4, 256, 256, 704, 8)
        x = jax.random.normal(k0, (B, S, H), dtype=jnp.float32)
        w_gate = jax.random.normal(k1, (E, H), dtype=jnp.float32) * 0.02
        w1 = jax.random.normal(k2, (E, I, H), dtype=jnp.float32) * 0.02
        w2 = jax.random.normal(k3, (E, H, I), dtype=jnp.float32) * 0.02
        w3 = jax.random.normal(k4, (E, I, H), dtype=jnp.float32) * 0.02
        return {'x': x, 'w_gate': w_gate, 'w1': w1, 'w2': w2, 'w3': w3}
    _L1_ffn_all = _L1_ffn_setup()
    _L1_ffn_in = {k: v for k, v in _L1_ffn_all.items() if k in ('w_gate', 'w1', 'w2', 'w3')}
    del _L1_ffn_all
    return {'x': x, 'ctx_2048': ctx_2048, 'mask_Bx1xSxS_fk0': mask_Bx1xSxS_fk0, 'g_xattn': g_xattn, 'g_ffn': g_ffn, 'L0_xattn_Wq': _L0_xattn_in['Wq'], 'L0_xattn_Wk': _L0_xattn_in['Wk'], 'L0_xattn_Wv': _L0_xattn_in['Wv'], 'L0_xattn_Wo': _L0_xattn_in['Wo'], 'L0_xattn_gate': _L0_xattn_in['gate'], 'L0_ffn_wg': _L0_ffn_in['wg'], 'L0_ffn_W': _L0_ffn_in['W'], 'L0_ffn_b': _L0_ffn_in['b'], 'L1_xattn_w': _L1_xattn_in['w'], 'L1_xattn_u': _L1_xattn_in['u'], 'L1_ffn_w_gate': _L1_ffn_in['w_gate'], 'L1_ffn_w1': _L1_ffn_in['w1'], 'L1_ffn_w2': _L1_ffn_in['w2'], 'L1_ffn_w3': _L1_ffn_in['w3']}

def reference(x, ctx_2048, mask_Bx1xSxS_fk0, g_xattn, g_ffn, L0_xattn_Wq, L0_xattn_Wk, L0_xattn_Wv, L0_xattn_Wo, L0_xattn_gate, L0_ffn_wg, L0_ffn_W, L0_ffn_b, L1_xattn_w, L1_xattn_u, L1_ffn_w_gate, L1_ffn_w1, L1_ffn_w2, L1_ffn_w3):
    import jax
    import jax.numpy as jnp

    def _L0_xattn_ref(hidden_states, attention_mask, adapter, Wq, Wk, Wv, Wo, gate):
        import jax, jax.numpy as jnp
        import numpy as np
        import math
        B, S, HID, H = (2, 256, 256, 32)
        D = HID // H
        AL = 10

        def _rope_tables(seq_len, dim, dtype):
            inv_freq = 1.0 / 10000.0 ** (np.arange(0, dim, 2, dtype=np.float32) / dim)
            t = np.arange(seq_len, dtype=np.float32)
            freqs = np.outer(t, inv_freq)
            emb = np.concatenate([freqs, freqs], -1)
            return (jnp.asarray(np.cos(emb), dtype), jnp.asarray(np.sin(emb), dtype))

        def _rotate_half(x):
            x1, x2 = jnp.split(x, 2, axis=-1)
            return jnp.concatenate([-x2, x1], axis=-1)
        bsz, q_len, hid = hidden_states.shape
        n_heads = gate.shape[1]
        head_dim = hid // n_heads
        inv_sqrt_d = 1.0 / math.sqrt(head_dim)

        def split_heads(x, length):
            return x.reshape(bsz, length, n_heads, head_dim).transpose(0, 2, 1, 3)
        q = split_heads(hidden_states @ Wq, q_len)
        k = split_heads(hidden_states @ Wk, q_len)
        v = split_heads(hidden_states @ Wv, q_len)
        cos, sin = _rope_tables(q_len, head_dim, q.dtype)
        q = q * cos + _rotate_half(q) * sin
        k = k * cos + _rotate_half(k) * sin
        scores = jnp.einsum('bhqd,bhkd->bhqk', q, k) * inv_sqrt_d
        scores = scores + attention_mask
        scores = jnp.maximum(scores, jnp.finfo(scores.dtype).min)
        w = jax.nn.softmax(scores.astype(jnp.float32), axis=-1).astype(q.dtype)
        attn_output = jnp.einsum('bhqk,bhkd->bhqd', w, v)
        adapter_len = adapter.shape[1]
        a_k = split_heads(adapter @ Wk, adapter_len)
        a_v = split_heads(adapter @ Wv, adapter_len)
        a_scores = jnp.einsum('bhqd,bhkd->bhqk', q, a_k) * inv_sqrt_d
        a_scores = jnp.tanh(gate) * jax.nn.softmax(a_scores.astype(jnp.float32), axis=-1).astype(q.dtype)
        attn_output = attn_output + jnp.einsum('bhqk,bhkd->bhqd', a_scores, a_v)
        attn_output = attn_output.transpose(0, 2, 1, 3).reshape(bsz, q_len, hid)
        return attn_output @ Wo

    def _L0_ffn_ref(x, wg, W, b):
        import jax, jax.numpy as jnp
        import numpy as np
        B, S, H, E = (4, 256, 256, 8)
        Bv, Sv, Hv = x.shape
        Ev = W.shape[0]
        xt = x.reshape(-1, Hv)
        logits = xt @ wg
        probs = jax.nn.softmax(logits, axis=-1)
        idx = jnp.argmax(probs, axis=-1)
        gate = jnp.take_along_axis(probs, idx[:, None], axis=1)
        onehot = jax.nn.one_hot(idx, Ev, dtype=x.dtype)
        expert_out = jnp.einsum('nh,eoh->neo', xt, W) + b[None, :, :]
        combine = onehot * gate
        out = jnp.einsum('ne,neo->no', combine, expert_out)
        return out.reshape(Bv, Sv, Hv)

    def _L1_xattn_ref(B, T, C, w, u, k, v):
        import jax, jax.numpy as jnp
        import numpy as np
        B_DIM, T_DIM, C_DIM = (16, 128, 256)

        def _wkv(w, u, k, v):
            Bn, Tn, Cn = k.shape
            NEG_INF = jnp.float32(-1e+38)

            def step(carry, kv_t):
                p, q, o = carry
                kt, vt = kv_t
                no = jnp.maximum(o, u + kt)
                A = jnp.exp(o - no)
                E = jnp.exp(u + kt - no)
                y = (A * p + E * vt) / (A * q + E)
                no2 = jnp.maximum(w + o, kt)
                A2 = jnp.exp(w + o - no2)
                E2 = jnp.exp(kt - no2)
                return ((A2 * p + E2 * vt, A2 * q + E2, no2), y)
            init = (jnp.zeros((Bn, Cn), k.dtype), jnp.zeros((Bn, Cn), k.dtype), jnp.full((Bn, Cn), NEG_INF, k.dtype))
            kT = jnp.moveaxis(k, 1, 0)
            vT = jnp.moveaxis(v, 1, 0)
            _, yT = jax.lax.scan(step, init, (kT, vT))
            return jnp.moveaxis(yT, 0, 1)
        return _wkv(w, u, k, v)

    def _L1_ffn_ref(x, w_gate, w1, w2, w3):
        import jax, jax.numpy as jnp
        import numpy as np
        _Q_IN = 128
        _LUT_MIN = -128
        _Q_OUT = 1 << 16
        _TOP_K = 2
        _EXP_LUT = (jnp.exp(jnp.arange(_LUT_MIN, 1, dtype=jnp.float32) / _Q_IN) * _Q_OUT).astype(jnp.int32)

        def softmax_integer(logits):
            li = jnp.round(logits.astype(jnp.float32) * _Q_IN).astype(jnp.int32)
            shifted = jnp.clip(li - li.max(axis=-1, keepdims=True), _LUT_MIN, None)
            exp_vals = _EXP_LUT[shifted - _LUT_MIN]
            exp_sum = jnp.clip(exp_vals.sum(axis=-1, keepdims=True), 1, None)
            return exp_vals.astype(jnp.float32) / exp_sum.astype(jnp.float32)
        orig_shape = x.shape
        H = orig_shape[-1]
        xf = x.reshape(-1, H)
        T = xf.shape[0]
        E = w_gate.shape[0]
        router_logits = xf @ w_gate.T
        routing_weights = softmax_integer(router_logits)
        top_w, top_i = jax.lax.top_k(routing_weights, _TOP_K)
        top_w = top_w / top_w.sum(axis=-1, keepdims=True)
        combine = jnp.zeros((T, E), xf.dtype).at[jnp.arange(T)[:, None], top_i].add(top_w)
        out = jnp.zeros_like(xf)
        for e in range(E):
            h = jax.nn.silu(xf @ w1[e].T) * (xf @ w3[e].T)
            out = out + combine[:, e:e + 1] * (h @ w2[e].T)
        return out.reshape(orig_shape)
    x = x + jnp.tanh(g_xattn[0]) * _L0_xattn_ref(_layernorm(x, axis=-1), mask_Bx1xSxS_fk0, ctx_2048, L0_xattn_Wq, L0_xattn_Wk, L0_xattn_Wv, L0_xattn_Wo, L0_xattn_gate)
    x = x + jnp.tanh(g_ffn[0]) * _L0_ffn_ref(_layernorm(x, axis=-1), L0_ffn_wg, L0_ffn_W, L0_ffn_b)
    x = x + jnp.tanh(g_xattn[1]) * _L1_xattn_ref(16, 64, 256, L1_xattn_w, L1_xattn_u, _layernorm(x, axis=-1), ctx_2048)
    x = x + jnp.tanh(g_ffn[1]) * _L1_ffn_ref(_layernorm(x, axis=-1), L1_ffn_w_gate, L1_ffn_w1, L1_ffn_w2, L1_ffn_w3)
    return x

_drawn_inputs = setup_inputs


def setup_inputs(seed=0):
    import zlib

    import numpy as np

    out = dict(_drawn_inputs(seed))
    spreads = {'g_ffn': (-1.0, 0.6)}
    factors = {'L0_xattn_Wq': 5.355,
     'L0_xattn_Wk': 6.559,
     'L0_xattn_gate': 4.15,
     'L0_ffn_b': 8.0,
     'L1_ffn_w_gate': 4.906,
     'L1_ffn_w1': 4.399,
     'L1_ffn_w2': 4.331,
     'L1_ffn_w3': 4.333}
    for name, (base, spread) in spreads.items():
        noise = np.random.default_rng([zlib.crc32(name.encode()), seed]).standard_normal(out[name].shape)
        drawn = base * np.exp(spread * noise) if base else spread * noise
        out[name] = jnp.asarray(drawn.astype(out[name].dtype))
    for name, factor in factors.items():
        out[name] = (out[name] * factor).astype(out[name].dtype)
    return out
```

```python
import math
from contextlib import ExitStack

import concourse.bass as bass
from concourse import mybir

F32 = mybir.dt.float32
F32R = mybir.dt.float32r
I32 = mybir.dt.int32
ALU = mybir.AluOpType
ACT = mybir.ActivationFunctionType
AX = mybir.AxisListType

B, S, HID, H = 16, 64, 256, 32
D = HID // H
P = 128
BT = 2
NT = B // BT
KT = HID // P
HG = 8
G = H // HG
NP = HG // 2
E0 = 8
NE = 8
VW = BT * 2 * (D + 1)
EPS = 1e-5
NEG_INF = -1e38

C_ID = 0
C_COSQ, C_SINQ, C_COSK, C_SINK = 128, 136, 144, 152
C_HM = 160
C_EV = 168
C_ONE = 176
C_TRI = C_ONE + 128
C_POS = C_TRI + 128
C_TOK = C_POS + 128
C_OWN = C_TOK + NT
C_J128 = C_OWN + 1
C_LUTX = C_J128 + NT
C_LUT = C_LUTX + 129
C_N = C_LUT + 129

TOPK = 2
I = 704
IH = I // 2
IT = -(-I // P)
NJ = (B * S * TOPK + NE * (P - 1)) // P
Q_IN, LUT_MIN, Q_OUT = 128.0, -128.0, 65536.0


def build(nc, A, out, H4):
    x_rows = A["x"].rearrange("b s h -> (b s) h").rearrange("(t p) h -> p t h", p=P)
    ctxT = A["ctxT"].rearrange("(c p) n -> p c n", p=P)
    mask_rows = A["mask"].rearrange("b o q k -> q (b o) k")
    out_rows = out[0:B * S, :].rearrange("(t p) h -> p t h", p=P)
    H4_rows = H4.rearrange("(t p) h -> p t h", p=P)

    ctx = ExitStack()
    with ctx:
        front = ExitStack()

        def keep(name, shape, dt=F32):
            return ctx.enter_context(nc.sbuf_tensor(name, shape, dt))

        def sb(name, shape, dt=F32):
            return front.enter_context(nc.sbuf_tensor(name, shape, dt))

        def sem(name):
            return ctx.enter_context(nc.semaphore(name))

        def bank(name):
            return ctx.enter_context(nc.psum_tensor(name, [P, 512], F32))

        LG = keep("LG", [P, NT, NE])
        CN = keep("CN", [P, C_N])
        tg = keep("tg", [P, 4])
        idx_in = keep("idx_in", [P, 1], I32)
        idx_out = keep("idx_out", [P, 1], I32)
        zrow = keep("zrow", [P, HID])
        X = sb("X", [P, NT, HID])
        CT = sb("CT", [P, KT, B * S])
        MK = sb("MK", [P, B, S])
        ident = CN[:, C_ID:C_ID + P]
        wq = sb("wq", [P, KT, HID])
        wkv = sb("wkv", [P, KT, 2 * HID])
        wo = sb("wo", [P, KT, HID])
        w0 = sb("w0", [P, KT, E0, HID])
        b0 = sb("b0", [E0, HID])
        wg0 = sb("wg0", [P, KT, E0])
        wg1 = sb("wg1", [P, KT, NE])
        wc = sb("wc", [P, KT])
        uc = sb("uc", [P, KT])
        nuc = sb("nuc", [P, KT])
        gts = sb("gts", [P, 4])
        hgr = sb("hgr", [P, H])
        thg = sb("thg", [P, H])
        Idup = sb("Idup", [P, P], F32R)
        Lm = sb("Lm", [P, P], F32R)
        mhalf = sb("mhalf", [P, 1])

        st = sb("st", [P, 4, 6])
        mv = sb("mv", [P, 4, 2])
        rstd = sb("rstd", [P, 4, 2])
        hn = sb("hn", [P, HID])
        HC = sb("HC", [P, KT, BT, P])
        qw = sb("qw", [P, HID])
        kw = sb("kw", [P, BT, HID])
        qt = sb("qt", [P, HID])
        qt2 = sb("qt2", [P, HID])
        qr = sb("qr", [P, G, 2, HG * D])
        kt1 = sb("kt1", [P, BT, HID])
        kt2 = sb("kt2", [P, BT, HID])
        kr = sb("kr", [P, BT, G, 2, HG * D])
        Vx = sb("Vx", [P, H, BT, 2, D + 1])
        qs = sb("qs", [P, G, BT, S], F32R)
        Qx = sb("Qx", [P, G, BT, HG, S], F32R)
        Kh = sb("Kh", [P, BT, G, P], F32R)
        Kl = sb("Kl", [P, BT, G, P], F32R)
        mk2 = sb("mk2", [P, BT, P], F32R)
        mx = sb("mx", [P, BT, 2, G, NP])
        mhl = sb("mhl", [BT * 2 * G * NP, 2, P], F32R)
        mrow = sb("mrow", [P, BT, H * S], F32R)
        Pt = sb("Pt", [P, H, BT, S])
        Oc = sb("Oc", [P, H, 2, D + 1])
        rec = sb("rec", [P, H, 2])
        On = sb("On", [P, 2, H, D])
        ao = sb("ao", [P, HID])
        aoT = sb("aoT", [P, KT, P])

        h2 = sb("h2", [P, HID])
        h2T = sb("h2T", [P, KT, P])
        lg = sb("lg", [P, 6, 8])
        comb = sb("comb", [P, E0])
        combT = sb("combT", [E0, P])
        h3 = sb("h3", [P, HID])
        kk = sb("kk", [P, KT * BT, S])
        Op = sb("Op", [P, KT * BT, S + 1])
        dd = sb("dd", [P, KT, BT * S])
        AR = sb("AR", [P, 2, 2, KT, BT * S])
        EX = sb("EX", [P, 2, KT, BT * S])
        VE = sb("VE", [P, 2, 2, KT * BT, S])
        PQ = sb("PQ", [P, 2, KT * BT, S + 1])
        ND = sb("ND", [P, 2, KT * BT, S])
        yy = sb("yy", [P, KT, BT * S])
        h4 = sb("h4", [P, HID])
        h4T = sb("h4T", [P, KT, P])
        front.close()

        w13 = keep("w13", [P, KT, NE, 4, IH])
        w2 = keep("w2", [P, IT, NE, HID])
        ones = keep("ones", [P, P])
        li = keep("li", [P, NT, NE], I32)
        sc = keep("sc", [P, NT, NE])
        key = keep("key", [P, NT, NE])
        key2 = keep("key2", [P, NT, NE])
        oh = keep("oh", [P, TOPK, NT, NE])
        tmp = keep("tmp", [P, TOPK, NT, NE])
        small = keep("small", [P, 16, NT])
        lutx = keep("lutx", [P, NT, 129])
        used = keep("used", [P, NT, NE])
        rank = keep("rank", [P, NT, NE])
        cum = keep("cum", [P, NT + 1, NE])
        gtj = keep("gtj", [P, NE, NT])
        ex = keep("ex", [P, 4, NE])
        slot = keep("slot", [P, TOPK * NT])
        slot_i = keep("slot_i", [P, TOPK * NT], I32)
        jt_i = keep("jt_i", [P, TOPK * NT], I32)
        pos_i = keep("pos_i", [P, TOPK * NT], I32)
        jt = keep("jt", [P, TOPK * NT])
        pos = keep("pos", [P, TOPK * NT])
        wts = keep("wts", [P, TOPK * NT])
        ohp = keep("ohp", [P, TOPK * NT, P])
        val = keep("val", [P, TOPK * NT, 3, NJ])
        tb = keep("tb", [P, 3, NJ])
        gi = keep("gi", [P, NJ], I32)
        so = keep("so", [P, NJ])
        si = keep("si", [P, NJ], I32)
        ejc = keep("ejc", [1, NJ, NE])
        ejs = keep("ejs", [1, NJ])
        ej = keep("ej", [1, NJ], I32)
        xg = keep("xg", [P, HID])
        xgT = keep("xgT", [P, KT, P])
        sg = keep("sg", [P, 2, IH])
        hh = keep("hh", [P, IT * P])
        hT = keep("hT", [P, IT, P])
        ys = keep("ys", [P, HID])

        bs = [bank(f"bank_s{i}") for i in range(2)]
        bt = [bank(f"bank_t{i}") for i in range(2)]
        bo, ba, bb, bc = bank("bank_o"), bank("bank_a"), bank("bank_b"), bank("bank_c")

        ld_const, ld_x, ld_attn, ld_ffn = sem("ld_const"), sem("ld_x"), sem("ld_attn"), sem("ld_ffn")
        zeroed, prep, prep_act = sem("zeroed"), sem("prep"), sem("prep_act")
        ln_sync = [sem(f"ln{i}_sync") for i in range(4)]
        dve_g = sem("dve_g")
        held = sem("held")
        ln_stat = [sem(f"ln{i}_stat") for i in range(4)]
        ln_rstd = [sem(f"ln{i}_rstd") for i in range(4)]
        ln_done = [sem(f"ln{i}_done") for i in range(4)]
        hnT, hc_self, hc_ctx = sem("hnT"), sem("hc_self"), sem("hc_ctx")
        q_in, k_in = sem("q_in"), sem("k_in")
        q_mm, kv_mm, q_rot, k_rot, v_in = sem("q_mm"), sem("kv_mm"), sem("q_rot"), sem("k_rot"), sem("v_in")
        qT, kT, q_hi, k_hi, q_lo, k_lo = sem("qT"), sem("kT"), sem("q_hi"), sem("k_hi"), sem("q_lo"), sem("k_lo")
        qx, mk_in = sem("qx"), sem("mk_in")
        s_mm, s_max, mT, m_hi, m_lo, m_row = sem("s_mm"), sem("s_max"), sem("mT"), sem("m_hi"), sem("m_lo"), sem("m_row")
        t_mm, p_exp, pv_mm, o_in, ao_in = sem("t_mm"), sem("p_exp"), sem("pv_mm"), sem("o_in"), sem("ao_in")
        aoT_mm, aoT_in, wo_mm, x1_in = sem("aoT_mm"), sem("aoT_in"), sem("wo_mm"), sem("x1_in")
        h2T_mm, h2T_in, lg_mm, l_max, l_exp, comb_in = (sem(n) for n in ("h2T_mm", "h2T_in", "lg_mm", "l_max", "l_exp", "comb_in"))
        combT_mm, combT_in, e_mm, e_add = sem("combT_mm"), sem("combT_in"), sem("e_mm"), sem("e_add")
        h3T_mm, kk_in, arg_in, dec_exp, ev_in = sem("h3T_mm"), sem("kk_in"), sem("arg_in"), sem("dec_exp"), sem("ev_in")
        y_in, yT_mm, x3_in = sem("y_in"), sem("yT_mm"), sem("x3_in")
        h4T_mm, h4T_in, rl_mm, rl_in, x_out = sem("h4T_mm"), sem("h4T_in"), sem("rl_mm"), sem("rl_in"), sem("x_out")
        dve_a, dve_c, dve_e, dve_f, pool_a, pool_l = (sem(n) for n in ("dve_a", "dve_c", "dve_e", "dve_f", "pool_a", "pool_l"))

        ld_w13, ld_w2, h4_out, z_out, zr = sem("ld_w13"), sem("ld_w2"), sem("h4_out"), sem("z_out"), sem("zr")
        dve_r, rk_mm, tb_mm, route, e_of = sem("dve_r"), sem("rk_mm"), sem("tb_mm"), sem("route"), sem("e_of")
        used_in, val_in = sem("used_in"), sem("val_in")
        idx_cp, gathered, xT_mm, xT_in, up_mm, silu, h_in = (sem(n) for n in ("idx_cp", "gathered", "xT_mm", "xT_in", "up_mm", "silu", "h_in"))
        hT_mm, hT_in_a, hT_in_v, y_mm, y_sc, added, idx_cp2 = (sem(n) for n in ("hT_mm", "hT_in_a", "hT_in_v", "y_mm", "y_sc", "added", "idx_cp2"))

        block = ctx.enter_context(nc.Block())

        def after(eng, s, t, per, n):
            if isinstance(t, int):
                if t * per + n > 0:
                    eng.wait_ge(s, t * per + n)
            else:
                eng.wait_ge(s, t * per + n)

        class Chain:

            def __init__(self, eng, s, t, per):
                self.eng, self.s, self.t, self.per, self.n = eng, s, t, per, 0

            def __call__(self, ins):
                self.n += 1
                ins.then_inc(self.s, 1)
                self.eng.wait_ge(self.s, self.t * self.per + self.n)

            def end(self):
                assert self.n == self.per, self.n

        @block.sync
        def _(sp):
            sp.dma_start(CN[:, :], A["const"]).then_inc(ld_const, 16)
            sp.dma_start(X[:, :, :], x_rows).then_inc(ld_x, 16)
            for name, dst in (("Wq", wq), ("Wkv", wkv), ("Wo", wo)):
                sp.dma_start(dst[:, :, :], A[name].rearrange("(c p) n -> p c n", p=P)).then_inc(ld_attn, 16)
            sp.dma_start(CT[:, :, :], ctxT).then_inc(ld_attn, 16)
            for half in range(2):
                sp.dma_start(MK[half * S:(half + 1) * S, :, :], mask_rows).then_inc(ld_attn, 16)
            sp.dma_start(gts[:, 0:4], A["gates"].partition_broadcast(P)).then_inc(ld_attn, 16)
            sp.dma_start(hgr[:, :], A["head_gate"].partition_broadcast(P)).then_inc(ld_attn, 16)
            sp.dma_start(wc[:, :], A["w"]).then_inc(ld_ffn, 16)
            sp.dma_start(uc[:, :], A["u"]).then_inc(ld_ffn, 16)
            sp.dma_start(b0[:, :], A["b"]).then_inc(ld_ffn, 16)
            sp.dma_start(wg0[:, :, :], A["wg"].rearrange("(c p) n -> p c n", p=P)).then_inc(ld_ffn, 16)
            sp.dma_start(wg1[:, :, :], A["wgateT"].rearrange("(c p) n -> p c n", p=P)).then_inc(ld_ffn, 16)
            for c in range(KT):
                sp.dma_start(w0[:, c, :, :], A["WT"][:, c * P:(c + 1) * P, :].rearrange("e p n -> p e n")).then_inc(ld_ffn, 16)

            sp.wait_ge(zeroed, 8)

            def shift_rows(t):
                after(sp, m_lo, t, 1, 1)
                after(sp, t_mm, t - 1, 8, 8)
                for b in range(BT):
                    for hl in range(2):
                        for s in range(2):
                            r = 2 * hl + s
                            sp.dma_start(mrow[r:r + 1, b, :].rearrange("o (g x) -> o g x", x=P).bitcast(F32),
                                         mhl[32 * b + 16 * s:32 * b + 16 * s + 16, hl, :].bitcast(F32)).then_inc(m_row, 16)

            sp.wait_ge(zr, 1)
            sp.dma_start(out[B * S:B * S + P, :], zrow[:, :]).then_inc(z_out, 16)

            def store(u):
                after(sp, x3_in, u, 1, 1)
                sp.dma_start(out_rows[:, u, :], X[:, u, :]).then_inc(x_out, 16)
                after(sp, ln_done[3], u, 1, 1)
                sp.dma_start(H4_rows[:, u, :], h4[:, :]).then_inc(h4_out, 16)

            shift_rows(0)
            with sp.Fori(1, NT) as t:
                shift_rows(t)
                store(t - 1)
            store(NT - 1)
            sp.wait_ge(x_out, 16 * NT)
            sp.wait_ge(h4_out, 16 * NT)
            sp.wait_ge(rl_in, NT)
            for e in range(NE):
                for c in range(KT):
                    sp.dma_start(w13[:, c, e, :, :], A["w13"][e, c * P:(c + 1) * P, :, :]).then_inc(ld_w13, 16)
            for e in range(NE):
                sp.dma_start(w2[:, 0:IT - 1, e, :], A["w2T"][e, 0:(IT - 1) * P, :].rearrange("(i p) n -> p i n", p=P)).then_inc(ld_w2, 16)
                sp.dma_start(w2[0:I - (IT - 1) * P, IT - 1, e, :], A["w2T"][e, (IT - 1) * P:I, :]).then_inc(ld_w2, 16)
            sp.wait_ge(z_out, 16)
            sp.wait_ge(added, 16 * NJ)

        @block.gpsimd
        def _(pool):
            pool.memset(mhalf[:, :], -0.5).then_inc(zeroed, 1)
            pool.wait_ge(zeroed, 8)

            def rstd_of(n, t, k):
                after(pool, ln_stat[n], t, 1, 1)
                pool.sem_inc(held, 1)
                pool.tensor_scalar_add(rstd[:, n, 0:1], mv[:, n, 1:2], EPS).then_inc(pool_l, 1)
                pool.wait_ge(pool_l, k)
                pool.tensor_tensor(rstd[:, n, 1:2], rstd[:, n, 0:1], mhalf[:, :], ALU.pow).then_inc(ln_rstd[n], 1)

            def ctx_and_mask(t):
                after(pool, kv_mm, t - 1, BT, BT)
                for c in range(KT):
                    pool.tensor_copy(HC[:, c, :, S:P], CT[:, c, bass.ts(t, P)].rearrange("p (b k) -> p b k", b=BT)).then_inc(hc_ctx, 1)
                after(pool, t_mm, t - 1, 8, 8)
                pool.tensor_copy(mk2[:, :, 0:S], MK[:, bass.ts(t, BT), :]).then_inc(pool_a, 1)

            def spread(t):
                after(pool, q_lo, t, 1, 1)
                after(pool, t_mm, t - 1, 8, 8)
                hm = CN[:, C_HM:C_HM + HG]
                for g in range(G):
                    for b in range(BT):
                        ins = pool.tensor_tensor(
                            Qx[:, g, b, :, :],
                            qs[:, g, b, :].bitcast(F32).rearrange("p (o q) -> p o q", o=1).to_broadcast([P, HG, S]),
                            hm.rearrange("p (h o) -> p h o", o=1).to_broadcast([P, HG, S]), ALU.mult)
                    ins.then_inc(qx, 1)

            def ev(u):
                after(pool, dec_exp, u, 3, 3)
                v = CT[:, :, bass.ts(u, P)]
                for i in range(2):
                    pool.tensor_tensor(VE[:, i, 0, :, :].rearrange("p (c b) s -> p c (b s)", c=KT),
                                       VE[:, i, 1, :, :].rearrange("p (c b) s -> p c (b s)", c=KT), v,
                                       ALU.mult).then_inc(ev_in, 1)

            pool.wait_ge(ld_attn, 16 * 8)
            pool.wait_ge(ld_const, 16)
            rstd_of(0, 0, 1)
            ctx_and_mask(0)
            spread(0)
            rstd_of(1, 0, 2)
            with pool.Fori(1, NT) as t:
                rstd_of(0, t, 4 * t + (-1))
                ctx_and_mask(t)
                spread(t)
                rstd_of(2, t - 1, 4 * t)
                ev(t - 1)
                rstd_of(3, t - 1, 4 * t + 1)
                rstd_of(1, t, 4 * t + 2)
            rstd_of(2, NT - 1, 4 * NT - 1)
            ev(NT - 1)
            rstd_of(3, NT - 1, 4 * NT)

            def gather(j):
                after(pool, xT_mm, j - 1, 1, 1)
                pool.tensor_copy(idx_in[:, :], gi[:, bass.ts(j, 1)]).then_inc(idx_cp, 1)
                after(pool, idx_cp, j, 1, 1)
                pool.sem_inc(held, 1)
                pool.indirect_dma_start(xg[:, :], None, H4, bass.IndirectOffsetOnAxis(ap=idx_in[:, :], axis=0)).then_inc(gathered, 16)

            def add(j):
                after(pool, added, j - 1, 16, 16)
                pool.tensor_copy(idx_out[:, :], si[:, bass.ts(j, 1)]).then_inc(idx_cp2, 1)
                after(pool, idx_cp2, j, 1, 1)
                after(pool, y_sc, j, 1, 1)
                pool.sem_inc(held, 1)
                pool.indirect_dma_start(out, bass.IndirectOffsetOnAxis(ap=idx_out[:, :], axis=0), ys[:, :], None,
                                        compute_op=ALU.add).then_inc(added, 16)

            pool.wait_ge(route, 2)
            pool.wait_ge(h4_out, 16 * NT)
            pool.wait_ge(x_out, 16 * NT)
            pool.wait_ge(z_out, 16)
            gather(0)
            gather(1)
            with pool.Fori(1, NJ - 1) as j:
                gather(j + 1)
                add(j - 1)
            add(NJ - 2)
            add(NJ - 1)

        @block.scalar
        def _(act):
            def copy(dst, src, scale=1.0):
                return act.activation(dst, src, ACT.Copy, scale=scale)

            act.wait_ge(ld_attn, 16 * 8)
            act.activation(tg[:, :], gts[:, :], ACT.Tanh).then_inc(prep_act, 1)
            act.activation(thg[:, :], hgr[:, :], ACT.Tanh).then_inc(prep_act, 1)
            act.wait_ge(zeroed, 8)

            def evac_hn(t):
                after(act, hnT, t, 1, 1)
                after(act, kv_mm, t - 1, BT, BT)
                copy(HC[:, :, :, 0:S], ba[:, 0:KT * P].rearrange("p (c b s) -> p c b s", c=KT, b=BT)).then_inc(hc_self, 1)

            def evac_v(t):
                after(act, q_mm, t, 1, 1)
                after(act, q_rot, t - 1, 1, 1)
                copy(qw[:, :], bb[:, 0:HID]).then_inc(q_in, 1)
                after(act, pv_mm, t - 1, G, G)
                after(act, k_rot, t - 1, BT, BT)
                for b in range(BT):
                    after(act, kv_mm, t, BT, b + 1)
                    copy(kw[:, b, :], (bc, ba)[b][:, 0:HID]).then_inc(k_in, 1)
                    src = (bc, ba)[b][:, HID:2 * HID].rearrange("p (h d) -> p h d", h=H)
                    for s in range(2):
                        r = slice(S * s, S * s + S)
                        copy(Vx[r, :, b, s, 0:D], src[r]).then_inc(v_in, 1)

            def evac_qk(t):
                after(act, qT, t, 1, 1)
                after(act, qx, t - 1, G, G)
                copy(qs[:, :, :, :], bb[:, :].rearrange("p (g b s) -> p g b s", g=G, b=BT)).then_inc(q_hi, 1)
                after(act, t_mm, t - 1, 8, 8)
                for b in range(BT):
                    after(act, kT, t, BT, b + 1)
                    copy(Kh[:, b, :, :], (bc, ba)[b][:, :].rearrange("p (g k) -> p g k", g=G)).then_inc(k_hi, 1)

            def shifts(t):
                after(act, m_row, t - 1, BT * 64, BT * 64)
                after(act, mT, t, 1, 1)
                copy(mhl[:, 0, :], bb[0:2 * H, 0:P], -1.0).then_inc(m_hi, 1)

            def attend(t):
                for g in range(G):
                    for b in range(BT):
                        after(act, t_mm, t, 8, 2 * g + b + 1)
                        if b == 0:
                            after(act, pv_mm, t - 1, G, g + 1)
                        act.activation(Pt[:, g * HG:(g + 1) * HG, b, :], bt[b][:, :].rearrange("p (h q) -> p h q", h=HG),
                                       ACT.Exp).then_inc(p_exp, 1)
                    if g >= 1:
                        heads_out(t, g - 1)
                heads_out(t, G - 1)

            def heads_out(t, g):
                after(act, pv_mm, t, G, g + 1)
                if g == 0:
                    after(act, ao_in, t - 1, 1, 1)
                src = bo[:, 0:HG * VW].rearrange("p (h b s d) -> p h b s d", h=HG, b=BT, s=2)
                for b in range(BT):
                    r = slice(S * b, S * b + S)
                    copy(Oc[r, g * HG:(g + 1) * HG, :, :], src[r, :, b, :, :]).then_inc(o_in, 1)

            def evac_ao(t):
                after(act, aoT_mm, t, 1, 1)
                copy(aoT[:, :, :], bc[:, 0:KT * P].rearrange("p (c n) -> p c n", c=KT)).then_inc(aoT_in, 1)

            def gate(u):
                after(act, h2T_mm, u, 1, 1)
                copy(h2T[:, :, :], bt[0][:, 0:KT * P].rearrange("p (c n) -> p c n", c=KT)).then_inc(h2T_in, 1)
                after(act, l_max, u, 1, 1)
                act.activation(lg[:, 1, :], lg[:, 3, :], ACT.Exp, bias=lg[:, 0, 1:2],
                               accum_out=lg[:, 0, 2:3]).then_inc(l_exp, 1)

            def evac_comb(u):
                after(act, combT_mm, u, 1, 1)
                copy(combT[:, :], bt[1][0:E0, P:2 * P]).then_inc(combT_in, 1)

            def evac_kk(u):
                after(act, h3T_mm, u, 1, 1)
                copy(kk[:, :, :], bc[:, 0:KT * P].rearrange("p (c s) -> p c s", c=KT * BT)).then_inc(kk_in, 1)

            def decay(u):
                after(act, arg_in, u, 1, 1)
                act.activation(EX[:, :, :, :], AR[:, 0, :, :, :], ACT.Exp).then_inc(dec_exp, 1)
                for i in range(2):
                    act.activation(VE[:, i, 1, :, :].rearrange("p (c b) s -> p c (b s)", c=KT), AR[:, 1, i, :, :], ACT.Exp,
                                   scale=-1.0).then_inc(dec_exp, 1)

            def evac_h4(u):
                after(act, h4T_mm, u, 1, 1)
                copy(h4T[:, :, :], bb[:, 0:KT * P].rearrange("p (c n) -> p c n", c=KT)).then_inc(h4T_in, 1)

            evac_hn(0)
            evac_v(0)
            evac_qk(0)
            shifts(0)
            attend(0)
            evac_ao(0)
            with act.Fori(1, NT) as t:
                evac_hn(t)
                gate(t - 1)
                evac_v(t)
                evac_qk(t)
                evac_comb(t - 1)
                evac_kk(t - 1)
                shifts(t)
                decay(t - 1)
                attend(t)
                evac_h4(t - 1)
                evac_ao(t)
            gate(NT - 1)
            evac_comb(NT - 1)
            evac_kk(NT - 1)
            decay(NT - 1)
            evac_h4(NT - 1)

            def rows_in(j):
                after(act, xT_mm, j, 1, 1)
                after(act, up_mm, j - 1, 4, 4)
                copy(xgT[:, :, :], ba[:, 0:KT * P].rearrange("p (c n) -> p c n", c=KT)).then_inc(xT_in, 1)

            def h_turned(j):
                after(act, hT_mm, j, 2, 1)
                after(act, y_mm, j - 1, 1, 1)
                copy(hT[:, 0:4, :], bb[:, :].rearrange("p (i n) -> p i n", i=4)).then_inc(hT_in_a, 1)

            def gates(j):
                for i in range(2):
                    after(act, up_mm, j, 4, 2 * i + 1)
                    after(act, h_in, j - 1, 2, i + 1)
                    act.activation(sg[:, i, :], (bs[0], bt[0])[i][:, 0:IH], ACT.Silu).then_inc(silu, 1)

            def scaled(j):
                after(act, y_mm, j, 1, 1)
                after(act, added, j - 1, 16, 16)
                act.activation(ys[:, :], bo[:, 0:HID], ACT.Copy, scale=tb[:, 1, bass.ts(j, 1)]).then_inc(y_sc, 1)

            act.wait_ge(route, 2)
            rows_in(0)
            gates(0)
            with act.Fori(1, NJ) as j:
                rows_in(j)
                h_turned(j - 1)
                gates(j)
                scaled(j - 1)
            h_turned(NJ - 1)
            scaled(NJ - 1)

        @block.vector
        def _(dve):
            dve.memset(zrow[:, :], 0.0).then_inc(zr, 1)
            dve.memset(Vx[:, :, :, :, :], 0.0).then_inc(zeroed, 1)
            dve.memset(mk2[:, :, :].bitcast(F32), 0.0).then_inc(zeroed, 1)
            dve.memset(mrow[:, :, :].bitcast(F32), 0.0).then_inc(zeroed, 1)
            dve.memset(Op[:, :, 0:1], NEG_INF).then_inc(zeroed, 1)
            dve.memset(PQ[:, :, :, 0:1], 0.0).then_inc(zeroed, 1)
            dve.wait_ge(zeroed, 6)
            dve.memset(Vx[0:S, :, :, 0, D:D + 1], 1.0).then_inc(zeroed, 1)
            dve.memset(Vx[S:P, :, :, 1, D:D + 1], 1.0).then_inc(zeroed, 1)
            dve.wait_ge(ld_const, 16)
            dve.wait_ge(ld_x, 16)
            dve.tensor_tensor(Idup[:, 0:S], CN[:, C_ID:C_ID + S], CN[:, C_ID + S:C_ID + P], ALU.add).then_inc(prep, 1)
            dve.tensor_tensor(Idup[:, S:P], CN[:, C_ID:C_ID + S], CN[:, C_ID + S:C_ID + P], ALU.add).then_inc(prep, 1)
            dve.tensor_copy(Lm[:, :], CN[:, C_ONE:C_ONE + P]).then_inc(prep, 1)
            dve.wait_ge(ld_ffn, 16 * 7)
            dve.tensor_scalar(nuc[:, :], uc[:, :], -1.0, None, ALU.mult).then_inc(prep, 1)
            dve.wait_ge(prep_act, 2)
            dve.wait_ge(prep, 4)

            def layer_norm(n, t, src, dst):
                dve.sem_inc(held, 1)
                dve.bn_stats(st[:, n, :], src).then_inc(ln_sync[n], 1)
                after(dve, ln_sync[n], t, 1, 1)
                dve.sem_inc(held, 1)
                dve.bn_aggr(mv[:, n, :], st[:, n, :]).then_inc(ln_stat[n], 1)
                after(dve, ln_rstd[n], t, 1, 1)
                after(dve, ln_stat[n], t, 1, 1)
                dve.tensor_scalar(dst, src, mv[:, n, 0:1], rstd[:, n, 1:2], ALU.subtract, ALU.mult).then_inc(ln_done[n], 1)

            def norm1(t):
                after(dve, hnT, t - 1, 1, 1)
                layer_norm(0, t, X[:, t, :], hn[:, :])

            def twice(ap):
                return ap.rearrange("p (g o d) -> p g o d", g=G, o=1).to_broadcast([P, G, 2, HG * D])

            def rope(src, cos, sin, t1, t2):
                v = src.rearrange("p (h d) -> p h d", h=H)

                def bc3(c, n):
                    return c.rearrange("p (o d) -> p o d", o=1).to_broadcast([P, H, n])

                a = t1.rearrange("p (h d) -> p h d", h=H)
                z = t2.rearrange("p (h d) -> p h d", h=H)
                h = D // 2
                dve.tensor_tensor(a, v, bc3(CN[:, cos:cos + D], D), ALU.mult)
                dve.tensor_tensor(z[:, :, 0:h], v[:, :, h:D], bc3(CN[:, sin:sin + h], h), ALU.mult)
                return dve.tensor_tensor(z[:, :, h:D], v[:, :, 0:h], bc3(CN[:, sin + h:sin + D], h), ALU.mult)

            def rotate(t):
                link = Chain(dve, dve_a, t, 1 + BT)
                after(dve, q_in, t, 1, 1)
                link(rope(qw[:, :], C_COSQ, C_SINQ, qt[:, :], qt2[:, :]))
                after(dve, qT, t - 1, 1, 1)
                dve.tensor_tensor(qr[:, :, :, :], twice(qt[:, :]), twice(qt2[:, :]), ALU.add).then_inc(q_rot, 1)
                for b in range(BT):
                    after(dve, k_in, t, BT, b + 1)
                    link(rope(kw[:, b, :], C_COSK, C_SINK, kt1[:, b, :], kt2[:, b, :]))
                    after(dve, kT, t - 1, BT, BT)
                    dve.tensor_tensor(kr[:, b, :, :, :], twice(kt1[:, b, :]), twice(kt2[:, b, :]), ALU.add).then_inc(k_rot, 1)
                link.end()

            def low_parts(t):
                after(dve, q_hi, t, 1, 1)
                dve.tensor_tensor(qs[S:P, :, :, :], bb[S:P, :].rearrange("p (g b s) -> p g b s", g=G, b=BT),
                                  qs[S:P, :, :, :].bitcast(F32), ALU.subtract).then_inc(q_lo, 1)
                after(dve, t_mm, t - 1, 8, 8)
                for b in range(BT):
                    after(dve, k_hi, t, BT, b + 1)
                    dve.tensor_tensor(Kl[:, b, :, :], (bc, ba)[b][:, :].rearrange("p (g k) -> p g k", g=G),
                                      Kh[:, b, :, :].bitcast(F32), ALU.subtract).then_inc(k_lo, 1)

            def mask_low(t):
                after(dve, pool_a, t, 1, 1)
                dve.tensor_tensor(mk2[S:P, :, 0:S], MK[S:P, bass.ts(t, BT), :], mk2[S:P, :, 0:S].bitcast(F32),
                                  ALU.subtract).then_inc(mk_in, 1)

            def maxima(t):
                mask_low(t)
                for b in range(BT):
                    for g in range(G):
                        n = G * b + g
                        after(dve, s_mm, t, 8, n + 1)
                        if n == 0:
                            after(dve, mT, t - 1, 1, 1)
                        dve.tensor_reduce(mx[:, b, :, g, :].rearrange("p s n -> p n s"),
                                          bs[n % 2][:, :].rearrange("p (n s k) -> p n s k", n=NP, s=2),
                                          AX.X, ALU.max).then_inc(s_max, 1)

            def shift_low(t):
                after(dve, m_row, t - 1, BT * 64, BT * 64)
                after(dve, m_hi, t, 1, 1)
                dve.scalar_tensor_tensor(mhl[:, 1, :], bb[0:2 * H, 0:P], -1.0, mhl[:, 0, :].bitcast(F32),
                                         ALU.mult, ALU.subtract).then_inc(m_lo, 1)

            def heads(t):
                link = Chain(dve, dve_c, t, 3)
                after(dve, o_in, t, 8, 8)
                link(dve.reciprocal(rec[:, :, :], Oc[:, :, :, D]))
                link(dve.tensor_tensor(rec[:, :, 1], rec[:, :, 1], thg[:, :], ALU.mult))
                for s in range(2):
                    ins = dve.tensor_tensor(On[:, s, :, :], Oc[:, :, s, 0:D],
                                            rec[:, :, s:s + 1].to_broadcast([P, H, D]), ALU.mult)
                link(ins)
                after(dve, aoT_mm, t - 1, 1, 1)
                dve.tensor_tensor(ao[:, :].rearrange("p (h d) -> p h d", h=H), On[:, 0, :, :], On[:, 1, :, :],
                                  ALU.add).then_inc(ao_in, 1)
                link.end()

            def residual1(t):
                after(dve, wo_mm, t, 1, 1)
                dve.scalar_tensor_tensor(X[:, t, :], ba[:, 0:HID], tg[:, 0:1], X[:, t, :], ALU.mult, ALU.add).then_inc(x1_in, 1)
                after(dve, x1_in, t, 1, 1)
                after(dve, h2T_mm, t - 1, 1, 1)
                layer_norm(1, t, X[:, t, :], h2[:, :])

            def gate(u):
                link = Chain(dve, dve_e, u, 5 + E0)
                after(dve, lg_mm, u, 1, 1)
                l = lg[:, 3, :]
                link(dve.tensor_copy(l, bt[1][:, 0:E0]))
                link(dve.tensor_reduce(lg[:, 0, 0:1], l, AX.X, ALU.max))
                dve.tensor_scalar(lg[:, 0, 1:2], lg[:, 0, 0:1], -1.0, None, ALU.mult).then_inc(l_max, 1)
                link(dve.scalar_tensor_tensor(lg[:, 2, :], l, lg[:, 0, 0:1], CN[:, C_EV:C_EV + 8], ALU.is_equal, ALU.mult))
                link(dve.tensor_reduce(lg[:, 0, 3:4], lg[:, 2, :], AX.X, ALU.max))
                after(dve, l_exp, u, 1, 1)
                dve.reciprocal(lg[:, 0, 4:5], lg[:, 0, 2:3]).then_inc(dve_g, 1)
                after(dve, dve_g, u, 1, 1)
                link(dve.tensor_scalar(lg[:, 0, 5:6], lg[:, 0, 4:5], tg[:, 1:2], None, ALU.mult))
                after(dve, combT_mm, u - 1, 1, 1)
                dve.tensor_scalar(comb[:, :], lg[:, 2, :], lg[:, 0, 3:4], lg[:, 0, 5:6], ALU.is_equal, ALU.mult).then_inc(comb_in, 1)
                assert link.n == 5

            def mix(u):
                link = Chain(dve, dve_e, u, 5 + E0)
                link.n = 5
                after(dve, comb_in, u, 1, 1)
                for n in range(E0 // 2):
                    after(dve, e_mm, u, 5, n + 1)
                    for j in range(2):
                        e = 2 * n + j
                        ins = dve.scalar_tensor_tensor(X[:, u, :], bt[n % 2][:, j * HID:(j + 1) * HID], comb[:, e:e + 1],
                                                       X[:, u, :], ALU.mult, ALU.add)
                        link(ins)
                after(dve, e_mm, u, 5, 5)
                dve.tensor_tensor(X[:, u, :], bo[:, 0:HID], X[:, u, :], ALU.add).then_inc(e_add, 1)
                after(dve, e_add, u, 1, 1)
                link.end()
                after(dve, h3T_mm, u - 1, 1, 1)
                layer_norm(2, u, X[:, u, :], h3[:, :])

            def flat(ap):
                return ap.rearrange("p (c b) s -> p c (b s)", c=KT)

            def wkv(u):
                link = Chain(dve, dve_f, u, 6)
                after(dve, kk_in, u, 1, 1)
                for i in range(KT * BT):
                    ins = dve.tensor_tensor_scan(Op[:, i, 1:S + 1], wc[:, i // BT:i // BT + 1].to_broadcast([P, S]), kk[:, i, :],
                                                 NEG_INF, ALU.add, ALU.max)
                link(ins)
                link(dve.tensor_tensor(dd[:, :, :].rearrange("p c (b s) -> p (c b) s", b=BT), Op[:, :, 0:S], kk[:, :, :], ALU.subtract))
                for c in range(KT):
                    for i, col in ((0, wc), (1, nuc)):
                        dve.tensor_scalar(AR[:, 0, i, c, :], dd[:, c, :], col[:, c:c + 1], 0.0, ALU.add, ALU.min)
                        ins = dve.tensor_scalar(AR[:, 1, i, c, :], dd[:, c, :], col[:, c:c + 1], 0.0, ALU.add, ALU.max)
                ins.then_inc(arg_in, 1)
                after(dve, dec_exp, u, 3, 3)
                for i in range(KT * BT):
                    c, b = i // BT, i % BT
                    dve.tensor_tensor_scan(PQ[:, 1, i, 1:S + 1], EX[:, 0, c, b * S:(b + 1) * S], VE[:, 0, 1, i, :], 0.0, ALU.mult, ALU.add)
                after(dve, ev_in, u, 2, 1)
                for i in range(KT * BT):
                    c, b = i // BT, i % BT
                    ins = dve.tensor_tensor_scan(PQ[:, 0, i, 1:S + 1], EX[:, 0, c, b * S:(b + 1) * S], VE[:, 0, 0, i, :], 0.0, ALU.mult, ALU.add)
                link(ins)
                for j in range(2):
                    ins = dve.tensor_tensor(ND[:, j, :, :], PQ[:, j, :, 0:S], EX[:, 1, :, :].rearrange("p c (b s) -> p (c b) s", b=BT), ALU.mult)
                link(ins)
                after(dve, ev_in, u, 2, 2)
                for j in range(2):
                    ins = dve.tensor_tensor(ND[:, j, :, :], ND[:, j, :, :], VE[:, 1, j, :, :], ALU.add)
                link(ins)
                link(dve.reciprocal(ND[:, 1, :, :], ND[:, 1, :, :]))
                after(dve, yT_mm, u - 1, 1, 1)
                dve.tensor_tensor(yy[:, :, :], flat(ND[:, 0, :, :]), flat(ND[:, 1, :, :]), ALU.mult).then_inc(y_in, 1)
                link.end()

            def residual3(u):
                after(dve, yT_mm, u, 1, 1)
                dve.scalar_tensor_tensor(X[:, u, :], bc[:, 0:HID], tg[:, 2:3], X[:, u, :], ALU.mult, ALU.add).then_inc(x3_in, 1)
                after(dve, x3_in, u, 1, 1)
                after(dve, h4T_mm, u - 1, 1, 1)
                after(dve, h4_out, u - 1, 16, 16)
                layer_norm(3, u, X[:, u, :], h4[:, :])

            def router(u):
                after(dve, rl_mm, u, 1, 1)
                dve.tensor_copy(LG[:, u, :], bb[:, HID:HID + NE]).then_inc(rl_in, 1)

            norm1(0)
            rotate(0)
            low_parts(0)
            maxima(0)
            shift_low(0)
            heads(0)
            residual1(0)
            with dve.Fori(1, NT) as t:
                norm1(t)
                gate(t - 1)
                rotate(t)
                low_parts(t)
                mix(t - 1)
                maxima(t)
                shift_low(t)
                wkv(t - 1)
                residual3(t - 1)
                heads(t)
                router(t - 1)
                residual1(t)
            gate(NT - 1)
            mix(NT - 1)
            wkv(NT - 1)
            residual3(NT - 1)
            router(NT - 1)

            n_r = [0]

            def step(ins):
                n_r[0] += 1
                ins.then_inc(dve_r, 1)
                dve.wait_ge(dve_r, n_r[0])

            def cols(ap, n, k):
                return ap.rearrange("p (n o) -> p n o", o=1).to_broadcast([P, n, k])

            def rows(ap, n, k):
                return ap.rearrange("p (o k) -> p o k", o=1).to_broadcast([P, n, k])

            dve.wait_ge(h4_out, 16 * NT)
            step(dve.memset(ones[:, :], 1.0))
            dve.wait_ge(x_out, 16 * NT)
            step(dve.tensor_copy(sc[:, :, :], LG[:, :, :]))
            step(dve.tensor_scalar(li[:, :, :], sc[:, :, :], Q_IN, None, ALU.mult))
            step(dve.tensor_copy(sc[:, :, :], li[:, :, :]))
            step(dve.tensor_reduce(small[:, 0, :], sc[:, :, :], AX.X, ALU.max))
            step(dve.tensor_tensor(sc[:, :, :], sc[:, :, :], cols(small[:, 0, :], NT, NE), ALU.subtract))
            step(dve.tensor_scalar(sc[:, :, :], sc[:, :, :], LUT_MIN, None, ALU.max))
            step(dve.scalar_tensor_tensor(key[:, :, :], sc[:, :, :], 8.0, rows(CN[:, C_EV:C_EV + 8], NT, NE), ALU.mult, ALU.add))
            step(dve.tensor_reduce(small[:, 1, :], key[:, :, :], AX.X, ALU.max))
            step(dve.tensor_tensor(oh[:, 0, :, :], key[:, :, :], cols(small[:, 1, :], NT, NE), ALU.is_equal))
            step(dve.scalar_tensor_tensor(key2[:, :, :], oh[:, 0, :, :], -1.0e5, key[:, :, :], ALU.mult, ALU.add))
            step(dve.tensor_reduce(small[:, 2, :], key2[:, :, :], AX.X, ALU.max))
            step(dve.tensor_tensor(oh[:, 1, :, :], key2[:, :, :], cols(small[:, 2, :], NT, NE), ALU.is_equal))
            dve.tensor_tensor(used[:, :, :], oh[:, 0, :, :], oh[:, 1, :, :], ALU.add).then_inc(used_in, 1)
            step(dve.tensor_tensor(tmp[:, 0, :, :], oh[:, 1, :, :], sc[:, :, :], ALU.mult))
            step(dve.tensor_reduce(small[:, 3, :], tmp[:, 0, :, :], AX.X, ALU.add))
            for t in range(NT):
                ins = dve.scalar_tensor_tensor(lutx[:, t, :], CN[:, C_LUTX:C_LUTX + 129], small[:, 3, t:t + 1],
                                               CN[:, C_LUT:C_LUT + 129], ALU.is_equal, ALU.mult, accum_out=small[:, 4, t:t + 1])
            step(ins)
            step(dve.tensor_scalar(small[:, 5, :], small[:, 4, :], Q_OUT, None, ALU.add))
            step(dve.reciprocal(small[:, 6, :], small[:, 5, :]))
            step(dve.tensor_scalar(small[:, 7, :], small[:, 6, :], tg[:, 3:4], None, ALU.mult))
            step(dve.tensor_scalar(wts[:, 0:NT], small[:, 7, :], Q_OUT, None, ALU.mult))
            step(dve.tensor_tensor(wts[:, NT:2 * NT], small[:, 7, :], small[:, 4, :], ALU.mult))
            dve.wait_ge(rk_mm, 1)
            step(dve.memset(cum[:, 0, :], 0.0))
            for t in range(NT):
                step(dve.tensor_tensor(cum[:, t + 1, :], cum[:, t, :], bt[0][:, NT * NE + t * NE:NT * NE + (t + 1) * NE], ALU.add))
            step(dve.tensor_tensor(rank[:, :, :], bt[0][:, 0:NT * NE].rearrange("p (t e) -> p t e", t=NT), cum[:, 0:NT, :], ALU.add))
            step(dve.tensor_tensor(gtj[:, :, :], cols(cum[:, NT, :], NE, NT), rows(CN[:, C_J128:C_J128 + NT], NE, NT), ALU.is_gt))
            step(dve.tensor_reduce(ex[:, 0, :], gtj[:, :, :], AX.X, ALU.add))
            step(dve.memset(ex[:, 3, :], 1.0))
            step(dve.tensor_tensor_scan(ex[:, 1, :], ex[:, 3, :], ex[:, 0, :], 0.0, ALU.mult, ALU.add))
            step(dve.tensor_tensor(ex[:, 2, :], ex[:, 1, :], ex[:, 0, :], ALU.subtract))
            step(dve.scalar_tensor_tensor(rank[:, :, :], rows(ex[:, 2, :], NT, NE), float(P), rank[:, :, :], ALU.mult, ALU.add))
            for k in range(TOPK):
                ins = dve.tensor_tensor(tmp[:, k, :, :], oh[:, k, :, :], rank[:, :, :], ALU.mult)
            step(ins)
            step(dve.tensor_reduce(slot[:, :], tmp[:, :, :, :].rearrange("p k t e -> p (k t) e"), AX.X, ALU.add))
            step(dve.tensor_copy(slot_i[:, :], slot[:, :]))
            dve.tensor_scalar(jt_i[:, :], slot_i[:, :], 7, None, ALU.arith_shift_right)
            step(dve.tensor_scalar(pos_i[:, :], slot_i[:, :], P - 1, None, ALU.bitwise_and))
            dve.tensor_copy(jt[:, :], jt_i[:, :])
            step(dve.tensor_copy(pos[:, :], pos_i[:, :]))
            step(dve.tensor_tensor(ohp[:, :, :], rows(CN[:, C_POS:C_POS + P], TOPK * NT, P), cols(pos[:, :], TOPK * NT, P), ALU.is_equal))
            step(dve.tensor_tensor(val[:, :, 2, :], rows(CN[:, C_POS:C_POS + NJ], TOPK * NT, NJ), cols(jt[:, :], TOPK * NT, NJ), ALU.is_equal))
            for k in range(TOPK):
                h = slice(k * NT, (k + 1) * NT)
                dve.tensor_tensor(val[:, h, 0, :], val[:, h, 2, :], cols(CN[:, C_TOK:C_TOK + NT], NT, NJ), ALU.mult)
            dve.tensor_tensor(val[:, :, 1, :], val[:, :, 2, :], cols(wts[:, :], TOPK * NT, NJ), ALU.mult).then_inc(val_in, 1)
            step(dve.tensor_tensor(ejc[:, :, :], CN[0:1, C_POS:C_POS + NJ].rearrange("p (n o) -> p n o", o=1).to_broadcast([1, NJ, NE]),
                                   ex[0:1, 1, :].rearrange("p (o k) -> p o k", o=1).to_broadcast([1, NJ, NE]), ALU.is_ge))
            step(dve.tensor_reduce(ejs[:, :], ejc[:, :, :], AX.X, ALU.add))
            dve.tensor_scalar(ej[:, :], ejs[:, :], float(NE - 1), None, ALU.min).then_inc(e_of, 1)
            dve.wait_ge(tb_mm, 1)
            step(dve.tensor_copy(tb[:, :, :], bt[1][:, 0:3 * NJ].rearrange("p (k j) -> p k j", k=3)))
            dve.tensor_copy(gi[:, :], tb[:, 0, :]).then_inc(route, 1)
            step(dve.tensor_scalar(so[:, :], tb[:, 2, :], -1.0, 1.0, ALU.mult, ALU.add))
            step(dve.scalar_tensor_tensor(so[:, :], so[:, :], CN[:, C_OWN:C_OWN + 1], tb[:, 0, :], ALU.mult, ALU.add))
            dve.tensor_copy(si[:, :], so[:, :]).then_inc(route, 1)

            def h_turned(j):
                after(dve, hT_mm, j, 2, 2)
                after(dve, y_mm, j - 1, 1, 1)
                dve.tensor_copy(hT[:, 4:IT, :], bc[:, 0:(IT - 4) * P].rearrange("p (i n) -> p i n", i=IT - 4)).then_inc(hT_in_v, 1)

            def gates(j):
                for i in range(2):
                    after(dve, silu, j, 2, i + 1)
                    after(dve, up_mm, j, 4, 2 * i + 2)
                    after(dve, hT_mm, j - 1, 2, 2)
                    dve.tensor_tensor(hh[:, i * IH:(i + 1) * IH], sg[:, i, :], (bs[1], bt[1])[i][:, 0:IH], ALU.mult).then_inc(h_in, 1)

            dve.memset(hh[:, I:IT * P], 0.0).then_inc(zr, 1)
            dve.wait_ge(zr, 2)
            gates(0)
            with dve.Fori(1, NJ) as j:
                h_turned(j - 1)
                gates(j)
            h_turned(NJ - 1)

        @block.tensor
        def _(pe):
            pe.wait_ge(ld_const, 16)

            def transposed(dst, src, done):
                for c in range(KT):
                    ins = pe.transpose(dst[:, c * P:(c + 1) * P], src[:, c * P:(c + 1) * P], ident)
                ins.then_inc(done, 1)

            def project(t):
                after(pe, ln_done[0], t, 1, 1)
                after(pe, x1_in, t - 1, 1, 1)
                transposed(ba, hn, hnT)
                after(pe, hc_self, t, 1, 1)
                after(pe, rl_in, t - 2, 1, 1)
                for b in range(BT):
                    for c in range(KT):
                        ins = pe.matmul(bb[b * S:(b + 1) * S, 0:HID], HC[:, c, b, 0:S], wq[:, c, :], start=(c == 0), stop=(c == KT - 1))
                ins.then_inc(q_mm, 1)
                after(pe, hc_ctx, t, KT, KT)
                after(pe, aoT_in, t - 1, 1, 1)
                for b in range(BT):
                    for c in range(KT):
                        ins = pe.matmul((bc, ba)[b][:, :], HC[:, c, b, :], wkv[:, c, :], start=(c == 0), stop=(c == KT - 1))
                    ins.then_inc(kv_mm, 1)

            def turn_qk(t):
                after(pe, q_rot, t, 1, 1)
                after(pe, q_in, t, 1, 1)
                for g in range(G):
                    ins = pe.transpose(bb[:, g * P:(g + 1) * P],
                                       qr[:, g, :, :].rearrange("p o d -> p (o d)"), ident)
                ins.then_inc(qT, 1)
                for b in range(BT):
                    after(pe, k_rot, t, BT, b + 1)
                    after(pe, v_in, t, 4, 2 * b + 2)
                    for g in range(G):
                        ins = pe.transpose((bc, ba)[b][:, g * P:(g + 1) * P],
                                           kr[:, b, g, :, :].rearrange("p o d -> p (o d)"), ident)
                    ins.then_inc(kT, 1)

            def row_scores(t):
                after(pe, mk_in, t, 1, 1)
                for b in range(BT):
                    after(pe, k_hi, t, BT, b + 1)
                    for g in range(G):
                        n = G * b + g
                        after(pe, qx, t, G, g + 1)
                        if n >= 2:
                            after(pe, s_max, t, 8, n - 1)
                        else:
                            after(pe, s_max, t - 1, 8, 7 + n)
                        o = bs[n % 2]
                        for p in range(NP):
                            pe.matmul(o[:, p * P:(p + 1) * P], Qx[:, g, b, 2 * p:2 * p + 2, :], Kh[:, b, g, :],
                                      start=(p == 0), stop=False)
                        pe.matmul(o[:, :].rearrange("p (n k) -> p n k", n=NP)[:, :, 0:S], Idup[:, :],
                                  mk2[:, b, 0:S].rearrange("p (o k) -> p o k", o=1).to_broadcast([P, NP, S]),
                                  start=False, stop=True).then_inc(s_mm, 1)

            def turn_maxima(t):
                after(pe, q_lo, t, 1, 1)
                after(pe, s_max, t, 8, 8)
                pe.sem_inc(held, 1)
                pe.transpose(bb[0:2 * H, 0:P], mx[:, :, :, :, :].rearrange("p b s g n -> p (b s g n)"), ident).then_inc(mT, 1)

            def attend(t):
                after(pe, k_lo, t, BT, BT)
                after(pe, v_in, t, 4, 4)
                for g in range(G):
                    for b in range(BT):
                        if g == 0:
                            after(pe, m_row, t, BT * 64, BT * 64)
                            after(pe, p_exp, t - 1, 8, 8)
                        else:
                            after(pe, p_exp, t, 8, 2 * g + b - 1)
                        o = bt[b]
                        q = Qx[:, g, b, :, :]
                        pe.matmul(o[:, :], Kl[:, b, g, :], q, start=True, stop=False)
                        pe.matmul(o[:, :], Kh[:, b, g, :], q, start=False, stop=False)
                        pe.matmul(o[:, :], mk2[:, b, :], Idup[:, 0:S].rearrange("p (o q) -> p o q", o=1).to_broadcast([P, HG, S]),
                                  start=False, stop=False)
                        pe.matmul(o[:, :], Lm[:, :], mrow[:, b, g * 512:(g + 1) * 512], start=False, stop=True).then_inc(t_mm, 1)
                    if g >= 1:
                        values(t, g - 1)
                values(t, G - 1)

            def values(t, g):
                after(pe, p_exp, t, 8, 2 * g + 2)
                if g >= 1:
                    after(pe, o_in, t, 8, 2 * g)
                else:
                    after(pe, o_in, t - 1, 8, 8)
                    if not isinstance(t, int):
                        after(pe, e_add, t - 1, 1, 1)
                for h in range(HG):
                    ins = pe.matmul(bo[:, h * VW:(h + 1) * VW], Pt[:, g * HG + h, :, :],
                                    Vx[:, g * HG + h, :, :, :].rearrange("p b s d -> p (b s d)"), start=True, stop=True)
                ins.then_inc(pv_mm, 1)

            def output(t):
                after(pe, ao_in, t, 1, 1)
                after(pe, x3_in, t - 1, 1, 1)
                transposed(bc, ao, aoT_mm)
                after(pe, aoT_in, t, 1, 1)
                for c in range(KT):
                    ins = pe.matmul(ba[:, 0:HID], aoT[:, c, :], wo[:, c, :], start=(c == 0), stop=(c == KT - 1))
                ins.then_inc(wo_mm, 1)

            def gate(u):
                after(pe, ln_done[1], u, 1, 1)
                after(pe, p_exp, u, 8, 8)
                transposed(bt[0], h2, h2T_mm)
                after(pe, h2T_in, u, 1, 1)
                for c in range(KT):
                    ins = pe.matmul(bt[1][:, 0:E0], h2T[:, c, :], wg0[:, c, :], start=(c == 0), stop=(c == KT - 1))
                ins.then_inc(lg_mm, 1)

            def experts0(u):
                after(pe, comb_in, u, 1, 1)
                pe.transpose(bt[1][0:E0, P:2 * P], comb[:, :], ident).then_inc(combT_mm, 1)
                for n in range(E0 // 2):
                    if n == 1:
                        after(pe, combT_in, u, 1, 1)
                    if n >= 2:
                        after(pe, dve_e, u, 5 + E0, 5 + 2 * (n - 1))
                    for c in range(KT):
                        ins = pe.matmul(bt[n % 2][:, :], h2T[:, c, :], w0[:, c, 2 * n:2 * n + 2, :].rearrange("p e n -> p (e n)"),
                                        start=(c == 0), stop=(c == KT - 1))
                    ins.then_inc(e_mm, 1)
                after(pe, o_in, u, 8, 8)
                pe.matmul(bo[:, 0:HID], combT[:, :], b0[:, :], start=True, stop=True).then_inc(e_mm, 1)

            def turn_h3(u):
                after(pe, ln_done[2], u, 1, 1)
                if isinstance(u, int):
                    after(pe, aoT_in, u, 1, 1)
                else:
                    after(pe, k_lo, u + 1, BT, BT)
                transposed(bc, h3, h3T_mm)

            def turn_y(u):
                after(pe, y_in, u, 1, 1)
                after(pe, kk_in, u, 1, 1)
                for c in range(KT):
                    ins = pe.transpose(bc[:, c * P:(c + 1) * P], yy[:, c, :], ident)
                ins.then_inc(yT_mm, 1)

            def router(u):
                after(pe, ln_done[3], u, 1, 1)
                if isinstance(u, int):
                    after(pe, m_lo, u, 1, 1)
                else:
                    after(pe, m_lo, u + 1, 1, 1)
                transposed(bb, h4, h4T_mm)
                after(pe, h4T_in, u, 1, 1)
                for c in range(KT):
                    ins = pe.matmul(bb[:, HID:HID + NE], h4T[:, c, :], wg1[:, c, :], start=(c == 0), stop=(c == KT - 1))
                ins.then_inc(rl_mm, 1)

            pe.wait_ge(ld_attn, 16 * 8)
            pe.wait_ge(prep, 4)
            pe.wait_ge(zeroed, 8)
            project(0)
            turn_qk(0)
            row_scores(0)
            turn_maxima(0)
            attend(0)
            output(0)
            with pe.Fori(1, NT) as t:
                project(t)
                gate(t - 1)
                turn_qk(t)
                experts0(t - 1)
                row_scores(t)
                turn_h3(t - 1)
                turn_maxima(t)
                attend(t)
                turn_y(t - 1)
                router(t - 1)
                output(t)
            gate(NT - 1)
            experts0(NT - 1)
            turn_h3(NT - 1)
            turn_y(NT - 1)
            router(NT - 1)

            pe.wait_ge(used_in, 1)
            u = used[:, :, :].rearrange("p t e -> p (t e)")
            pe.matmul(bt[0][:, 0:NT * NE], CN[:, C_TRI:C_TRI + P], u, start=True, stop=True)
            pe.matmul(bt[0][:, NT * NE:2 * NT * NE], ones[:, :], u, start=True, stop=True).then_inc(rk_mm, 1)
            pe.wait_ge(val_in, 1)
            for i in range(TOPK * NT):
                ins = pe.matmul(bt[1][:, 0:3 * NJ], ohp[:, i, :], val[:, i, :, :].rearrange("p k j -> p (k j)"),
                                start=(i == 0), stop=(i == TOPK * NT - 1))
            ins.then_inc(tb_mm, 1)

            def turn_rows(j):
                after(pe, gathered, j, 16, 16)
                after(pe, xT_in, j - 1, 1, 1)
                for c in range(KT):
                    ins = pe.transpose(ba[:, c * P:(c + 1) * P], xg[:, c * P:(c + 1) * P], ident)
                ins.then_inc(xT_mm, 1)

            def up(j):
                e = pe.value_load(ej[0:1, bass.ts(j, 1)], min_val=0, max_val=NE - 1)
                after(pe, xT_in, j, 1, 1)
                for q, o in enumerate((bs[0], bs[1], bt[0], bt[1])):
                    if q % 2 == 0:
                        after(pe, silu, j - 1, 2, q // 2 + 1)
                    else:
                        after(pe, h_in, j - 1, 2, q // 2 + 1)
                    for c in range(KT):
                        ins = pe.matmul(o[:, 0:IH], xgT[:, c, :], w13[:, c, bass.ts(e, 1), q, :].rearrange("p o n -> p (o n)"),
                                        start=(c == 0), stop=(c == KT - 1))
                    ins.then_inc(up_mm, 1)

            def turn_h(j):
                after(pe, h_in, j, 2, 2)
                after(pe, hT_in_a, j - 1, 1, 1)
                after(pe, hT_in_v, j - 1, 1, 1)
                for i in range(IT):
                    o = bb if i < 4 else bc
                    ins = pe.transpose(o[:, (i % 4) * P:(i % 4 + 1) * P], hh[:, i * P:(i + 1) * P], ident)
                    if i == 3:
                        ins.then_inc(hT_mm, 1)
                ins.then_inc(hT_mm, 1)

            def down(j):
                e = pe.value_load(ej[0:1, bass.ts(j, 1)], min_val=0, max_val=NE - 1)
                after(pe, hT_in_a, j, 1, 1)
                after(pe, hT_in_v, j, 1, 1)
                after(pe, y_sc, j - 1, 1, 1)
                for i in range(IT):
                    k = P if i < IT - 1 else I - (IT - 1) * P
                    ins = pe.matmul(bo[:, 0:HID], hT[0:k, i, :], w2[0:k, i, bass.ts(e, 1), :].rearrange("p o n -> p (o n)"),
                                    start=(i == 0), stop=(i == IT - 1))
                ins.then_inc(y_mm, 1)

            pe.wait_ge(e_of, 1)
            turn_rows(0)
            pe.wait_ge(ld_w13, 16 * KT * NE)
            up(0)
            pe.wait_ge(ld_w2, 16 * 2 * NE)
            with pe.Fori(1, NJ) as j:
                turn_rows(j)
                turn_h(j - 1)
                up(j)
                down(j - 1)
            turn_h(NJ - 1)
            down(NJ - 1)


INS = ["x", "ctxT", "mask", "const", "Wq", "Wkv", "Wo", "gates", "head_gate", "wg", "WT", "b", "w", "u", "wgateT", "w13", "w2T"]


def constants():
    import numpy as np
    c = np.zeros((P, C_N), np.float32)
    c[:, C_ID:C_ID + P] = np.eye(P)
    inv = 1.0 / 10000.0 ** (np.arange(0, D, 2, dtype=np.float32) / D)
    emb = np.outer(np.arange(S, dtype=np.float32), inv)
    emb = np.concatenate([emb, emb], -1)
    cos, sin = np.cos(emb).astype(np.float32), np.sin(emb).astype(np.float32)
    sin[:, :D // 2] *= -1
    scale = np.float32(1 / math.sqrt(D))
    c[:, C_COSQ:C_COSQ + D] = np.tile(cos * scale, (2, 1))
    c[:, C_SINQ:C_SINQ + D] = np.tile(sin * scale, (2, 1))
    c[:S, C_COSK:C_COSK + D] = cos
    c[S:, C_COSK:C_COSK + D] = 1
    c[:S, C_SINK:C_SINK + D] = sin
    c[np.arange(P), C_HM + np.arange(P) % S // D] = 1
    c[:, C_EV:C_EV + 8] = 8 - np.arange(8)
    for r in range(4):
        c[r, C_ONE + S * (r % 2):C_ONE + S * (r % 2) + S] = 1
    n = np.arange(P)
    c[:, C_TRI:C_TRI + P] = n[:, None] < n[None, :]
    c[:, C_POS:C_POS + P] = n
    c[:, C_TOK:C_TOK + NT] = n[:, None] + P * np.arange(NT)
    c[:, C_OWN] = B * S + n
    c[:, C_J128:C_J128 + NT] = P * np.arange(NT)
    lut = np.arange(LUT_MIN, 1, dtype=np.float32)
    c[:, C_LUTX:C_LUTX + 129] = lut
    c[:, C_LUT:C_LUT + 129] = (np.exp(lut / np.float32(Q_IN)) * np.float32(Q_OUT)).astype(np.int32)
    return c


def kernel(x, ctx_2048, mask_Bx1xSxS_fk0, g_xattn, g_ffn, L0_xattn_Wq, L0_xattn_Wk, L0_xattn_Wv, L0_xattn_Wo,
           L0_xattn_gate, L0_ffn_wg, L0_ffn_W, L0_ffn_b, L1_xattn_w, L1_xattn_u, L1_ffn_w_gate, L1_ffn_w1, L1_ffn_w2,
           L1_ffn_w3):
    import numpy as np
    import concourse.bacc as bacc
    from concourse.bass_utils import run_bass_kernel_spmd as run

    f = lambda a: np.ascontiguousarray(np.asarray(a))
    gx, gf = np.asarray(g_xattn), np.asarray(g_ffn)
    arrays = {
        "x": f(x), "ctxT": f(np.asarray(ctx_2048).reshape(B * S, HID).T), "mask": f(mask_Bx1xSxS_fk0), "const": constants(),
        "Wq": f(L0_xattn_Wq), "Wkv": f(np.concatenate([L0_xattn_Wk, L0_xattn_Wv], 1)), "Wo": f(L0_xattn_Wo),
        "gates": f(np.stack([gx[0], gf[0], gx[1], gf[1]])), "head_gate": f(np.asarray(L0_xattn_gate).reshape(-1)),
        "wg": f(L0_ffn_wg), "WT": f(np.asarray(L0_ffn_W).transpose(0, 2, 1)), "b": f(L0_ffn_b),
        "w": f(np.asarray(L1_xattn_w).reshape(KT, P).T), "u": f(np.asarray(L1_xattn_u).reshape(KT, P).T), "wgateT": f(np.asarray(L1_ffn_w_gate).T),
        "w13": f(np.stack([np.asarray(w).transpose(0, 2, 1).reshape(NE, HID, 2, IH) for w in (L1_ffn_w1, L1_ffn_w3)], 3)
                 .reshape(NE, HID, 4, IH)),
        "w2T": f(np.asarray(L1_ffn_w2).transpose(0, 2, 1)),
    }
    nc = bacc.Bacc("TRN2", target_bir_lowering=False, num_devices=1)
    A = {n: nc.dram_tensor(f"in_{n}", a.shape, mybir.dt.from_np(a.dtype), kind="ExternalInput").ap() for n, a in arrays.items()}
    out = nc.dram_tensor("out_x", (B * S + P, HID), F32, kind="ExternalOutput").ap()
    H4 = nc.dram_tensor("normed", (B * S, HID), F32, kind="Internal").ap()
    build(nc, A, out, H4)
    r = run(nc, [{f"in_{n}": a for n, a in arrays.items()}], core_ids=[0])
    return r.results[0]["out_x"][0:B * S].reshape(B, S, HID)
```

```python
import math
from contextlib import ExitStack

import concourse.bass as bass
from concourse import mybir

F32 = mybir.dt.float32
F32R = mybir.dt.float32r
I32 = mybir.dt.int32
ALU = mybir.AluOpType
ACT = mybir.ActivationFunctionType
AX = mybir.AxisListType

B, S, HID, H = 16, 64, 256, 32
D = HID // H
P = 128
BT = 2
NT = B // BT
KT = HID // P
HG = 8
G = H // HG
NP = HG // 2
E0 = 8
NE = 8
VW = BT * 2 * (D + 1)
EPS = 1e-5
NEG_INF = -1e38

C_ID = 0
C_COSQ, C_SINQ, C_COSK, C_SINK = 128, 136, 144, 152
C_HM = 160
C_EV = 168
C_ONE = 176
C_TRI = C_ONE + 128
C_POS = C_TRI + 128
C_TOK = C_POS + 128
C_OWN = C_TOK + NT
C_J128 = C_OWN + 1
C_LUTX = C_J128 + NT
C_LUT = C_LUTX + 129
C_N = C_LUT + 129

TOPK = 2
I = 704
IH = I // 2
IT = -(-I // P)
NJ = (B * S * TOPK + NE * (P - 1)) // P
Q_IN, LUT_MIN, Q_OUT = 128.0, -128.0, 65536.0


def build(nc, A, out, H4):
    x_rows = A["x"].rearrange("b s h -> (b s) h").rearrange("(t p) h -> p t h", p=P)
    ctxT = A["ctxT"].rearrange("(c p) n -> p c n", p=P)
    mask_rows = A["mask"].rearrange("b o q k -> q (b o) k")
    out_rows = out[0:B * S, :].rearrange("(t p) h -> p t h", p=P)
    H4_rows = H4.rearrange("(t p) h -> p t h", p=P)

    ctx = ExitStack()
    with ctx:
        front = ExitStack()
        attn = ExitStack()

        def keep(name, shape, dt=F32):
            return ctx.enter_context(nc.sbuf_tensor(name, shape, dt))

        def sb(name, shape, dt=F32):
            return front.enter_context(nc.sbuf_tensor(name, shape, dt))

        def at(name, shape, dt=F32):
            return attn.enter_context(nc.sbuf_tensor(name, shape, dt, side="right"))

        def late(name, shape, dt=F32):
            return ctx.enter_context(nc.sbuf_tensor(name, shape, dt, side="right"))

        def sem(name):
            return ctx.enter_context(nc.semaphore(name))

        def bank(name):
            return ctx.enter_context(nc.psum_tensor(name, [P, 512], F32))

        LG = keep("LG", [P, NT, NE])
        CN = keep("CN", [P, C_N])
        tg = keep("tg", [P, 4])
        idx_in = keep("idx_in", [P, 1], I32)
        idx_out = keep("idx_out", [P, 1], I32)
        zrow = keep("zrow", [P, HID])
        X = keep("X", [P, NT, HID])
        h4 = keep("h4", [P, HID])
        CT = sb("CT", [P, KT, B * S])
        MK = at("MK", [P, B, S])
        ident = CN[:, C_ID:C_ID + P]
        wq = at("wq", [P, KT, HID])
        wkv = at("wkv", [P, KT, 2 * HID])
        wo = at("wo", [P, KT, HID])
        w0 = sb("w0", [P, KT, E0, HID])
        b0 = sb("b0", [E0, HID])
        wg0 = sb("wg0", [P, KT, E0])
        wg1 = sb("wg1", [P, KT, NE])
        wc = sb("wc", [P, KT])
        uc = sb("uc", [P, KT])
        nuc = sb("nuc", [P, KT])
        gts = sb("gts", [P, 4])
        hgr = sb("hgr", [P, H])
        thg = sb("thg", [P, H])
        Idup = at("Idup", [P, P], F32R)
        Lm = at("Lm", [P, P], F32R)
        mhalf = sb("mhalf", [P, 1])

        st = sb("st", [P, 4, 6])
        mv = sb("mv", [P, 4, 2])
        rstd = sb("rstd", [P, 4, 2])
        hn = at("hn", [P, HID])
        HC = at("HC", [P, KT, BT, P])
        qw = at("qw", [P, HID])
        kw = at("kw", [P, BT, HID])
        qt = at("qt", [P, HID])
        qt2 = at("qt2", [P, HID])
        qr = at("qr", [P, G, 2, HG * D])
        kt1 = at("kt1", [P, BT, HID])
        kt2 = at("kt2", [P, BT, HID])
        kr = at("kr", [P, BT, G, 2, HG * D])
        Vx = [at(f"Vx{i}", [P, H, BT, 2, D + 1]) for i in range(2)]
        qs = at("qs", [P, G, BT, S], F32R)
        Qx = [at(f"Qx{i}", [P, G, BT, HG, S], F32R) for i in range(2)]
        Kh = [at(f"Kh{i}", [P, BT, G, P], F32R) for i in range(2)]
        Kl = [at(f"Kl{i}", [P, BT, G, P], F32R) for i in range(2)]
        mk2 = [at(f"mk2{i}", [P, BT, P], F32R) for i in range(2)]
        mx = at("mx", [P, BT, 2, G, NP])
        mhl = at("mhl", [BT * 2 * G * NP, 2, P], F32R)
        mrow = at("mrow", [P, BT, H * S], F32R)
        Pt = at("Pt", [P, H, BT, S])
        Oc = at("Oc", [P, H, 2, D + 1])
        rec = at("rec", [P, H, 2])
        On = at("On", [P, 2, H, D])
        ao = at("ao", [P, HID])
        aoT = at("aoT", [P, KT, P])

        h2 = sb("h2", [P, HID])
        h2T = sb("h2T", [P, KT, P])
        lg = sb("lg", [P, 6, 8])
        comb = sb("comb", [P, E0])
        combT = sb("combT", [E0, P])
        h3 = sb("h3", [P, HID])
        kk = sb("kk", [P, KT * BT, S])
        Op = sb("Op", [P, KT * BT, S + 1])
        dd = sb("dd", [P, KT, BT * S])
        AR = sb("AR", [P, 2, 2, KT, BT * S])
        EX = sb("EX", [P, 2, KT, BT * S])
        VE = sb("VE", [P, 2, 2, KT * BT, S])
        PQ = sb("PQ", [P, 2, KT * BT, S + 1])
        ND = sb("ND", [P, 2, KT * BT, S])
        yy = sb("yy", [P, KT, BT * S])
        h4T = sb("h4T", [P, KT, P])
        front.close()
        attn.close()

        w13 = late("w13", [P, KT, NE, 4, IH])
        w2 = late("w2", [P, IT, NE, HID])
        ones = keep("ones", [P, P])
        li = keep("li", [P, NT, NE], I32)
        sc = keep("sc", [P, NT, NE])
        key = keep("key", [P, NT, NE])
        key2 = keep("key2", [P, NT, NE])
        oh = keep("oh", [P, TOPK, NT, NE])
        tmp = keep("tmp", [P, TOPK, NT, NE])
        small = keep("small", [P, 16, NT])
        lutx = keep("lutx", [P, NT, 129])
        used = keep("used", [P, NT, NE])
        rank = keep("rank", [P, NT, NE])
        cum = keep("cum", [P, NT + 1, NE])
        gtj = keep("gtj", [P, NE, NT])
        ex = keep("ex", [P, 4, NE])
        slot = keep("slot", [P, TOPK * NT])
        slot_i = keep("slot_i", [P, TOPK * NT], I32)
        jt_i = keep("jt_i", [P, TOPK * NT], I32)
        pos_i = keep("pos_i", [P, TOPK * NT], I32)
        jt = keep("jt", [P, TOPK * NT])
        pos = keep("pos", [P, TOPK * NT])
        wts = keep("wts", [P, TOPK * NT])
        ohp = keep("ohp", [P, TOPK * NT, P])
        val = keep("val", [P, TOPK * NT, 3, NJ])
        tb = keep("tb", [P, 3, NJ])
        gi = keep("gi", [P, NJ], I32)
        so = keep("so", [P, NJ])
        si = keep("si", [P, NJ], I32)
        ejc = keep("ejc", [1, NJ, NE])
        ejs = keep("ejs", [1, NJ])
        ej = keep("ej", [1, NJ], I32)
        xg = keep("xg", [P, HID])
        xgT = keep("xgT", [P, KT, P])
        sg = keep("sg", [P, 2, IH])
        hh = keep("hh", [P, IT * P])
        hT = keep("hT", [P, IT, P])
        ys = keep("ys", [P, HID])

        bs = [bank(f"bank_s{i}") for i in range(2)]
        bt = [bank(f"bank_t{i}") for i in range(2)]
        bo, ba, bb, bc = bank("bank_o"), bank("bank_a"), bank("bank_b"), bank("bank_c")

        ld_const, ld_x, ld_gate, ld_proj, ld_attn, ld_ffn = (sem(n) for n in ("ld_const", "ld_x", "ld_gate", "ld_proj", "ld_attn", "ld_ffn"))
        zeroed, prep, prep_act = sem("zeroed"), sem("prep"), sem("prep_act")
        ln_sync = [sem(f"ln{i}_sync") for i in range(4)]
        dve_g = sem("dve_g")
        held = sem("held")
        ln_eps = [sem(f"ln{i}_eps") for i in range(4)]
        ln_stat = [sem(f"ln{i}_stat") for i in range(4)]
        ln_rstd = [sem(f"ln{i}_rstd") for i in range(4)]
        ln_done = [sem(f"ln{i}_done") for i in range(4)]
        hnT, hc_self, hc_ctx = sem("hnT"), sem("hc_self"), sem("hc_ctx")
        q_in, k_in = sem("q_in"), sem("k_in")
        q_mm, kv_mm, q_rot, k_rot, v_in = sem("q_mm"), sem("kv_mm"), sem("q_rot"), sem("k_rot"), sem("v_in")
        qT, kT, q_hi, k_hi, q_lo, k_lo = sem("qT"), sem("kT"), sem("q_hi"), sem("k_hi"), sem("q_lo"), sem("k_lo")
        qx, mk_in = sem("qx"), sem("mk_in")
        s_mm, s_max, mT, m_hi, m_lo, m_row = sem("s_mm"), sem("s_max"), sem("mT"), sem("m_hi"), sem("m_lo"), sem("m_row")
        t_mm, p_exp, pv_mm, o_in, ao_in = sem("t_mm"), sem("p_exp"), sem("pv_mm"), sem("o_in"), sem("ao_in")
        aoT_mm, aoT_in, wo_mm, x1_in = sem("aoT_mm"), sem("aoT_in"), sem("wo_mm"), sem("x1_in")
        h2T_mm, h2T_in, lg_mm, l_max, l_exp, comb_in = (sem(n) for n in ("h2T_mm", "h2T_in", "lg_mm", "l_max", "l_exp", "comb_in"))
        combT_mm, combT_in, e_mm, e_add = sem("combT_mm"), sem("combT_in"), sem("e_mm"), sem("e_add")
        h3T_mm, kk_in, arg_in, dec_exp, ev_in = sem("h3T_mm"), sem("kk_in"), sem("arg_in"), sem("dec_exp"), sem("ev_in")
        y_in, yT_mm, x3_in = sem("y_in"), sem("yT_mm"), sem("x3_in")
        h4T_mm, h4T_in, rl_mm, rl_in, x_out = sem("h4T_mm"), sem("h4T_in"), sem("rl_mm"), sem("rl_in"), sem("x_out")
        dve_a, dve_c, dve_e, dve_f, pool_a, pool_l = (sem(n) for n in ("dve_a", "dve_c", "dve_e", "dve_f", "pool_a", "pool_l"))

        ld_w13, ld_w2, h4_out, z_out, zr = sem("ld_w13"), sem("ld_w2"), sem("h4_out"), sem("z_out"), sem("zr")
        dve_r, rk_mm, tb_mm, route, e_of = sem("dve_r"), sem("rk_mm"), sem("tb_mm"), sem("route"), sem("e_of")
        used_in, val_in = sem("used_in"), sem("val_in")
        idx_cp, gathered, xT_mm, xT_in, up_mm, silu, h_in = (sem(n) for n in ("idx_cp", "gathered", "xT_mm", "xT_in", "up_mm", "silu", "h_in"))
        hT_mm, hT_in_a, hT_in_v, y_mm, y_sc, added, idx_cp2 = (sem(n) for n in ("hT_mm", "hT_in_a", "hT_in_v", "y_mm", "y_sc", "added", "idx_cp2"))

        block = ctx.enter_context(nc.Block())

        def after(eng, s, t, per, n):
            if isinstance(t, int):
                if t * per + n > 0:
                    eng.wait_ge(s, t * per + n)
            else:
                eng.wait_ge(s, t * per + n)

        def over_tiles(eng, body):
            body(0, 0, False, True)
            with eng.Fori(1, NT - 2, 2) as t:
                body(t, 1, True, True)
                body(t + 1, 0, True, True)
            body(NT - 1, (NT - 1) % 2, True, False)

        class Chain:

            def __init__(self, eng, s, t, per, n=0):
                self.eng, self.s, self.t, self.per, self.n = eng, s, t, per, n

            def __call__(self, ins):
                self.n += 1
                ins.then_inc(self.s, 1)
                self.eng.wait_ge(self.s, self.t * self.per + self.n)

            def end(self):
                assert self.n == self.per, self.n

        @block.sync
        def _(sp):
            sp.dma_start(CN[:, :], A["const"]).then_inc(ld_const, 16)
            sp.dma_start(X[:, :, :], x_rows).then_inc(ld_x, 16)
            for name, dst in (("Wq", wq), ("Wkv", wkv)):
                sp.dma_start(dst[:, :, :], A[name].rearrange("(c p) n -> p c n", p=P)).then_inc(ld_proj, 16)
            sp.dma_start(CT[:, :, :], ctxT).then_inc(ld_proj, 16)
            for half in range(2):
                sp.dma_start(MK[half * S:(half + 1) * S, :, :], mask_rows).then_inc(ld_attn, 16)
            sp.dma_start(wo[:, :, :], A["Wo"].rearrange("(c p) n -> p c n", p=P)).then_inc(ld_attn, 16)
            sp.dma_start(wc[:, :], A["w"]).then_inc(ld_ffn, 16)
            sp.dma_start(uc[:, :], A["u"]).then_inc(ld_ffn, 16)
            sp.dma_start(b0[:, :], A["b"]).then_inc(ld_ffn, 16)
            sp.dma_start(wg0[:, :, :], A["wg"].rearrange("(c p) n -> p c n", p=P)).then_inc(ld_ffn, 16)
            sp.dma_start(wg1[:, :, :], A["wgateT"].rearrange("(c p) n -> p c n", p=P)).then_inc(ld_ffn, 16)
            for c in range(KT):
                sp.dma_start(w0[:, c, :, :], A["WT"][:, c * P:(c + 1) * P, :].rearrange("e p n -> p e n")).then_inc(ld_ffn, 16)

            sp.wait_ge(zeroed, 12)

            def shift_rows(t):
                after(sp, m_lo, t, 1, 1)
                after(sp, t_mm, t - 1, 8, 8)
                for b in range(BT):
                    for hl in range(2):
                        for s in range(2):
                            r = 2 * hl + s
                            sp.dma_start(mrow[r:r + 1, b, :].rearrange("o (g x) -> o g x", x=P).bitcast(F32),
                                         mhl[32 * b + 16 * s:32 * b + 16 * s + 16, hl, :].bitcast(F32)).then_inc(m_row, 16)

            sp.wait_ge(zr, 1)
            sp.dma_start(out[B * S:B * S + P, :], zrow[:, :]).then_inc(z_out, 16)

            def store(u):
                after(sp, x3_in, u, 1, 1)
                sp.dma_start(out_rows[:, u, :], X[:, u, :]).then_inc(x_out, 16)
                after(sp, ln_done[3], u, 1, 1)
                sp.dma_start(H4_rows[:, u, :], h4[:, :]).then_inc(h4_out, 16)

            def tile(t, par, prev, nxt):
                shift_rows(t)
                if prev:
                    store(t - 1)

            over_tiles(sp, tile)
            sp.wait_ge(x1_in, NT)
            for e in range(NE):
                for c in range(KT):
                    sp.dma_start(w13[:, c, e, :, :], A["w13"][e, c * P:(c + 1) * P, :, :]).then_inc(ld_w13, 16)
            for e in range(NE):
                sp.dma_start(w2[:, 0:IT - 1, e, :], A["w2T"][e, 0:(IT - 1) * P, :].rearrange("(i p) n -> p i n", p=P)).then_inc(ld_w2, 16)
                sp.dma_start(w2[0:I - (IT - 1) * P, IT - 1, e, :], A["w2T"][e, (IT - 1) * P:I, :]).then_inc(ld_w2, 16)
            sp.wait_ge(z_out, 16)
            sp.wait_ge(added, 16 * NJ)

        @block.gpsimd
        def _(pool):
            pool.memset(mhalf[:, :], -0.5).then_inc(zeroed, 1)
            pool.wait_ge(zeroed, 12)

            def rstd_of(n, t):
                after(pool, ln_stat[n], t, 1, 1)
                pool.sem_inc(held, 1)
                pool.tensor_scalar_add(rstd[:, n, 0:1], mv[:, n, 1:2], EPS).then_inc(ln_eps[n], 1)
                after(pool, ln_eps[n], t, 1, 1)
                pool.tensor_tensor(rstd[:, n, 1:2], rstd[:, n, 0:1], mhalf[:, :], ALU.pow).then_inc(ln_rstd[n], 1)

            def ctx_and_mask(t, par):
                after(pool, kv_mm, t - 1, BT, BT)
                for c in range(KT):
                    pool.tensor_copy(HC[:, c, :, S:P], CT[:, c, bass.ts(t, P)].rearrange("p (b k) -> p b k", b=BT)).then_inc(hc_ctx, 1)
                after(pool, t_mm, t - 2, 8, 8)
                pool.tensor_copy(mk2[par][:, :, 0:S], MK[:, bass.ts(t, BT), :]).then_inc(pool_a, 1)

            def spread(t, par):
                after(pool, q_lo, t, 1, 1)
                after(pool, t_mm, t - 2, 8, 8)
                hm = CN[:, C_HM:C_HM + HG]
                for g in range(G):
                    for b in range(BT):
                        ins = pool.tensor_tensor(
                            Qx[par][:, g, b, :, :],
                            qs[:, g, b, :].bitcast(F32).rearrange("p (o q) -> p o q", o=1).to_broadcast([P, HG, S]),
                            hm.rearrange("p (h o) -> p h o", o=1).to_broadcast([P, HG, S]), ALU.mult)
                    ins.then_inc(qx, 1)

            def ev(u):
                after(pool, dec_exp, u, 3, 3)
                v = CT[:, :, bass.ts(u, P)]
                for i in range(2):
                    pool.tensor_tensor(VE[:, i, 0, :, :].rearrange("p (c b) s -> p c (b s)", c=KT),
                                       VE[:, i, 1, :, :].rearrange("p (c b) s -> p c (b s)", c=KT), v,
                                       ALU.mult).then_inc(ev_in, 1)

            pool.wait_ge(ld_const, 16)
            rstd_of(0, 0)
            pool.wait_ge(ld_proj, 16 * 3)
            pool.wait_ge(ld_attn, 16 * 3)
            ctx_and_mask(0, 0)
            spread(0, 0)

            def tile(t, par, prev, nxt):
                if nxt:
                    rstd_of(0, t + 1)
                if prev:
                    rstd_of(1, t - 1)
                if nxt:
                    ctx_and_mask(t + 1, 1 - par)
                if prev:
                    rstd_of(2, t - 1)
                    ev(t - 1)
                if nxt:
                    spread(t + 1, 1 - par)
                if prev:
                    rstd_of(3, t - 1)

            over_tiles(pool, tile)
            rstd_of(1, NT - 1)
            rstd_of(2, NT - 1)
            ev(NT - 1)
            rstd_of(3, NT - 1)

            def gather(j):
                after(pool, xT_mm, j - 1, 1, 1)
                pool.tensor_copy(idx_in[:, :], gi[:, bass.ts(j, 1)]).then_inc(idx_cp, 1)
                after(pool, idx_cp, j, 1, 1)
                pool.sem_inc(held, 1)
                pool.indirect_dma_start(xg[:, :], None, H4, bass.IndirectOffsetOnAxis(ap=idx_in[:, :], axis=0)).then_inc(gathered, 16)

            def add(j):
                after(pool, added, j - 1, 16, 16)
                pool.tensor_copy(idx_out[:, :], si[:, bass.ts(j, 1)]).then_inc(idx_cp2, 1)
                after(pool, idx_cp2, j, 1, 1)
                after(pool, y_sc, j, 1, 1)
                pool.sem_inc(held, 1)
                pool.indirect_dma_start(out, bass.IndirectOffsetOnAxis(ap=idx_out[:, :], axis=0), ys[:, :], None,
                                        compute_op=ALU.add).then_inc(added, 16)

            pool.wait_ge(route, 2)
            pool.wait_ge(h4_out, 16 * NT)
            pool.wait_ge(x_out, 16 * NT)
            pool.wait_ge(z_out, 16)
            gather(0)
            gather(1)
            with pool.Fori(1, NJ - 1) as j:
                gather(j + 1)
                add(j - 1)
            add(NJ - 2)
            add(NJ - 1)

        @block.scalar
        def _(act):
            def copy(dst, src, scale=1.0):
                return act.activation(dst, src, ACT.Copy, scale=scale)

            act.dma_start(gts[:, 0:4], A["gates"].partition_broadcast(P)).then_inc(ld_gate, 16)
            act.dma_start(hgr[:, :], A["head_gate"].partition_broadcast(P)).then_inc(ld_gate, 16)
            act.wait_ge(ld_gate, 16 * 2)
            act.activation(tg[:, :], gts[:, :], ACT.Tanh).then_inc(prep_act, 1)
            act.activation(thg[:, :], hgr[:, :], ACT.Tanh).then_inc(prep_act, 1)
            act.wait_ge(zeroed, 12)

            def evac_hn(t):
                after(act, hnT, t, 1, 1)
                after(act, kv_mm, t - 1, BT, BT)
                copy(HC[:, :, :, 0:S], ba[:, 0:KT * P].rearrange("p (c b s) -> p c b s", c=KT, b=BT)).then_inc(hc_self, 1)

            def evac_q(t):
                after(act, q_mm, t, 1, 1)
                after(act, q_rot, t - 1, 1, 1)
                copy(qw[:, :], bb[:, 0:HID]).then_inc(q_in, 1)

            def evac_v(t, par):
                after(act, pv_mm, t - 2, G, G)
                after(act, k_rot, t - 1, BT, BT)
                for b in range(BT):
                    after(act, kv_mm, t, BT, b + 1)
                    copy(kw[:, b, :], (bc, ba)[b][:, 0:HID]).then_inc(k_in, 1)
                    src = (bc, ba)[b][:, HID:2 * HID].rearrange("p (h d) -> p h d", h=H)
                    for s in range(2):
                        r = slice(S * s, S * s + S)
                        copy(Vx[par][r, :, b, s, 0:D], src[r]).then_inc(v_in, 1)

            def evac_qk(t, par):
                after(act, qT, t, 1, 1)
                after(act, qx, t - 1, G, G)
                copy(qs[:, :, :, :], bb[:, :].rearrange("p (g b s) -> p g b s", g=G, b=BT)).then_inc(q_hi, 1)
                after(act, t_mm, t - 2, 8, 8)
                for b in range(BT):
                    after(act, kT, t, BT, b + 1)
                    copy(Kh[par][:, b, :, :], (bc, ba)[b][:, :].rearrange("p (g k) -> p g k", g=G)).then_inc(k_hi, 1)

            def shifts(t):
                after(act, m_row, t - 1, BT * 64, BT * 64)
                after(act, mT, t, 1, 1)
                copy(mhl[:, 0, :], bb[0:2 * H, 0:P], -1.0).then_inc(m_hi, 1)

            def attend(t, g):
                for b in range(BT):
                    after(act, t_mm, t, 8, 2 * g + b + 1)
                    if b == 0:
                        after(act, pv_mm, t - 1, G, g + 1)
                    act.activation(Pt[:, g * HG:(g + 1) * HG, b, :], bt[b][:, :].rearrange("p (h q) -> p h q", h=HG),
                                   ACT.Exp).then_inc(p_exp, 1)

            def heads_out(t, g):
                after(act, pv_mm, t, G, g + 1)
                if g == 0:
                    after(act, ao_in, t - 1, 1, 1)
                src = bo[:, 0:HG * VW].rearrange("p (h b s d) -> p h b s d", h=HG, b=BT, s=2)
                for b in range(BT):
                    r = slice(S * b, S * b + S)
                    copy(Oc[r, g * HG:(g + 1) * HG, :, :], src[r, :, b, :, :]).then_inc(o_in, 1)

            def evac_ao(t):
                after(act, aoT_mm, t, 1, 1)
                copy(aoT[:, :, :], bc[:, 0:KT * P].rearrange("p (c n) -> p c n", c=KT)).then_inc(aoT_in, 1)

            def evac_h2(u):
                after(act, h2T_mm, u, 1, 1)
                copy(h2T[:, :, :], bt[0][:, 0:KT * P].rearrange("p (c n) -> p c n", c=KT)).then_inc(h2T_in, 1)

            def gate(u):
                after(act, l_max, u, 1, 1)
                act.activation(lg[:, 1, :], lg[:, 3, :], ACT.Exp, bias=lg[:, 0, 1:2],
                               accum_out=lg[:, 0, 2:3]).then_inc(l_exp, 1)

            def evac_comb(u):
                after(act, combT_mm, u, 1, 1)
                copy(combT[:, :], bt[1][0:E0, P:2 * P]).then_inc(combT_in, 1)

            def evac_kk(u):
                after(act, h3T_mm, u, 1, 1)
                copy(kk[:, :, :], bs[0][:, 0:KT * P].rearrange("p (c s) -> p c s", c=KT * BT)).then_inc(kk_in, 1)

            def decay(u):
                after(act, arg_in, u, 1, 1)
                act.activation(EX[:, :, :, :], AR[:, 0, :, :, :], ACT.Exp).then_inc(dec_exp, 1)
                for i in range(2):
                    act.activation(VE[:, i, 1, :, :].rearrange("p (c b) s -> p c (b s)", c=KT), AR[:, 1, i, :, :], ACT.Exp,
                                   scale=-1.0).then_inc(dec_exp, 1)

            def evac_h4(u):
                after(act, h4T_mm, u, 1, 1)
                copy(h4T[:, :, :], bb[:, 0:KT * P].rearrange("p (c n) -> p c n", c=KT)).then_inc(h4T_in, 1)

            def router(u):
                after(act, rl_mm, u, 1, 1)
                copy(LG[:, u, :], bb[:, HID:HID + NE]).then_inc(rl_in, 1)

            evac_hn(0)
            evac_q(0)
            evac_v(0, 0)
            evac_qk(0, 0)

            def tile(t, par, prev, nxt):
                if nxt:
                    evac_hn(t + 1)
                if prev:
                    evac_h2(t - 1)
                shifts(t)
                if nxt:
                    evac_q(t + 1)
                if prev:
                    gate(t - 1)
                if nxt:
                    evac_v(t + 1, 1 - par)
                if prev:
                    evac_comb(t - 1)
                attend(t, 0)
                if prev:
                    evac_kk(t - 1)
                attend(t, 1)
                heads_out(t, 0)
                if nxt:
                    evac_qk(t + 1, 1 - par)
                if prev:
                    decay(t - 1)
                attend(t, 2)
                heads_out(t, 1)
                attend(t, 3)
                heads_out(t, 2)
                heads_out(t, 3)
                evac_ao(t)
                if prev:
                    evac_h4(t - 1)
                    router(t - 1)

            over_tiles(act, tile)
            evac_h2(NT - 1)
            gate(NT - 1)
            evac_comb(NT - 1)
            evac_kk(NT - 1)
            decay(NT - 1)
            act.wait_ge(x3_in, NT)
            act.dma_start(out_rows[:, NT - 1, :], X[:, NT - 1, :]).then_inc(x_out, 16)
            act.wait_ge(ln_done[3], NT)
            act.dma_start(H4_rows[:, NT - 1, :], h4[:, :]).then_inc(h4_out, 16)
            evac_h4(NT - 1)
            router(NT - 1)

            def rows_in(j):
                after(act, xT_mm, j, 1, 1)
                after(act, up_mm, j - 1, 4, 4)
                copy(xgT[:, :, :], ba[:, 0:KT * P].rearrange("p (c n) -> p c n", c=KT)).then_inc(xT_in, 1)

            def h_turned(j):
                after(act, hT_mm, j, 2, 1)
                after(act, y_mm, j - 1, 1, 1)
                copy(hT[:, 0:4, :], bb[:, :].rearrange("p (i n) -> p i n", i=4)).then_inc(hT_in_a, 1)

            def gates(j):
                for i in range(2):
                    after(act, up_mm, j, 4, 2 * i + 1)
                    after(act, h_in, j - 1, 2, i + 1)
                    act.activation(sg[:, i, :], (bs[0], bt[0])[i][:, 0:IH], ACT.Silu).then_inc(silu, 1)

            def scaled(j):
                after(act, y_mm, j, 1, 1)
                after(act, added, j - 1, 16, 16)
                act.activation(ys[:, :], bo[:, 0:HID], ACT.Copy, scale=tb[:, 1, bass.ts(j, 1)]).then_inc(y_sc, 1)

            act.wait_ge(route, 2)
            rows_in(0)
            gates(0)
            with act.Fori(1, NJ) as j:
                rows_in(j)
                h_turned(j - 1)
                gates(j)
                scaled(j - 1)
            h_turned(NJ - 1)
            scaled(NJ - 1)

        @block.vector
        def _(dve):
            dve.memset(zrow[:, :], 0.0).then_inc(zr, 1)
            for i in range(2):
                dve.memset(Vx[i][:, :, :, :, :], 0.0).then_inc(zeroed, 1)
                dve.memset(mk2[i][:, :, :].bitcast(F32), 0.0).then_inc(zeroed, 1)
            dve.memset(mrow[:, :, :].bitcast(F32), 0.0).then_inc(zeroed, 1)
            dve.memset(Op[:, :, 0:1], NEG_INF).then_inc(zeroed, 1)
            dve.memset(PQ[:, :, :, 0:1], 0.0).then_inc(zeroed, 1)
            dve.wait_ge(zeroed, 8)
            for i in range(2):
                dve.memset(Vx[i][0:S, :, :, 0, D:D + 1], 1.0).then_inc(zeroed, 1)
                dve.memset(Vx[i][S:P, :, :, 1, D:D + 1], 1.0).then_inc(zeroed, 1)
            dve.wait_ge(ld_const, 16)
            dve.wait_ge(ld_x, 16)
            dve.tensor_tensor(Idup[:, 0:S], CN[:, C_ID:C_ID + S], CN[:, C_ID + S:C_ID + P], ALU.add).then_inc(prep, 1)
            dve.tensor_tensor(Idup[:, S:P], CN[:, C_ID:C_ID + S], CN[:, C_ID + S:C_ID + P], ALU.add).then_inc(prep, 1)
            dve.tensor_copy(Lm[:, :], CN[:, C_ONE:C_ONE + P]).then_inc(prep, 1)
            dve.wait_ge(prep, 3)

            def ln_stats(n, t):
                dve.sem_inc(held, 1)
                dve.bn_stats(st[:, n, :], X[:, t, :]).then_inc(ln_sync[n], 1)
                after(dve, ln_sync[n], t, 1, 1)
                dve.sem_inc(held, 1)
                dve.bn_aggr(mv[:, n, :], st[:, n, :]).then_inc(ln_stat[n], 1)

            def ln_apply(n, t):
                after(dve, (hnT, h2T_mm, h3T_mm, h4T_mm)[n], t - 1, 1, 1)
                if n == 3:
                    after(dve, h4_out, t - 1, 16, 16)
                after(dve, ln_rstd[n], t, 1, 1)
                after(dve, ln_stat[n], t, 1, 1)
                dve.tensor_scalar((hn, h2, h3, h4)[n][:, :], X[:, t, :], mv[:, n, 0:1], rstd[:, n, 1:2],
                                  ALU.subtract, ALU.mult).then_inc(ln_done[n], 1)

            def twice(ap):
                return ap.rearrange("p (g o d) -> p g o d", g=G, o=1).to_broadcast([P, G, 2, HG * D])

            def rope(src, cos, sin, t1, t2):
                v = src.rearrange("p (h d) -> p h d", h=H)

                def bc3(c, n):
                    return c.rearrange("p (o d) -> p o d", o=1).to_broadcast([P, H, n])

                a = t1.rearrange("p (h d) -> p h d", h=H)
                z = t2.rearrange("p (h d) -> p h d", h=H)
                h = D // 2
                dve.tensor_tensor(a, v, bc3(CN[:, cos:cos + D], D), ALU.mult)
                dve.tensor_tensor(z[:, :, 0:h], v[:, :, h:D], bc3(CN[:, sin:sin + h], h), ALU.mult)
                return dve.tensor_tensor(z[:, :, h:D], v[:, :, 0:h], bc3(CN[:, sin + h:sin + D], h), ALU.mult)

            def rotate_q(t):
                link = Chain(dve, dve_a, t, 1 + BT)
                after(dve, q_in, t, 1, 1)
                link(rope(qw[:, :], C_COSQ, C_SINQ, qt[:, :], qt2[:, :]))
                after(dve, qT, t - 1, 1, 1)
                dve.tensor_tensor(qr[:, :, :, :], twice(qt[:, :]), twice(qt2[:, :]), ALU.add).then_inc(q_rot, 1)

            def rotate_k(t, b):
                link = Chain(dve, dve_a, t, 1 + BT, 1 + b)
                after(dve, k_in, t, BT, b + 1)
                link(rope(kw[:, b, :], C_COSK, C_SINK, kt1[:, b, :], kt2[:, b, :]))
                after(dve, kT, t - 1, BT, BT)
                dve.tensor_tensor(kr[:, b, :, :, :], twice(kt1[:, b, :]), twice(kt2[:, b, :]), ALU.add).then_inc(k_rot, 1)

            def low_parts(t, par):
                after(dve, q_hi, t, 1, 1)
                after(dve, qx, t - 1, G, G)
                dve.tensor_tensor(qs[S:P, :, :, :], bb[S:P, :].rearrange("p (g b s) -> p g b s", g=G, b=BT),
                                  qs[S:P, :, :, :].bitcast(F32), ALU.subtract).then_inc(q_lo, 1)
                after(dve, t_mm, t - 2, 8, 8)
                for b in range(BT):
                    after(dve, k_hi, t, BT, b + 1)
                    dve.tensor_tensor(Kl[par][:, b, :, :], (bc, ba)[b][:, :].rearrange("p (g k) -> p g k", g=G),
                                      Kh[par][:, b, :, :].bitcast(F32), ALU.subtract).then_inc(k_lo, 1)

            def mask_low(t, par):
                after(dve, pool_a, t, 1, 1)
                dve.tensor_tensor(mk2[par][S:P, :, 0:S], MK[S:P, bass.ts(t, BT), :], mk2[par][S:P, :, 0:S].bitcast(F32),
                                  ALU.subtract).then_inc(mk_in, 1)

            def maxima(t, units):
                for n in units:
                    g, b = n // BT, n % BT
                    after(dve, s_mm, t, 8, n + 1)
                    if n == 0:
                        after(dve, mT, t - 1, 1, 1)
                    dve.tensor_reduce(mx[:, b, :, g, :].rearrange("p s n -> p n s"),
                                      bs[n % 2][:, :].rearrange("p (n s k) -> p n s k", n=NP, s=2),
                                      AX.X, ALU.max).then_inc(s_max, 1)

            def shift_low(t):
                after(dve, m_row, t - 1, BT * 64, BT * 64)
                after(dve, m_hi, t, 1, 1)
                dve.scalar_tensor_tensor(mhl[:, 1, :], bb[0:2 * H, 0:P], -1.0, mhl[:, 0, :].bitcast(F32),
                                         ALU.mult, ALU.subtract).then_inc(m_lo, 1)

            def heads(t):
                link = Chain(dve, dve_c, t, 3)
                after(dve, o_in, t, 8, 8)
                link(dve.reciprocal(rec[:, :, :], Oc[:, :, :, D]))
                link(dve.tensor_tensor(rec[:, :, 1], rec[:, :, 1], thg[:, :], ALU.mult))
                for s in range(2):
                    ins = dve.tensor_tensor(On[:, s, :, :], Oc[:, :, s, 0:D],
                                            rec[:, :, s:s + 1].to_broadcast([P, H, D]), ALU.mult)
                link(ins)
                after(dve, aoT_mm, t - 1, 1, 1)
                dve.tensor_tensor(ao[:, :].rearrange("p (h d) -> p h d", h=H), On[:, 0, :, :], On[:, 1, :, :],
                                  ALU.add).then_inc(ao_in, 1)
                link.end()

            def residual1(t):
                after(dve, wo_mm, t, 1, 1)
                dve.scalar_tensor_tensor(X[:, t, :], ba[:, 0:HID], tg[:, 0:1], X[:, t, :], ALU.mult, ALU.add).then_inc(x1_in, 1)
                after(dve, x1_in, t, 1, 1)

            def gate(u):
                link = Chain(dve, dve_e, u, 5 + E0)
                after(dve, lg_mm, u, 1, 1)
                l = lg[:, 3, :]
                link(dve.tensor_copy(l, bt[1][:, 0:E0]))
                link(dve.tensor_reduce(lg[:, 0, 0:1], l, AX.X, ALU.max))
                dve.tensor_scalar(lg[:, 0, 1:2], lg[:, 0, 0:1], -1.0, None, ALU.mult).then_inc(l_max, 1)
                link(dve.scalar_tensor_tensor(lg[:, 2, :], l, lg[:, 0, 0:1], CN[:, C_EV:C_EV + 8], ALU.is_equal, ALU.mult))
                link(dve.tensor_reduce(lg[:, 0, 3:4], lg[:, 2, :], AX.X, ALU.max))
                after(dve, l_exp, u, 1, 1)
                dve.reciprocal(lg[:, 0, 4:5], lg[:, 0, 2:3]).then_inc(dve_g, 1)
                after(dve, dve_g, u, 1, 1)
                link(dve.tensor_scalar(lg[:, 0, 5:6], lg[:, 0, 4:5], tg[:, 1:2], None, ALU.mult))
                after(dve, combT_mm, u - 1, 1, 1)
                dve.tensor_scalar(comb[:, :], lg[:, 2, :], lg[:, 0, 3:4], lg[:, 0, 5:6], ALU.is_equal, ALU.mult).then_inc(comb_in, 1)
                assert link.n == 5

            def mix(u):
                link = Chain(dve, dve_e, u, 5 + E0)
                link.n = 5
                after(dve, comb_in, u, 1, 1)
                for n in range(E0 // 2):
                    after(dve, e_mm, u, 5, n + 1)
                    for j in range(2):
                        e = 2 * n + j
                        ins = dve.scalar_tensor_tensor(X[:, u, :], bt[n % 2][:, j * HID:(j + 1) * HID], comb[:, e:e + 1],
                                                       X[:, u, :], ALU.mult, ALU.add)
                        link(ins)
                after(dve, e_mm, u, 5, 5)
                dve.tensor_tensor(X[:, u, :], bo[:, 0:HID], X[:, u, :], ALU.add).then_inc(e_add, 1)
                after(dve, e_add, u, 1, 1)
                link.end()

            def flat(ap):
                return ap.rearrange("p (c b) s -> p c (b s)", c=KT)

            def wkv_args(u):
                link = Chain(dve, dve_f, u, 6)
                after(dve, kk_in, u, 1, 1)
                for i in range(KT * BT):
                    ins = dve.tensor_tensor_scan(Op[:, i, 1:S + 1], wc[:, i // BT:i // BT + 1].to_broadcast([P, S]), kk[:, i, :],
                                                 NEG_INF, ALU.add, ALU.max)
                link(ins)
                link(dve.tensor_tensor(dd[:, :, :].rearrange("p c (b s) -> p (c b) s", b=BT), Op[:, :, 0:S], kk[:, :, :], ALU.subtract))
                for c in range(KT):
                    for i, col in ((0, wc), (1, nuc)):
                        dve.tensor_scalar(AR[:, 0, i, c, :], dd[:, c, :], col[:, c:c + 1], 0.0, ALU.add, ALU.min)
                        ins = dve.tensor_scalar(AR[:, 1, i, c, :], dd[:, c, :], col[:, c:c + 1], 0.0, ALU.add, ALU.max)
                ins.then_inc(arg_in, 1)

            def wkv(u):
                link = Chain(dve, dve_f, u, 6, 2)
                after(dve, dec_exp, u, 3, 3)
                for i in range(KT * BT):
                    c, b = i // BT, i % BT
                    dve.tensor_tensor_scan(PQ[:, 1, i, 1:S + 1], EX[:, 0, c, b * S:(b + 1) * S], VE[:, 0, 1, i, :], 0.0, ALU.mult, ALU.add)
                after(dve, ev_in, u, 2, 1)
                for i in range(KT * BT):
                    c, b = i // BT, i % BT
                    ins = dve.tensor_tensor_scan(PQ[:, 0, i, 1:S + 1], EX[:, 0, c, b * S:(b + 1) * S], VE[:, 0, 0, i, :], 0.0, ALU.mult, ALU.add)
                link(ins)
                for j in range(2):
                    ins = dve.tensor_tensor(ND[:, j, :, :], PQ[:, j, :, 0:S], EX[:, 1, :, :].rearrange("p c (b s) -> p (c b) s", b=BT), ALU.mult)
                link(ins)
                after(dve, ev_in, u, 2, 2)
                for j in range(2):
                    ins = dve.tensor_tensor(ND[:, j, :, :], ND[:, j, :, :], VE[:, 1, j, :, :], ALU.add)
                link(ins)
                link(dve.reciprocal(ND[:, 1, :, :], ND[:, 1, :, :]))
                after(dve, yT_mm, u - 1, 1, 1)
                dve.tensor_tensor(yy[:, :, :], flat(ND[:, 0, :, :]), flat(ND[:, 1, :, :]), ALU.mult).then_inc(y_in, 1)
                link.end()

            def residual3(u):
                after(dve, yT_mm, u, 1, 1)
                dve.scalar_tensor_tensor(X[:, u, :], ba[:, 0:HID], tg[:, 2:3], X[:, u, :], ALU.mult, ALU.add).then_inc(x3_in, 1)
                after(dve, x3_in, u, 1, 1)

            ln_stats(0, 0)
            ln_apply(0, 0)
            rotate_q(0)
            for b in range(BT):
                rotate_k(0, b)
            low_parts(0, 0)
            dve.wait_ge(ld_attn, 16 * 3)
            mask_low(0, 0)
            maxima(0, range(4))
            dve.wait_ge(prep_act, 2)
            dve.wait_ge(ld_ffn, 16 * 7)
            dve.tensor_scalar(nuc[:, :], uc[:, :], -1.0, None, ALU.mult).then_inc(prep, 1)
            dve.wait_ge(prep, 4)

            def tile(t, par, prev, nxt):
                u = t - 1
                if nxt:
                    ln_stats(0, t + 1)
                maxima(t, range(4, 5))
                if prev:
                    residual1(u)
                    ln_stats(1, u)
                if nxt:
                    ln_apply(0, t + 1)
                maxima(t, range(5, 6))
                if prev:
                    ln_apply(1, u)
                maxima(t, range(6, 8))
                shift_low(t)
                if prev:
                    gate(u)
                if nxt:
                    rotate_q(t + 1)
                if prev:
                    mix(u)
                    ln_stats(2, u)
                if nxt:
                    rotate_k(t + 1, 0)
                if prev:
                    ln_apply(2, u)
                if nxt:
                    rotate_k(t + 1, 1)
                if prev:
                    wkv_args(u)
                if nxt:
                    low_parts(t + 1, 1 - par)
                    mask_low(t + 1, 1 - par)
                if prev:
                    wkv(u)
                if nxt:
                    maxima(t + 1, range(2))
                heads(t)
                if nxt:
                    maxima(t + 1, range(2, 3))
                if prev:
                    residual3(u)
                    ln_stats(3, u)
                if nxt:
                    maxima(t + 1, range(3, 4))
                if prev:
                    ln_apply(3, u)

            over_tiles(dve, tile)
            u = NT - 1
            residual1(u)
            ln_stats(1, u)
            ln_apply(1, u)
            gate(u)
            mix(u)
            ln_stats(2, u)
            ln_apply(2, u)
            wkv_args(u)
            wkv(u)
            residual3(u)
            ln_stats(3, u)
            ln_apply(3, u)
            dve.wait_ge(rl_in, NT)

            n_r = [0]

            def step(ins):
                n_r[0] += 1
                ins.then_inc(dve_r, 1)
                dve.wait_ge(dve_r, n_r[0])

            def cols(ap, n, k):
                return ap.rearrange("p (n o) -> p n o", o=1).to_broadcast([P, n, k])

            def rows(ap, n, k):
                return ap.rearrange("p (o k) -> p o k", o=1).to_broadcast([P, n, k])

            step(dve.memset(ones[:, :], 1.0))
            step(dve.tensor_copy(sc[:, :, :], LG[:, :, :]))
            step(dve.tensor_scalar(li[:, :, :], sc[:, :, :], Q_IN, None, ALU.mult))
            step(dve.tensor_copy(sc[:, :, :], li[:, :, :]))
            step(dve.tensor_reduce(small[:, 0, :], sc[:, :, :], AX.X, ALU.max))
            step(dve.tensor_tensor(sc[:, :, :], sc[:, :, :], cols(small[:, 0, :], NT, NE), ALU.subtract))
            step(dve.tensor_scalar(sc[:, :, :], sc[:, :, :], LUT_MIN, None, ALU.max))
            step(dve.scalar_tensor_tensor(key[:, :, :], sc[:, :, :], 8.0, rows(CN[:, C_EV:C_EV + 8], NT, NE), ALU.mult, ALU.add))
            step(dve.tensor_reduce(small[:, 1, :], key[:, :, :], AX.X, ALU.max))
            step(dve.tensor_tensor(oh[:, 0, :, :], key[:, :, :], cols(small[:, 1, :], NT, NE), ALU.is_equal))
            step(dve.scalar_tensor_tensor(key2[:, :, :], oh[:, 0, :, :], -1.0e5, key[:, :, :], ALU.mult, ALU.add))
            step(dve.tensor_reduce(small[:, 2, :], key2[:, :, :], AX.X, ALU.max))
            step(dve.tensor_tensor(oh[:, 1, :, :], key2[:, :, :], cols(small[:, 2, :], NT, NE), ALU.is_equal))
            dve.tensor_tensor(used[:, :, :], oh[:, 0, :, :], oh[:, 1, :, :], ALU.add).then_inc(used_in, 1)
            step(dve.tensor_tensor(tmp[:, 0, :, :], oh[:, 1, :, :], sc[:, :, :], ALU.mult))
            step(dve.tensor_reduce(small[:, 3, :], tmp[:, 0, :, :], AX.X, ALU.add))
            for t in range(NT):
                ins = dve.scalar_tensor_tensor(lutx[:, t, :], CN[:, C_LUTX:C_LUTX + 129], small[:, 3, t:t + 1],
                                               CN[:, C_LUT:C_LUT + 129], ALU.is_equal, ALU.mult, accum_out=small[:, 4, t:t + 1])
            step(ins)
            step(dve.tensor_scalar(small[:, 5, :], small[:, 4, :], Q_OUT, None, ALU.add))
            step(dve.reciprocal(small[:, 6, :], small[:, 5, :]))
            step(dve.tensor_scalar(small[:, 7, :], small[:, 6, :], tg[:, 3:4], None, ALU.mult))
            step(dve.tensor_scalar(wts[:, 0:NT], small[:, 7, :], Q_OUT, None, ALU.mult))
            step(dve.tensor_tensor(wts[:, NT:2 * NT], small[:, 7, :], small[:, 4, :], ALU.mult))
            dve.wait_ge(rk_mm, 1)
            step(dve.memset(cum[:, 0, :], 0.0))
            for t in range(NT):
                step(dve.tensor_tensor(cum[:, t + 1, :], cum[:, t, :], bt[0][:, NT * NE + t * NE:NT * NE + (t + 1) * NE], ALU.add))
            step(dve.tensor_tensor(rank[:, :, :], bt[0][:, 0:NT * NE].rearrange("p (t e) -> p t e", t=NT), cum[:, 0:NT, :], ALU.add))
            step(dve.tensor_tensor(gtj[:, :, :], cols(cum[:, NT, :], NE, NT), rows(CN[:, C_J128:C_J128 + NT], NE, NT), ALU.is_gt))
            step(dve.tensor_reduce(ex[:, 0, :], gtj[:, :, :], AX.X, ALU.add))
            step(dve.memset(ex[:, 3, :], 1.0))
            step(dve.tensor_tensor_scan(ex[:, 1, :], ex[:, 3, :], ex[:, 0, :], 0.0, ALU.mult, ALU.add))
            step(dve.tensor_tensor(ex[:, 2, :], ex[:, 1, :], ex[:, 0, :], ALU.subtract))
            step(dve.scalar_tensor_tensor(rank[:, :, :], rows(ex[:, 2, :], NT, NE), float(P), rank[:, :, :], ALU.mult, ALU.add))
            for k in range(TOPK):
                ins = dve.tensor_tensor(tmp[:, k, :, :], oh[:, k, :, :], rank[:, :, :], ALU.mult)
            step(ins)
            step(dve.tensor_reduce(slot[:, :], tmp[:, :, :, :].rearrange("p k t e -> p (k t) e"), AX.X, ALU.add))
            step(dve.tensor_copy(slot_i[:, :], slot[:, :]))
            dve.tensor_scalar(jt_i[:, :], slot_i[:, :], 7, None, ALU.arith_shift_right)
            step(dve.tensor_scalar(pos_i[:, :], slot_i[:, :], P - 1, None, ALU.bitwise_and))
            dve.tensor_copy(jt[:, :], jt_i[:, :])
            step(dve.tensor_copy(pos[:, :], pos_i[:, :]))
            step(dve.tensor_tensor(ohp[:, :, :], rows(CN[:, C_POS:C_POS + P], TOPK * NT, P), cols(pos[:, :], TOPK * NT, P), ALU.is_equal))
            step(dve.tensor_tensor(val[:, :, 2, :], rows(CN[:, C_POS:C_POS + NJ], TOPK * NT, NJ), cols(jt[:, :], TOPK * NT, NJ), ALU.is_equal))
            for k in range(TOPK):
                h = slice(k * NT, (k + 1) * NT)
                dve.tensor_tensor(val[:, h, 0, :], val[:, h, 2, :], cols(CN[:, C_TOK:C_TOK + NT], NT, NJ), ALU.mult)
            dve.tensor_tensor(val[:, :, 1, :], val[:, :, 2, :], cols(wts[:, :], TOPK * NT, NJ), ALU.mult).then_inc(val_in, 1)
            step(dve.tensor_tensor(ejc[:, :, :], CN[0:1, C_POS:C_POS + NJ].rearrange("p (n o) -> p n o", o=1).to_broadcast([1, NJ, NE]),
                                   ex[0:1, 1, :].rearrange("p (o k) -> p o k", o=1).to_broadcast([1, NJ, NE]), ALU.is_ge))
            step(dve.tensor_reduce(ejs[:, :], ejc[:, :, :], AX.X, ALU.add))
            dve.tensor_scalar(ej[:, :], ejs[:, :], float(NE - 1), None, ALU.min).then_inc(e_of, 1)
            dve.wait_ge(tb_mm, 1)
            step(dve.tensor_copy(tb[:, :, :], bt[1][:, 0:3 * NJ].rearrange("p (k j) -> p k j", k=3)))
            dve.tensor_copy(gi[:, :], tb[:, 0, :]).then_inc(route, 1)
            step(dve.tensor_scalar(so[:, :], tb[:, 2, :], -1.0, 1.0, ALU.mult, ALU.add))
            step(dve.scalar_tensor_tensor(so[:, :], so[:, :], CN[:, C_OWN:C_OWN + 1], tb[:, 0, :], ALU.mult, ALU.add))
            dve.tensor_copy(si[:, :], so[:, :]).then_inc(route, 1)

            def h_turned(j):
                after(dve, hT_mm, j, 2, 2)
                after(dve, y_mm, j - 1, 1, 1)
                dve.tensor_copy(hT[:, 4:IT, :], bc[:, 0:(IT - 4) * P].rearrange("p (i n) -> p i n", i=IT - 4)).then_inc(hT_in_v, 1)

            def gates(j):
                for i in range(2):
                    after(dve, silu, j, 2, i + 1)
                    after(dve, up_mm, j, 4, 2 * i + 2)
                    after(dve, hT_mm, j - 1, 2, 2)
                    dve.tensor_tensor(hh[:, i * IH:(i + 1) * IH], sg[:, i, :], (bs[1], bt[1])[i][:, 0:IH], ALU.mult).then_inc(h_in, 1)

            dve.memset(hh[:, I:IT * P], 0.0).then_inc(zr, 1)
            dve.wait_ge(zr, 2)
            gates(0)
            with dve.Fori(1, NJ) as j:
                h_turned(j - 1)
                gates(j)
            h_turned(NJ - 1)

        @block.tensor
        def _(pe):
            pe.wait_ge(ld_const, 16)

            def transposed(dst, src, done):
                for c in range(KT):
                    ins = pe.transpose(dst[:, c * P:(c + 1) * P], src[:, c * P:(c + 1) * P], ident)
                ins.then_inc(done, 1)

            def turn_hn(t):
                after(pe, ln_done[0], t, 1, 1)
                after(pe, x1_in, t - 2, 1, 1)
                transposed(ba, hn, hnT)

            def project_q(t):
                after(pe, hc_self, t, 1, 1)
                after(pe, m_lo, t - 1, 1, 1)
                for b in range(BT):
                    for c in range(KT):
                        ins = pe.matmul(bb[b * S:(b + 1) * S, 0:HID], HC[:, c, b, 0:S], wq[:, c, :], start=(c == 0), stop=(c == KT - 1))
                ins.then_inc(q_mm, 1)

            def project_kv(t):
                after(pe, hc_ctx, t, KT, KT)
                after(pe, aoT_in, t - 2, 1, 1)
                for b in range(BT):
                    for c in range(KT):
                        ins = pe.matmul((bc, ba)[b][:, :], HC[:, c, b, :], wkv[:, c, :], start=(c == 0), stop=(c == KT - 1))
                    ins.then_inc(kv_mm, 1)

            def turn_qk(t):
                after(pe, q_rot, t, 1, 1)
                after(pe, q_in, t, 1, 1)
                for g in range(G):
                    ins = pe.transpose(bb[:, g * P:(g + 1) * P],
                                       qr[:, g, :, :].rearrange("p o d -> p (o d)"), ident)
                ins.then_inc(qT, 1)
                for b in range(BT):
                    after(pe, k_rot, t, BT, b + 1)
                    after(pe, v_in, t, 4, 2 * b + 2)
                    for g in range(G):
                        ins = pe.transpose((bc, ba)[b][:, g * P:(g + 1) * P],
                                           kr[:, b, g, :, :].rearrange("p o d -> p (o d)"), ident)
                    ins.then_inc(kT, 1)

            def row_scores(t, par, units):
                for n in units:
                    g, b = n // BT, n % BT
                    if n == 0:
                        after(pe, mk_in, t, 1, 1)
                        after(pe, k_hi, t, BT, BT)
                    after(pe, qx, t, G, g + 1)
                    if n >= 2:
                        after(pe, s_max, t, 8, n - 1)
                    else:
                        after(pe, s_max, t - 1, 8, 7 + n)
                    if n == 0:
                        after(pe, kk_in, t - 2, 1, 1)
                    o = bs[n % 2]
                    for p in range(NP):
                        pe.matmul(o[:, p * P:(p + 1) * P], Qx[par][:, g, b, 2 * p:2 * p + 2, :], Kh[par][:, b, g, :],
                                  start=(p == 0), stop=False)
                    pe.matmul(o[:, :].rearrange("p (n k) -> p n k", n=NP)[:, :, 0:S], Idup[:, :],
                              mk2[par][:, b, 0:S].rearrange("p (o k) -> p o k", o=1).to_broadcast([P, NP, S]),
                              start=False, stop=True).then_inc(s_mm, 1)

            def turn_maxima(t):
                after(pe, q_lo, t, 1, 1)
                after(pe, rl_in, t - 2, 1, 1)
                after(pe, s_max, t, 8, 8)
                pe.sem_inc(held, 1)
                pe.transpose(bb[0:2 * H, 0:P], mx[:, :, :, :, :].rearrange("p b s g n -> p (b s g n)"), ident).then_inc(mT, 1)

            def attend(t, par, g, prev):
                for b in range(BT):
                    if g == 0:
                        after(pe, k_lo, t, BT, BT)
                        after(pe, p_exp, t - 1, 8, 8)
                        if prev:
                            after(pe, dve_e, t - 1, 5 + E0, 5 + E0 - 2 * (1 - b))
                    else:
                        after(pe, p_exp, t, 8, 2 * g + b - 1)
                    o = bt[b]
                    q = Qx[par][:, g, b, :, :]
                    pe.matmul(o[:, :], Kl[par][:, b, g, :], q, start=True, stop=False)
                    pe.matmul(o[:, :], Kh[par][:, b, g, :], q, start=False, stop=False)
                    pe.matmul(o[:, :], mk2[par][:, b, :], Idup[:, 0:S].rearrange("p (o q) -> p o q", o=1).to_broadcast([P, HG, S]),
                              start=False, stop=False)
                    if g == 0:
                        after(pe, m_row, t, BT * 64, BT * 64)
                    pe.matmul(o[:, :], Lm[:, :], mrow[:, b, g * 512:(g + 1) * 512], start=False, stop=True).then_inc(t_mm, 1)

            def values(t, par, g, prev):
                after(pe, p_exp, t, 8, 2 * g + 2)
                if g >= 1:
                    after(pe, o_in, t, 8, 2 * g)
                else:
                    after(pe, o_in, t - 1, 8, 8)
                    after(pe, v_in, t, 4, 4)
                    if prev:
                        after(pe, e_add, t - 1, 1, 1)
                for h in range(HG):
                    ins = pe.matmul(bo[:, h * VW:(h + 1) * VW], Pt[:, g * HG + h, :, :],
                                    Vx[par][:, g * HG + h, :, :, :].rearrange("p b s d -> p (b s d)"), start=True, stop=True)
                ins.then_inc(pv_mm, 1)

            def turn_heads(t, nxt):
                after(pe, ao_in, t, 1, 1)
                if nxt:
                    after(pe, k_lo, t + 1, BT, 1)
                transposed(bc, ao, aoT_mm)

            def output(t):
                after(pe, x3_in, t - 1, 1, 1)
                after(pe, aoT_in, t, 1, 1)
                for c in range(KT):
                    ins = pe.matmul(ba[:, 0:HID], aoT[:, c, :], wo[:, c, :], start=(c == 0), stop=(c == KT - 1))
                ins.then_inc(wo_mm, 1)

            def turn_h2(u):
                after(pe, ln_done[1], u, 1, 1)
                after(pe, p_exp, u, 8, 8)
                transposed(bt[0], h2, h2T_mm)

            def gate_logits(u):
                after(pe, h2T_in, u, 1, 1)
                for c in range(KT):
                    ins = pe.matmul(bt[1][:, 0:E0], h2T[:, c, :], wg0[:, c, :], start=(c == 0), stop=(c == KT - 1))
                ins.then_inc(lg_mm, 1)

            def experts0(u):
                after(pe, comb_in, u, 1, 1)
                pe.transpose(bt[1][0:E0, P:2 * P], comb[:, :], ident).then_inc(combT_mm, 1)
                for n in range(E0 // 2):
                    if n == 1:
                        after(pe, combT_in, u, 1, 1)
                    if n >= 2:
                        after(pe, dve_e, u, 5 + E0, 5 + 2 * (n - 1))
                    for c in range(KT):
                        ins = pe.matmul(bt[n % 2][:, :], h2T[:, c, :], w0[:, c, 2 * n:2 * n + 2, :].rearrange("p e n -> p (e n)"),
                                        start=(c == 0), stop=(c == KT - 1))
                    ins.then_inc(e_mm, 1)
                after(pe, o_in, u, 8, 8)
                pe.matmul(bo[:, 0:HID], combT[:, :], b0[:, :], start=True, stop=True).then_inc(e_mm, 1)

            def turn_h3(u):
                after(pe, ln_done[2], u, 1, 1)
                transposed(bs[0], h3, h3T_mm)

            def turn_y(u):
                after(pe, y_in, u, 1, 1)
                for c in range(KT):
                    ins = pe.transpose(ba[:, c * P:(c + 1) * P], yy[:, c, :], ident)
                ins.then_inc(yT_mm, 1)

            def router(u):
                after(pe, ln_done[3], u, 1, 1)
                transposed(bb, h4, h4T_mm)
                after(pe, h4T_in, u, 1, 1)
                for c in range(KT):
                    ins = pe.matmul(bb[:, HID:HID + NE], h4T[:, c, :], wg1[:, c, :], start=(c == 0), stop=(c == KT - 1))
                ins.then_inc(rl_mm, 1)

            pe.wait_ge(prep, 3)
            pe.wait_ge(zeroed, 12)
            turn_hn(0)
            pe.wait_ge(ld_proj, 16 * 3)
            project_q(0)
            project_kv(0)
            turn_qk(0)
            row_scores(0, 0, range(6))
            pe.wait_ge(ld_attn, 16 * 3)
            pe.wait_ge(ld_ffn, 16 * 7)

            def tile(t, par, prev, nxt):
                if nxt:
                    turn_hn(t + 1)
                row_scores(t, par, range(6, 8))
                if prev:
                    turn_h2(t - 1)
                turn_maxima(t)
                if nxt:
                    project_q(t + 1)
                if prev:
                    gate_logits(t - 1)
                if nxt:
                    project_kv(t + 1)
                if prev:
                    experts0(t - 1)
                attend(t, par, 0, prev)
                attend(t, par, 1, prev)
                values(t, par, 0, prev)
                if prev:
                    turn_h3(t - 1)
                if nxt:
                    turn_qk(t + 1)
                attend(t, par, 2, prev)
                values(t, par, 1, prev)
                attend(t, par, 3, prev)
                values(t, par, 2, prev)
                if nxt:
                    row_scores(t + 1, 1 - par, range(2))
                values(t, par, 3, prev)
                if prev:
                    if nxt:
                        after(pe, k_lo, t + 1, BT, BT)
                    turn_y(t - 1)
                if nxt:
                    row_scores(t + 1, 1 - par, range(2, 4))
                turn_heads(t, nxt)
                if nxt:
                    row_scores(t + 1, 1 - par, range(4, 5))
                output(t)
                if prev:
                    if nxt:
                        after(pe, q_lo, t + 1, 1, 1)
                    router(t - 1)
                if nxt:
                    row_scores(t + 1, 1 - par, range(5, 6))

            over_tiles(pe, tile)
            turn_h2(NT - 1)
            gate_logits(NT - 1)
            experts0(NT - 1)
            turn_h3(NT - 1)
            after(pe, x1_in, NT - 1, 1, 1)
            turn_y(NT - 1)
            after(pe, rl_in, NT - 2, 1, 1)
            router(NT - 1)

            pe.wait_ge(used_in, 1)
            u = used[:, :, :].rearrange("p t e -> p (t e)")
            pe.matmul(bt[0][:, 0:NT * NE], CN[:, C_TRI:C_TRI + P], u, start=True, stop=True)
            pe.matmul(bt[0][:, NT * NE:2 * NT * NE], ones[:, :], u, start=True, stop=True).then_inc(rk_mm, 1)
            pe.wait_ge(val_in, 1)
            for i in range(TOPK * NT):
                ins = pe.matmul(bt[1][:, 0:3 * NJ], ohp[:, i, :], val[:, i, :, :].rearrange("p k j -> p (k j)"),
                                start=(i == 0), stop=(i == TOPK * NT - 1))
            ins.then_inc(tb_mm, 1)

            def turn_rows(j):
                after(pe, gathered, j, 16, 16)
                after(pe, xT_in, j - 1, 1, 1)
                for c in range(KT):
                    ins = pe.transpose(ba[:, c * P:(c + 1) * P], xg[:, c * P:(c + 1) * P], ident)
                ins.then_inc(xT_mm, 1)

            def up(j):
                e = pe.value_load(ej[0:1, bass.ts(j, 1)], min_val=0, max_val=NE - 1)
                after(pe, xT_in, j, 1, 1)
                for q, o in enumerate((bs[0], bs[1], bt[0], bt[1])):
                    if q % 2 == 0:
                        after(pe, silu, j - 1, 2, q // 2 + 1)
                    else:
                        after(pe, h_in, j - 1, 2, q // 2 + 1)
                    for c in range(KT):
                        ins = pe.matmul(o[:, 0:IH], xgT[:, c, :], w13[:, c, bass.ts(e, 1), q, :].rearrange("p o n -> p (o n)"),
                                        start=(c == 0), stop=(c == KT - 1))
                    ins.then_inc(up_mm, 1)

            def turn_h(j):
                after(pe, h_in, j, 2, 2)
                after(pe, hT_in_a, j - 1, 1, 1)
                after(pe, hT_in_v, j - 1, 1, 1)
                for i in range(IT):
                    o = bb if i < 4 else bc
                    ins = pe.transpose(o[:, (i % 4) * P:(i % 4 + 1) * P], hh[:, i * P:(i + 1) * P], ident)
                    if i == 3:
                        ins.then_inc(hT_mm, 1)
                ins.then_inc(hT_mm, 1)

            def down(j):
                e = pe.value_load(ej[0:1, bass.ts(j, 1)], min_val=0, max_val=NE - 1)
                after(pe, hT_in_a, j, 1, 1)
                after(pe, hT_in_v, j, 1, 1)
                after(pe, y_sc, j - 1, 1, 1)
                for i in range(IT):
                    k = P if i < IT - 1 else I - (IT - 1) * P
                    ins = pe.matmul(bo[:, 0:HID], hT[0:k, i, :], w2[0:k, i, bass.ts(e, 1), :].rearrange("p o n -> p (o n)"),
                                    start=(i == 0), stop=(i == IT - 1))
                ins.then_inc(y_mm, 1)

            pe.wait_ge(e_of, 1)
            turn_rows(0)
            pe.wait_ge(ld_w13, 16 * KT * NE)
            up(0)
            pe.wait_ge(ld_w2, 16 * 2 * NE)
            with pe.Fori(1, NJ) as j:
                turn_rows(j)
                turn_h(j - 1)
                up(j)
                down(j - 1)
            turn_h(NJ - 1)
            down(NJ - 1)


INS = ["x", "ctxT", "mask", "const", "Wq", "Wkv", "Wo", "gates", "head_gate", "wg", "WT", "b", "w", "u", "wgateT", "w13", "w2T"]


def constants():
    import numpy as np
    c = np.zeros((P, C_N), np.float32)
    c[:, C_ID:C_ID + P] = np.eye(P)
    inv = 1.0 / 10000.0 ** (np.arange(0, D, 2, dtype=np.float32) / D)
    emb = np.outer(np.arange(S, dtype=np.float32), inv)
    emb = np.concatenate([emb, emb], -1)
    cos, sin = np.cos(emb).astype(np.float32), np.sin(emb).astype(np.float32)
    sin[:, :D // 2] *= -1
    scale = np.float32(1 / math.sqrt(D))
    c[:, C_COSQ:C_COSQ + D] = np.tile(cos * scale, (2, 1))
    c[:, C_SINQ:C_SINQ + D] = np.tile(sin * scale, (2, 1))
    c[:S, C_COSK:C_COSK + D] = cos
    c[S:, C_COSK:C_COSK + D] = 1
    c[:S, C_SINK:C_SINK + D] = sin
    c[np.arange(P), C_HM + np.arange(P) % S // D] = 1
    c[:, C_EV:C_EV + 8] = 8 - np.arange(8)
    for r in range(4):
        c[r, C_ONE + S * (r % 2):C_ONE + S * (r % 2) + S] = 1
    n = np.arange(P)
    c[:, C_TRI:C_TRI + P] = n[:, None] < n[None, :]
    c[:, C_POS:C_POS + P] = n
    c[:, C_TOK:C_TOK + NT] = n[:, None] + P * np.arange(NT)
    c[:, C_OWN] = B * S + n
    c[:, C_J128:C_J128 + NT] = P * np.arange(NT)
    lut = np.arange(LUT_MIN, 1, dtype=np.float32)
    c[:, C_LUTX:C_LUTX + 129] = lut
    c[:, C_LUT:C_LUT + 129] = (np.exp(lut / np.float32(Q_IN)) * np.float32(Q_OUT)).astype(np.int32)
    return c


def kernel(x, ctx_2048, mask_Bx1xSxS_fk0, g_xattn, g_ffn, L0_xattn_Wq, L0_xattn_Wk, L0_xattn_Wv, L0_xattn_Wo,
           L0_xattn_gate, L0_ffn_wg, L0_ffn_W, L0_ffn_b, L1_xattn_w, L1_xattn_u, L1_ffn_w_gate, L1_ffn_w1, L1_ffn_w2,
           L1_ffn_w3):
    import numpy as np
    import concourse.bacc as bacc
    from concourse.bass_utils import run_bass_kernel_spmd as run

    f = lambda a: np.ascontiguousarray(np.asarray(a))
    gx, gf = np.asarray(g_xattn), np.asarray(g_ffn)
    arrays = {
        "x": f(x), "ctxT": f(np.asarray(ctx_2048).reshape(B * S, HID).T), "mask": f(mask_Bx1xSxS_fk0), "const": constants(),
        "Wq": f(L0_xattn_Wq), "Wkv": f(np.concatenate([L0_xattn_Wk, L0_xattn_Wv], 1)), "Wo": f(L0_xattn_Wo),
        "gates": f(np.stack([gx[0], gf[0], gx[1], gf[1]])), "head_gate": f(np.asarray(L0_xattn_gate).reshape(-1)),
        "wg": f(L0_ffn_wg), "WT": f(np.asarray(L0_ffn_W).transpose(0, 2, 1)), "b": f(L0_ffn_b),
        "w": f(np.asarray(L1_xattn_w).reshape(KT, P).T), "u": f(np.asarray(L1_xattn_u).reshape(KT, P).T), "wgateT": f(np.asarray(L1_ffn_w_gate).T),
        "w13": f(np.stack([np.asarray(w).transpose(0, 2, 1).reshape(NE, HID, 2, IH) for w in (L1_ffn_w1, L1_ffn_w3)], 3)
                 .reshape(NE, HID, 4, IH)),
        "w2T": f(np.asarray(L1_ffn_w2).transpose(0, 2, 1)),
    }
    nc = bacc.Bacc("TRN2", target_bir_lowering=False, num_devices=1)
    A = {n: nc.dram_tensor(f"in_{n}", a.shape, mybir.dt.from_np(a.dtype), kind="ExternalInput").ap() for n, a in arrays.items()}
    out = nc.dram_tensor("out_x", (B * S + P, HID), F32, kind="ExternalOutput").ap()
    H4 = nc.dram_tensor("normed", (B * S, HID), F32, kind="Internal").ap()
    build(nc, A, out, H4)
    r = run(nc, [{f"in_{n}": a for n, a in arrays.items()}], core_ids=[0])
    return r.results[0]["out_x"][0:B * S].reshape(B, S, HID)
```

```python
import math
from contextlib import ExitStack

import concourse.bass as bass
from concourse import mybir

F32 = mybir.dt.float32
F32R = mybir.dt.float32r
I32 = mybir.dt.int32
ALU = mybir.AluOpType
ACT = mybir.ActivationFunctionType
AX = mybir.AxisListType

B, S, HID, H = 16, 64, 256, 32
D = HID // H
P = 128
BT = 2
NT = B // BT
KT = HID // P
HG = 8
G = H // HG
NP = HG // 2
E0 = 8
NE = 8
VW = BT * 2 * (D + 1)
EPS = 1e-5
NEG_INF = -1e38

C_ID = 0
C_COSQ, C_SINQ, C_COSK, C_SINK = 128, 136, 144, 152
C_HM = 160
C_EV = 168
C_ONE = 176
C_TRI = C_ONE + 128
C_POS = C_TRI + 128
C_TOK = C_POS + 128
C_OWN = C_TOK + NT
C_J128 = C_OWN + 1
C_LUTX = C_J128 + NT
C_LUT = C_LUTX + 129
C_N = C_LUT + 129

TOPK = 2
I = 704
IH = I // 2
IT = -(-I // P)
NJ = (B * S * TOPK + NE * (P - 1)) // P
Q_IN, LUT_MIN, Q_OUT = 128.0, -128.0, 65536.0


def build(nc, A, out, H4):
    x_rows = A["x"].rearrange("b s h -> (b s) h").rearrange("(t p) h -> p t h", p=P)
    ctxT = A["ctxT"].rearrange("(c p) n -> p c n", p=P)
    mask_rows = A["mask"].rearrange("b o q k -> q (b o) k")
    out_rows = out[0:B * S, :].rearrange("(t p) h -> p t h", p=P)
    H4_rows = H4.rearrange("(t p) h -> p t h", p=P)

    ctx = ExitStack()
    with ctx:
        front = ExitStack()
        attn = ExitStack()

        def keep(name, shape, dt=F32):
            return ctx.enter_context(nc.sbuf_tensor(name, shape, dt))

        def sb(name, shape, dt=F32):
            return front.enter_context(nc.sbuf_tensor(name, shape, dt))

        def at(name, shape, dt=F32):
            return attn.enter_context(nc.sbuf_tensor(name, shape, dt, side="right"))

        def late(name, shape, dt=F32):
            return ctx.enter_context(nc.sbuf_tensor(name, shape, dt, side="right"))

        def sem(name):
            return ctx.enter_context(nc.semaphore(name))

        def bank(name):
            return ctx.enter_context(nc.psum_tensor(name, [P, 512], F32))

        LG = keep("LG", [P, NT, NE])
        CN = keep("CN", [P, C_N])
        tg = keep("tg", [P, 4])
        idx_in = keep("idx_in", [P, 1], I32)
        idx_out = keep("idx_out", [P, 1], I32)
        zrow = keep("zrow", [P, HID])
        X = keep("X", [P, NT, HID])
        h4 = [keep(f"h4{i}", [P, HID]) for i in range(2)]
        CT = sb("CT", [P, KT, B * S])
        MK = at("MK", [P, B, S])
        ident = CN[:, C_ID:C_ID + P]
        wq = at("wq", [P, KT, HID])
        wkv = at("wkv", [P, KT, 2 * HID])
        wo = at("wo", [P, KT, HID])
        w0h = sb("w0h", [P, KT, E0, HID], F32R)
        h2h = sb("h2h", [P, KT, P], F32R)
        h2l = sb("h2l", [P, KT, P], F32R)
        b0 = sb("b0", [E0, HID])
        wg0 = sb("wg0", [P, KT, E0])
        wg1 = sb("wg1", [P, KT, NE])
        wc = sb("wc", [P, KT])
        uc = sb("uc", [P, KT])
        nuc = sb("nuc", [P, KT])
        gts = sb("gts", [P, 4])
        hgr = sb("hgr", [P, H])
        thg = sb("thg", [P, H])
        Idup = at("Idup", [P, P], F32R)
        Lm = at("Lm", [P, P], F32R)
        mhalf = sb("mhalf", [P, 1])

        st = sb("st", [P, 4, 6])
        mv = sb("mv", [P, 4, 2])
        rstd = sb("rstd", [P, 4, 2])
        hn = at("hn", [P, HID])
        HC = at("HC", [P, KT, BT, P])
        qw = at("qw", [P, HID])
        kw = at("kw", [P, BT, HID])
        qt = at("qt", [P, HID])
        qt2 = at("qt2", [P, HID])
        qr = at("qr", [P, G, 2, HG * D])
        kt1 = at("kt1", [P, BT, HID])
        kt2 = at("kt2", [P, BT, HID])
        kr = at("kr", [P, BT, G, 2, HG * D])
        Vx = [at(f"Vx{i}", [P, H, BT, 2, D + 1]) for i in range(2)]
        qs = at("qs", [P, G, BT, S], F32R)
        Qx = [at(f"Qx{i}", [P, G, BT, HG, S], F32R) for i in range(2)]
        Kh = [at(f"Kh{i}", [P, BT, G, P], F32R) for i in range(2)]
        Kl = [at(f"Kl{i}", [P, BT, G, P], F32R) for i in range(2)]
        mk2 = [at(f"mk2{i}", [P, BT, P], F32R) for i in range(2)]
        mx = at("mx", [P, BT, 2, G, NP])
        mhl = at("mhl", [BT * 2 * G * NP, 2, P], F32R)
        mrow = at("mrow", [P, BT, H * S], F32R)
        Pt = at("Pt", [P, 2, HG, BT, S])
        Oc = at("Oc", [P, H, 2, D + 1])
        rec = at("rec", [P, H, 2])
        On = at("On", [P, 2, H, D])
        ao = at("ao", [P, HID])
        aoT = at("aoT", [P, KT, P])

        h2 = sb("h2", [P, HID])
        h2T = sb("h2T", [P, KT, P])
        lg = sb("lg", [P, 6, 8])
        comb = sb("comb", [P, E0])
        combT = sb("combT", [E0, P])
        h3 = sb("h3", [P, HID])
        kk = sb("kk", [P, KT * BT, S])
        Op = sb("Op", [P, KT * BT, S + 1])
        dd = sb("dd", [P, KT, BT * S])
        AR = sb("AR", [P, 2, 2, KT, BT * S])
        EX = sb("EX", [P, 2, KT, BT * S])
        VE = sb("VE", [P, 2, 2, KT * BT, S])
        PQ = sb("PQ", [P, 2, KT * BT, S + 1])
        ND = sb("ND", [P, 2, KT * BT, S])
        yy = sb("yy", [P, KT, BT * S])
        h4T = sb("h4T", [P, KT, P])
        w0l = sb("w0l", [P, KT, E0, HID], F32R)
        w0_raw = ((0, 0, E0, Pt[:, :, :, :, :].rearrange("p g h b s -> p (g h b s)").rearrange("p (e n) -> p e n", n=HID)),
                  (1, 0, E0 // 2, AR[:, :, :, :, :].rearrange("p a i c s -> p (a i c s)").rearrange("p (e n) -> p e n", n=HID)),
                  (1, E0 // 2, E0 // 2, VE[:, :, :, :, :].rearrange("p i j c s -> p (i j c s)").rearrange("p (e n) -> p e n", n=HID)))
        front.close()
        attn.close()

        w13 = late("w13", [P, KT, NE, 4, IH])
        w2 = late("w2", [P, IT, NE, HID])
        ones = keep("ones", [P, P])
        li = keep("li", [P, NT, NE], I32)
        sc = keep("sc", [P, NT, NE])
        key = keep("key", [P, NT, NE])
        key2 = keep("key2", [P, NT, NE])
        oh = keep("oh", [P, TOPK, NT, NE])
        tmp = keep("tmp", [P, TOPK, NT, NE])
        small = keep("small", [P, 16, NT])
        lutx = keep("lutx", [P, NT, 129])
        used = keep("used", [P, NT, NE])
        rank = keep("rank", [P, NT, NE])
        cum = keep("cum", [P, NT + 1, NE])
        gtj = keep("gtj", [P, NE, NT])
        ex = keep("ex", [P, 4, NE])
        slot = keep("slot", [P, TOPK * NT])
        slot_i = keep("slot_i", [P, TOPK * NT], I32)
        jt_i = keep("jt_i", [P, TOPK * NT], I32)
        pos_i = keep("pos_i", [P, TOPK * NT], I32)
        jt = keep("jt", [P, TOPK * NT])
        pos = keep("pos", [P, TOPK * NT])
        wts = keep("wts", [P, TOPK * NT])
        ohp = keep("ohp", [P, TOPK * NT, P])
        val = keep("val", [P, TOPK * NT, 3, NJ])
        tb = keep("tb", [P, 3, NJ])
        gi = keep("gi", [P, NJ], I32)
        so = keep("so", [P, NJ])
        si = keep("si", [P, NJ], I32)
        ejc = keep("ejc", [1, NJ, NE])
        ejs = keep("ejs", [1, NJ])
        ej = keep("ej", [1, NJ], I32)
        xg = keep("xg", [P, HID])
        xgT = keep("xgT", [P, KT, P])
        sg = keep("sg", [P, 2, IH])
        hh = keep("hh", [P, IT * P])
        hT = keep("hT", [P, IT, P])
        ys = keep("ys", [P, HID])

        bs = [bank(f"bank_s{i}") for i in range(2)]
        bt = [bank(f"bank_t{i}") for i in range(2)]
        bo, ba, bb, bc = bank("bank_o"), bank("bank_a"), bank("bank_b"), bank("bank_c")

        ld_const, ld_x0, ld_x, ld_gate, ld_proj, ld_attn, ld_ffn = (sem(n) for n in ("ld_const", "ld_x0", "ld_x", "ld_gate", "ld_proj", "ld_attn", "ld_ffn"))
        zeroed, mrow_zero, half_in, prep, prep_act = sem("zeroed"), sem("mrow_zero"), sem("half_in"), sem("prep"), sem("prep_act")
        ln_sync = [sem(f"ln{i}_sync") for i in range(4)]
        gate_step = sem("gate_step")
        held = sem("held")
        ln_eps = [sem(f"ln{i}_eps") for i in range(4)]
        ln_stat = [sem(f"ln{i}_stat") for i in range(4)]
        ln_rstd = [sem(f"ln{i}_rstd") for i in range(4)]
        ln_done = [sem(f"ln{i}_done") for i in range(4)]
        hnT, hc_self, hc_ctx = sem("hnT"), sem("hc_self"), sem("hc_ctx")
        q_in, k_in = sem("q_in"), sem("k_in")
        q_mm, kv_mm, q_rot, k_rot, v_in = sem("q_mm"), sem("kv_mm"), sem("q_rot"), sem("k_rot"), sem("v_in")
        qT, kT, q_hi, k_hi, q_lo, k_lo = sem("qT"), sem("kT"), sem("q_hi"), sem("k_hi"), sem("q_lo"), sem("k_lo")
        qx, mk_in = sem("qx"), sem("mk_in")
        s_mm, s_max, mT, m_hi, m_lo, m_row = sem("s_mm"), sem("s_max"), sem("mT"), sem("m_hi"), sem("m_lo"), sem("m_row")
        t_mm, p_exp, pv_mm, o_in, ao_in = sem("t_mm"), sem("p_exp"), sem("pv_mm"), sem("o_in"), sem("ao_in")
        aoT_mm, aoT_in, wo_mm, x1_in = sem("aoT_mm"), sem("aoT_in"), sem("wo_mm"), sem("x1_in")
        h2T_mm, h2T_in, lg_mm, l_max, l_exp, comb_in = (sem(n) for n in ("h2T_mm", "h2T_in", "lg_mm", "l_max", "l_exp", "comb_in"))
        combT_mm, combT_in, e_mm, e_add = sem("combT_mm"), sem("combT_in"), sem("e_mm"), sem("e_add")
        h3T_mm, kk_in, arg_in, dec_exp, ev_in = sem("h3T_mm"), sem("kk_in"), sem("arg_in"), sem("dec_exp"), sem("ev_in")
        y_in, yT_mm, x3_in = sem("y_in"), sem("yT_mm"), sem("x3_in")
        h4T_mm, h4T_in, rl_mm, rl_in, x_out = sem("h4T_mm"), sem("h4T_in"), sem("rl_mm"), sem("rl_in"), sem("x_out")
        rope_step, heads_step, mix_step, wkv_step, mk_hi = (sem(n) for n in ("rope_step", "heads_step", "mix_step", "wkv_step", "mk_hi"))

        ld_w13, ld_w2, h4_out, z_out, zr = sem("ld_w13"), sem("ld_w2"), sem("h4_out"), sem("z_out"), sem("zr")
        route_step, rk_mm, tb_mm, route, e_of = sem("route_step"), sem("rk_mm"), sem("tb_mm"), sem("route"), sem("e_of")
        nd_mul, nd_sum = sem("nd_mul"), sem("nd_sum")
        w0_hi, w0_lo, h2_hi, h2_lo = sem("w0_hi"), sem("w0_lo"), sem("h2_hi"), sem("h2_lo")
        used_in, val_in, oh_in = sem("used_in"), sem("val_in"), sem("oh_in")
        idx_cp, gathered, xT_mm, xT_in, up_mm, silu, h_in = (sem(n) for n in ("idx_cp", "gathered", "xT_mm", "xT_in", "up_mm", "silu", "h_in"))
        hT_mm, hT_in_a, hT_in_v, y_mm, y_sc, added, idx_cp2 = (sem(n) for n in ("hT_mm", "hT_in_a", "hT_in_v", "y_mm", "y_sc", "added", "idx_cp2"))

        block = ctx.enter_context(nc.Block())

        def after(eng, s, t, per, n):
            if isinstance(t, int):
                if t * per + n > 0:
                    eng.wait_ge(s, t * per + n)
            else:
                eng.wait_ge(s, t * per + n)

        def over_tiles(eng, body):
            body(0, 0, False, False, True)
            body(1, 1, False, True, True)
            with eng.Fori(2, NT - 2, 2) as t:
                body(t, 0, True, True, True)
                body(t + 1, 1, True, True, True)
            body(NT - 2, 0, True, True, True)
            body(NT - 1, 1, True, True, False)

        def wkv_products(eng, u):
            after(eng, dec_exp, u, 3, 3)
            v = CT[:, :, bass.ts(u, P)]
            for i in range(2):
                eng.tensor_tensor(VE[:, i, 0, :, :].rearrange("p (c b) s -> p c (b s)", c=KT),
                                  VE[:, i, 1, :, :].rearrange("p (c b) s -> p c (b s)", c=KT), v,
                                  ALU.mult).then_inc(ev_in, 1)

        def wkv_sums(eng, u):
            after(eng, wkv_step, u, 4, 3)
            for j in range(2):
                eng.tensor_tensor(ND[:, j, :, :], PQ[:, j, :, 0:S], EX[:, 1, :, :].rearrange("p c (b s) -> p (c b) s", b=BT),
                                  ALU.mult).then_inc(nd_mul, 1)
            after(eng, ev_in, u, 2, 2)
            for j in range(2):
                after(eng, nd_mul, u, 2, j + 1)
                eng.tensor_tensor(ND[:, j, :, :], ND[:, j, :, :], VE[:, 1, j, :, :], ALU.add).then_inc(nd_sum, 1)

        class Chain:

            def __init__(self, eng, s, t, per, n=0):
                self.eng, self.s, self.t, self.per, self.n = eng, s, t, per, n

            def __call__(self, ins):
                self.n += 1
                ins.then_inc(self.s, 1)
                self.eng.wait_ge(self.s, self.t * self.per + self.n)

            def end(self):
                assert self.n == self.per, self.n

        @block.sync
        def _(sp):
            sp.dma_start(X[:, 0, :], x_rows[:, 0, :]).then_inc(ld_x0, 16)
            sp.dma_start(CN[:, :], A["const"]).then_inc(ld_const, 16)
            for name, dst in (("Wq", wq), ("Wkv", wkv)):
                sp.dma_start(dst[:, :, :], A[name].rearrange("(c p) n -> p c n", p=P)).then_inc(ld_proj, 16)
            sp.dma_start(CT[:, :, :], ctxT).then_inc(ld_proj, 16)
            for half in range(2):
                sp.dma_start(MK[half * S:(half + 1) * S, :, :], mask_rows).then_inc(ld_attn, 16)
            sp.dma_start(wo[:, :, :], A["Wo"].rearrange("(c p) n -> p c n", p=P)).then_inc(ld_attn, 16)
            sp.dma_start(X[:, 1:NT, :], x_rows[:, 1:NT, :]).then_inc(ld_x, 16)
            sp.dma_start(wc[:, :], A["w"]).then_inc(ld_ffn, 16)
            sp.dma_start(uc[:, :], A["u"]).then_inc(ld_ffn, 16)
            sp.dma_start(b0[:, :], A["b"]).then_inc(ld_ffn, 16)
            sp.dma_start(wg0[:, :, :], A["wg"].rearrange("(c p) n -> p c n", p=P)).then_inc(ld_ffn, 16)
            sp.dma_start(wg1[:, :, :], A["wgateT"].rearrange("(c p) n -> p c n", p=P)).then_inc(ld_ffn, 16)
            for c, e, n, raw in w0_raw:
                sp.dma_start(raw, A["WT"][e:e + n, c * P:(c + 1) * P, :].rearrange("e p n -> p e n")).then_inc(ld_ffn, 16)

            sp.wait_ge(mrow_zero, 1)

            def shift_rows(t):
                after(sp, m_lo, t, 1, 1)
                after(sp, t_mm, t - 1, 8, 8)
                for b in range(BT):
                    for hl in range(2):
                        for s in range(2):
                            r = 2 * hl + s
                            sp.dma_start(mrow[r:r + 1, b, :].rearrange("o (g x) -> o g x", x=P).bitcast(F32),
                                         mhl[32 * b + 16 * s:32 * b + 16 * s + 16, hl, :].bitcast(F32)).then_inc(m_row, 16)

            sp.wait_ge(zr, 1)
            sp.dma_start(out[B * S:B * S + P, :], zrow[:, :]).then_inc(z_out, 16)

            def store(u, par):
                after(sp, x3_in, u, 1, 1)
                sp.dma_start(out_rows[:, u, :], X[:, u, :]).then_inc(x_out, 16)
                after(sp, ln_done[3], u, 1, 1)
                sp.dma_start(H4_rows[:, u, :], h4[par][:, :]).then_inc(h4_out, 16)

            def tile(t, par, prev2, prev, nxt):
                shift_rows(t)
                if prev2:
                    store(t - 2, par)

            over_tiles(sp, tile)
            sp.wait_ge(x1_in, NT)
            for e in range(NE):
                for c in range(KT):
                    sp.dma_start(w13[:, c, e, :, :], A["w13"][e, c * P:(c + 1) * P, :, :]).then_inc(ld_w13, 16)
            sp.wait_ge(e_mm, 5 * NT)
            for e in range(NE):
                sp.dma_start(w2[:, 0:IT - 1, e, :], A["w2T"][e, 0:(IT - 1) * P, :].rearrange("(i p) n -> p i n", p=P)).then_inc(ld_w2, 16)
                sp.dma_start(w2[0:I - (IT - 1) * P, IT - 1, e, :], A["w2T"][e, (IT - 1) * P:I, :]).then_inc(ld_w2, 16)
            sp.wait_ge(z_out, 16)
            sp.wait_ge(added, 16 * NJ)

        @block.gpsimd
        def _(pool):
            pool.memset(mhalf[:, :], -0.5).then_inc(half_in, 1)
            pool.wait_ge(half_in, 1)

            def rstd_of(n, t):
                after(pool, ln_stat[n], t, 1, 1)
                pool.sem_inc(held, 1)
                pool.tensor_scalar_add(rstd[:, n, 0:1], mv[:, n, 1:2], EPS).then_inc(ln_eps[n], 1)
                after(pool, ln_eps[n], t, 1, 1)
                pool.tensor_tensor(rstd[:, n, 1:2], rstd[:, n, 0:1], mhalf[:, :], ALU.pow).then_inc(ln_rstd[n], 1)

            def ctx_of(t):
                after(pool, kv_mm, t - 1, BT, BT)
                for c in range(KT):
                    pool.tensor_copy(HC[:, c, :, S:P], CT[:, c, bass.ts(t, P)].rearrange("p (b k) -> p b k", b=BT)).then_inc(hc_ctx, 1)

            def mask_of(t, par):
                after(pool, t_mm, t - 2, 8, 8)
                pool.tensor_copy(mk2[par][:, :, 0:S], MK[:, bass.ts(t, BT), :]).then_inc(mk_hi, 1)

            def spread(t, par, groups):
                after(pool, q_lo, t, 1, 1)
                after(pool, t_mm, t - 2, 8, 8)
                hm = CN[:, C_HM:C_HM + HG]
                for g in groups:
                    for b in range(BT):
                        ins = pool.tensor_tensor(
                            Qx[par][:, g, b, :, :],
                            qs[:, g, b, :].bitcast(F32).rearrange("p (o q) -> p o q", o=1).to_broadcast([P, HG, S]),
                            hm.rearrange("p (h o) -> p h o", o=1).to_broadcast([P, HG, S]), ALU.mult)
                    ins.then_inc(qx, 1)

            def low_w0():
                for i, (c, e, n, raw) in enumerate(w0_raw):
                    pool.wait_ge(w0_hi, i + 1)
                    pool.tensor_tensor(w0l[:, c, e:e + n, :], raw, w0h[:, c, e:e + n, :].bitcast(F32), ALU.subtract).then_inc(w0_lo, 1)

            def low_h2(u):
                after(pool, h2_hi, u, 1, 1)
                after(pool, h2T_in, u, 1, 1)
                pool.tensor_tensor(h2l[:, :, :], h2T[:, :, :], h2h[:, :, :].bitcast(F32), ALU.subtract).then_inc(h2_lo, 1)

            rstd_of(0, 0)
            pool.memset(mrow[:, :, :].bitcast(F32), 0.0).then_inc(mrow_zero, 1)
            pool.wait_ge(zeroed, 10)
            pool.wait_ge(ld_const, 16)
            pool.wait_ge(ld_proj, 16 * 3)
            ctx_of(0)
            pool.wait_ge(ld_attn, 16 * 3)
            mask_of(0, 0)
            spread(0, 0, range(3))
            rstd_of(0, 1)
            spread(0, 0, range(3, G))

            def tile(t, par, prev2, prev, nxt):
                if nxt and prev:
                    rstd_of(0, t + 1)
                if nxt:
                    ctx_of(t + 1)
                    mask_of(t + 1, 1 - par)
                if not prev:
                    low_w0()
                if prev:
                    rstd_of(1, t - 1)
                    low_h2(t - 1)
                if prev2:
                    rstd_of(3, t - 2)
                if nxt:
                    spread(t + 1, 1 - par, range(2))
                if prev:
                    rstd_of(2, t - 1)
                if nxt:
                    spread(t + 1, 1 - par, range(2, G))
                if prev:
                    wkv_products(pool, t - 1)
                    wkv_sums(pool, t - 1)

            over_tiles(pool, tile)
            rstd_of(3, NT - 2)
            rstd_of(1, NT - 1)
            low_h2(NT - 1)
            rstd_of(2, NT - 1)
            rstd_of(3, NT - 1)

            def gather(j):
                after(pool, xT_mm, j - 1, 1, 1)
                pool.tensor_copy(idx_in[:, :], gi[:, bass.ts(j, 1)]).then_inc(idx_cp, 1)
                after(pool, idx_cp, j, 1, 1)
                pool.sem_inc(held, 1)
                pool.indirect_dma_start(xg[:, :], None, H4, bass.IndirectOffsetOnAxis(ap=idx_in[:, :], axis=0)).then_inc(gathered, 16)

            def add(j):
                after(pool, added, j - 1, 16, 16)
                pool.tensor_copy(idx_out[:, :], si[:, bass.ts(j, 1)]).then_inc(idx_cp2, 1)
                after(pool, idx_cp2, j, 1, 1)
                after(pool, y_sc, j, 1, 1)
                pool.sem_inc(held, 1)
                pool.indirect_dma_start(out, bass.IndirectOffsetOnAxis(ap=idx_out[:, :], axis=0), ys[:, :], None,
                                        compute_op=ALU.add).then_inc(added, 16)

            pool.wait_ge(route, 2)
            pool.wait_ge(h4_out, 16 * NT)
            pool.wait_ge(x_out, 16 * NT)
            pool.wait_ge(z_out, 16)
            gather(0)
            gather(1)

            def slots(j):
                gather(j + 1)
                add(j - 1)

            slots(1)
            with pool.Fori(2, NJ - 1) as j:
                slots(j)
            add(NJ - 2)
            add(NJ - 1)

        @block.scalar
        def _(act):
            def copy(dst, src, scale=1.0):
                return act.activation(dst, src, ACT.Copy, scale=scale)

            act.dma_start(gts[:, 0:4], A["gates"].partition_broadcast(P)).then_inc(ld_gate, 16)
            act.dma_start(hgr[:, :], A["head_gate"].partition_broadcast(P)).then_inc(ld_gate, 16)
            act.wait_ge(ld_gate, 16 * 2)
            act.activation(tg[:, :], gts[:, :], ACT.Tanh).then_inc(prep_act, 1)
            act.activation(thg[:, :], hgr[:, :], ACT.Tanh).then_inc(prep_act, 1)

            def evac_hn(t):
                after(act, hnT, t, 1, 1)
                after(act, kv_mm, t - 1, BT, BT)
                copy(HC[:, :, :, 0:S], ba[:, 0:KT * P].rearrange("p (c b s) -> p c b s", c=KT, b=BT)).then_inc(hc_self, 1)

            def evac_q(t):
                after(act, q_mm, t, 1, 1)
                after(act, q_rot, t - 1, 1, 1)
                copy(qw[:, :], bb[:, 0:HID]).then_inc(q_in, 1)

            def evac_v(t, par, b):
                if b == 0:
                    after(act, pv_mm, t - 2, G, G)
                    after(act, k_rot, t - 1, BT, BT)
                after(act, kv_mm, t, BT, b + 1)
                copy(kw[:, b, :], (bc, ba)[b][:, 0:HID]).then_inc(k_in, 1)
                src = (bc, ba)[b][:, HID:2 * HID].rearrange("p (h d) -> p h d", h=H)
                for s in range(2):
                    r = slice(S * s, S * s + S)
                    copy(Vx[par][r, :, b, s, 0:D], src[r]).then_inc(v_in, 1)

            def evac_qT(t):
                after(act, qT, t, 1, 1)
                after(act, qx, t - 1, G, G)
                copy(qs[:, :, :, :], bb[:, :].rearrange("p (g b s) -> p g b s", g=G, b=BT)).then_inc(q_hi, 1)

            def evac_kT(t, par):
                after(act, t_mm, t - 2, 8, 8)
                for b in range(BT):
                    after(act, kT, t, BT, b + 1)
                    copy(Kh[par][:, b, :, :], (bc, ba)[b][:, :].rearrange("p (g k) -> p g k", g=G)).then_inc(k_hi, 1)

            def shifts(t):
                after(act, m_row, t - 1, BT * 64, BT * 64)
                after(act, mT, t, 1, 1)
                copy(mhl[:, 0, :], bs[0][0:2 * H, 0:P], -1.0).then_inc(m_hi, 1)

            def attend(t, g):
                for b in range(BT):
                    after(act, t_mm, t, 8, 2 * g + b + 1)
                    if b == 0:
                        if g >= 2:
                            after(act, pv_mm, t, G, g - 1)
                        else:
                            after(act, pv_mm, t - 1, G, g + G - 1)
                    act.activation(Pt[:, g % 2, :, b, :], bt[b][:, :].rearrange("p (h q) -> p h q", h=HG),
                                   ACT.Exp).then_inc(p_exp, 1)

            def heads_out(t, g):
                after(act, pv_mm, t, G, g + 1)
                if g == 0:
                    after(act, ao_in, t - 1, 2, 2)
                src = bo[:, 0:HG * VW].rearrange("p (h b s d) -> p h b s d", h=HG, b=BT, s=2)
                for b in range(BT):
                    r = slice(S * b, S * b + S)
                    copy(Oc[r, g * HG:(g + 1) * HG, :, :], src[r, :, b, :, :]).then_inc(o_in, 1)

            def evac_ao(t):
                after(act, aoT_mm, t, 1, 1)
                copy(aoT[:, :, :], bc[:, 0:KT * P].rearrange("p (c n) -> p c n", c=KT)).then_inc(aoT_in, 1)

            def evac_h2(u):
                after(act, h2T_mm, u, 1, 1)
                copy(h2T[:, :, :], bt[0][:, 0:KT * P].rearrange("p (c n) -> p c n", c=KT)).then_inc(h2T_in, 1)

            def high_h2(u):
                copy(h2h[:, :, :], bt[0][:, 0:KT * P].rearrange("p (c n) -> p c n", c=KT)).then_inc(h2_hi, 1)

            def high_w0():
                act.wait_ge(ld_ffn, 16 * 8)
                for c, e, n, raw in w0_raw:
                    copy(w0h[:, c, e:e + n, :], raw).then_inc(w0_hi, 1)

            def gate(u):
                after(act, l_max, u, 1, 1)
                act.activation(lg[:, 1, :], lg[:, 3, :], ACT.Exp, bias=lg[:, 0, 1:2],
                               accum_out=lg[:, 0, 2:3]).then_inc(l_exp, 1)

            def evac_comb(u):
                after(act, combT_mm, u, 1, 1)
                copy(combT[:, :], bt[1][0:E0, P:2 * P]).then_inc(combT_in, 1)

            def evac_kk(u):
                after(act, h3T_mm, u, 1, 1)
                copy(kk[:, :, :], bs[0][:, 0:KT * P].rearrange("p (c s) -> p c s", c=KT * BT)).then_inc(kk_in, 1)

            def decay(u):
                after(act, arg_in, u, 1, 1)
                act.activation(EX[:, :, :, :], AR[:, 0, :, :, :], ACT.Exp).then_inc(dec_exp, 1)
                for i in range(2):
                    act.activation(VE[:, i, 1, :, :].rearrange("p (c b) s -> p c (b s)", c=KT), AR[:, 1, i, :, :], ACT.Exp,
                                   scale=-1.0).then_inc(dec_exp, 1)

            def evac_h4(u):
                after(act, h4T_mm, u, 1, 1)
                copy(h4T[:, :, :], bs[1][:, 0:KT * P].rearrange("p (c n) -> p c n", c=KT)).then_inc(h4T_in, 1)

            def store(u):
                act.wait_ge(x3_in, u + 1)
                act.dma_start(out_rows[:, u, :], X[:, u, :]).then_inc(x_out, 16)
                act.wait_ge(ln_done[3], u + 1)
                act.dma_start(H4_rows[:, u, :], h4[u % 2][:, :]).then_inc(h4_out, 16)

            def router(u):
                after(act, rl_mm, u, 1, 1)
                copy(LG[:, u, :], bs[1][:, HID:HID + NE]).then_inc(rl_in, 1)

            evac_hn(0)
            evac_q(0)
            act.wait_ge(zeroed, 10)
            for b in range(BT):
                evac_v(0, 0, b)
            evac_qT(0)
            evac_kT(0, 0)
            high_w0()

            def tile(t, par, prev2, prev, nxt):
                if nxt:
                    evac_hn(t + 1)
                    evac_q(t + 1)
                if prev:
                    evac_ao(t - 1)
                    evac_h2(t - 1)
                    high_h2(t - 1)
                shifts(t)
                if nxt:
                    evac_v(t + 1, 1 - par, 0)
                if prev:
                    gate(t - 1)
                if nxt:
                    evac_qT(t + 1)
                    evac_v(t + 1, 1 - par, 1)
                if prev:
                    evac_comb(t - 1)
                else:
                    act.wait_ge(w0_lo, 1)
                attend(t, 0)
                if prev2:
                    evac_h4(t - 2)
                attend(t, 1)
                heads_out(t, 0)
                if prev2:
                    router(t - 2)
                if prev:
                    evac_kk(t - 1)
                if nxt:
                    evac_kT(t + 1, 1 - par)
                if prev:
                    decay(t - 1)
                attend(t, 2)
                heads_out(t, 1)
                attend(t, 3)
                heads_out(t, 2)
                heads_out(t, 3)

            over_tiles(act, tile)
            evac_ao(NT - 1)
            evac_h4(NT - 2)
            router(NT - 2)
            evac_h2(NT - 1)
            high_h2(NT - 1)
            store(NT - 2)
            gate(NT - 1)
            evac_comb(NT - 1)
            evac_kk(NT - 1)
            decay(NT - 1)
            store(NT - 1)
            evac_h4(NT - 1)
            router(NT - 1)

            def rows_in(j):
                after(act, xT_mm, j, 1, 1)
                after(act, up_mm, j - 1, 4, 4)
                copy(xgT[:, :, :], ba[:, 0:KT * P].rearrange("p (c n) -> p c n", c=KT)).then_inc(xT_in, 1)

            def h_turned(j):
                after(act, hT_mm, j, 2, 1)
                after(act, y_mm, j - 1, 1, 1)
                copy(hT[:, 0:4, :], bb[:, :].rearrange("p (i n) -> p i n", i=4)).then_inc(hT_in_a, 1)

            def gates(j):
                for i in range(2):
                    after(act, up_mm, j, 4, 2 * i + 1)
                    after(act, h_in, j - 1, 2, i + 1)
                    act.activation(sg[:, i, :], (bs[0], bt[0])[i][:, 0:IH], ACT.Silu).then_inc(silu, 1)

            def scaled(j):
                after(act, y_mm, j, 1, 1)
                after(act, added, j - 1, 16, 16)
                act.activation(ys[:, :], bo[:, 0:HID], ACT.Copy, scale=tb[:, 1, bass.ts(j, 1)]).then_inc(y_sc, 1)

            act.wait_ge(route, 2)
            rows_in(0)
            gates(0)
            rows_in(1)

            def slots(j):
                h_turned(j - 1)
                gates(j)
                rows_in(j + 1)
                scaled(j - 1)

            slots(1)
            with act.Fori(2, NJ - 1) as j:
                slots(j)
            h_turned(NJ - 2)
            gates(NJ - 1)
            scaled(NJ - 2)
            h_turned(NJ - 1)
            scaled(NJ - 1)

        @block.vector
        def _(dve):
            dve.memset(zrow[:, :], 0.0).then_inc(zr, 1)
            for i in range(2):
                dve.memset(Vx[i][:, :, :, :, :], 0.0).then_inc(zeroed, 1)
                dve.memset(mk2[i][:, :, :].bitcast(F32), 0.0).then_inc(zeroed, 1)
            dve.memset(Op[:, :, 0:1], NEG_INF).then_inc(zeroed, 1)
            dve.memset(PQ[:, :, :, 0:1], 0.0).then_inc(zeroed, 1)

            def ln_stats(n, t):
                dve.sem_inc(held, 1)
                dve.bn_stats(st[:, n, :], X[:, t, :]).then_inc(ln_sync[n], 1)
                after(dve, ln_sync[n], t, 1, 1)
                dve.sem_inc(held, 1)
                dve.bn_aggr(mv[:, n, :], st[:, n, :]).then_inc(ln_stat[n], 1)

            def ln_apply(n, t, par=0):
                if n < 3:
                    after(dve, (hnT, h2T_mm, h3T_mm)[n], t - 1, 1, 1)
                after(dve, ln_rstd[n], t, 1, 1)
                after(dve, ln_stat[n], t, 1, 1)
                dve.tensor_scalar((hn, h2, h3, h4[par])[n][:, :], X[:, t, :], mv[:, n, 0:1], rstd[:, n, 1:2],
                                  ALU.subtract, ALU.mult).then_inc(ln_done[n], 1)

            def twice(ap):
                return ap.rearrange("p (g o d) -> p g o d", g=G, o=1).to_broadcast([P, G, 2, HG * D])

            def rope(src, cos, sin, t1, t2):
                v = src.rearrange("p (h d) -> p h d", h=H)

                def bc3(c, n):
                    return c.rearrange("p (o d) -> p o d", o=1).to_broadcast([P, H, n])

                a = t1.rearrange("p (h d) -> p h d", h=H)
                z = t2.rearrange("p (h d) -> p h d", h=H)
                h = D // 2
                dve.tensor_tensor(a, v, bc3(CN[:, cos:cos + D], D), ALU.mult)
                dve.tensor_tensor(z[:, :, 0:h], v[:, :, h:D], bc3(CN[:, sin:sin + h], h), ALU.mult)
                return dve.tensor_tensor(z[:, :, h:D], v[:, :, 0:h], bc3(CN[:, sin + h:sin + D], h), ALU.mult)

            def rotate_q(t):
                link = Chain(dve, rope_step, t, 1 + BT)
                after(dve, q_in, t, 1, 1)
                link(rope(qw[:, :], C_COSQ, C_SINQ, qt[:, :], qt2[:, :]))
                after(dve, qT, t - 1, 1, 1)
                dve.tensor_tensor(qr[:, :, :, :], twice(qt[:, :]), twice(qt2[:, :]), ALU.add).then_inc(q_rot, 1)

            def rotate_k(t, b):
                link = Chain(dve, rope_step, t, 1 + BT, 1 + b)
                after(dve, k_in, t, BT, b + 1)
                link(rope(kw[:, b, :], C_COSK, C_SINK, kt1[:, b, :], kt2[:, b, :]))
                after(dve, kT, t - 1, BT, BT)
                dve.tensor_tensor(kr[:, b, :, :, :], twice(kt1[:, b, :]), twice(kt2[:, b, :]), ALU.add).then_inc(k_rot, 1)

            def low_q(t):
                after(dve, q_hi, t, 1, 1)
                after(dve, qx, t - 1, G, G)
                dve.tensor_tensor(qs[S:P, :, :, :], bb[S:P, :].rearrange("p (g b s) -> p g b s", g=G, b=BT),
                                  qs[S:P, :, :, :].bitcast(F32), ALU.subtract).then_inc(q_lo, 1)

            def low_k(t, par):
                after(dve, t_mm, t - 2, 8, 8)
                for b in range(BT):
                    after(dve, k_hi, t, BT, b + 1)
                    dve.tensor_tensor(Kl[par][:, b, :, :], (bc, ba)[b][:, :].rearrange("p (g k) -> p g k", g=G),
                                      Kh[par][:, b, :, :].bitcast(F32), ALU.subtract).then_inc(k_lo, 1)

            def mask_low(t, par):
                after(dve, mk_hi, t, 1, 1)
                dve.tensor_tensor(mk2[par][S:P, :, 0:S], MK[S:P, bass.ts(t, BT), :], mk2[par][S:P, :, 0:S].bitcast(F32),
                                  ALU.subtract).then_inc(mk_in, 1)

            def maxima(t, units):
                for n in units:
                    g, b = n // BT, n % BT
                    after(dve, s_mm, t, 8, n + 1)
                    if n == 0:
                        after(dve, mT, t - 1, 1, 1)
                    dve.tensor_reduce(mx[:, b, :, g, :].rearrange("p s n -> p n s"),
                                      bs[n % 2][:, :].rearrange("p (n s k) -> p n s k", n=NP, s=2),
                                      AX.X, ALU.max).then_inc(s_max, 1)

            def shift_low(t):
                after(dve, m_row, t - 1, BT * 64, BT * 64)
                after(dve, m_hi, t, 1, 1)
                dve.scalar_tensor_tensor(mhl[:, 1, :], bs[0][0:2 * H, 0:P], -1.0, mhl[:, 0, :].bitcast(F32),
                                         ALU.mult, ALU.subtract).then_inc(m_lo, 1)

            def heads(t, part):
                r = (slice(0, H - HG), slice(H - HG, H))[part]
                n = r.stop - r.start
                link = Chain(dve, heads_step, t, 6, 3 * part)
                after(dve, o_in, t, 8, (6, 8)[part])
                link(dve.reciprocal(rec[:, r, :], Oc[:, r, :, D]))
                link(dve.tensor_tensor(rec[:, r, 1], rec[:, r, 1], thg[:, r], ALU.mult))
                for s in range(2):
                    ins = dve.tensor_tensor(On[:, s, r, :], Oc[:, r, s, 0:D],
                                            rec[:, r, s:s + 1].to_broadcast([P, n, D]), ALU.mult)
                link(ins)
                after(dve, aoT_mm, t - 1, 1, 1)
                dve.tensor_tensor(ao[:, r.start * D:r.stop * D].rearrange("p (h d) -> p h d", h=n), On[:, 0, r, :], On[:, 1, r, :],
                                  ALU.add).then_inc(ao_in, 1)

            def residual1(t):
                after(dve, wo_mm, t, 1, 1)
                dve.scalar_tensor_tensor(X[:, t, :], ba[:, 0:HID], tg[:, 0:1], X[:, t, :], ALU.mult, ALU.add).then_inc(x1_in, 1)
                after(dve, x1_in, t, 1, 1)

            def gate(u):
                link = Chain(dve, mix_step, u, 5 + E0)
                after(dve, lg_mm, u, 1, 1)
                l = lg[:, 3, :]
                link(dve.tensor_copy(l, bt[1][:, 0:E0]))
                link(dve.tensor_reduce(lg[:, 0, 0:1], l, AX.X, ALU.max))
                dve.tensor_scalar(lg[:, 0, 1:2], lg[:, 0, 0:1], -1.0, None, ALU.mult).then_inc(l_max, 1)
                link(dve.scalar_tensor_tensor(lg[:, 2, :], l, lg[:, 0, 0:1], CN[:, C_EV:C_EV + 8], ALU.is_equal, ALU.mult))
                link(dve.tensor_reduce(lg[:, 0, 3:4], lg[:, 2, :], AX.X, ALU.max))
                after(dve, l_exp, u, 1, 1)
                dve.reciprocal(lg[:, 0, 4:5], lg[:, 0, 2:3]).then_inc(gate_step, 1)
                after(dve, gate_step, u, 1, 1)
                link(dve.tensor_scalar(lg[:, 0, 5:6], lg[:, 0, 4:5], tg[:, 1:2], None, ALU.mult))
                after(dve, combT_mm, u - 1, 1, 1)
                dve.tensor_scalar(comb[:, :], lg[:, 2, :], lg[:, 0, 3:4], lg[:, 0, 5:6], ALU.is_equal, ALU.mult).then_inc(comb_in, 1)
                assert link.n == 5

            def mix(u, n):
                link = Chain(dve, mix_step, u, 5 + E0, 5 + 2 * n)
                if n == 0:
                    after(dve, comb_in, u, 1, 1)
                after(dve, e_mm, u, 5, n + 1)
                for j in range(2):
                    e = 2 * n + j
                    link(dve.scalar_tensor_tensor(X[:, u, :], bt[n % 2][:, j * HID:(j + 1) * HID], comb[:, e:e + 1],
                                                  X[:, u, :], ALU.mult, ALU.add))

            def mix_bias(u):
                after(dve, e_mm, u, 5, 5)
                dve.tensor_tensor(X[:, u, :], bo[:, 0:HID], X[:, u, :], ALU.add).then_inc(e_add, 1)
                after(dve, e_add, u, 1, 1)

            def flat(ap):
                return ap.rearrange("p (c b) s -> p c (b s)", c=KT)

            def wkv_args(u):
                link = Chain(dve, wkv_step, u, 4)
                after(dve, kk_in, u, 1, 1)
                for i in range(KT * BT):
                    ins = dve.tensor_tensor_scan(Op[:, i, 1:S + 1], wc[:, i // BT:i // BT + 1].to_broadcast([P, S]), kk[:, i, :],
                                                 NEG_INF, ALU.add, ALU.max)
                link(ins)
                link(dve.tensor_tensor(dd[:, :, :].rearrange("p c (b s) -> p (c b) s", b=BT), Op[:, :, 0:S], kk[:, :, :], ALU.subtract))
                for c in range(KT):
                    for i, col in ((0, wc), (1, nuc)):
                        dve.tensor_scalar(AR[:, 0, i, c, :], dd[:, c, :], col[:, c:c + 1], 0.0, ALU.add, ALU.min)
                        ins = dve.tensor_scalar(AR[:, 1, i, c, :], dd[:, c, :], col[:, c:c + 1], 0.0, ALU.add, ALU.max)
                ins.then_inc(arg_in, 1)

            def wkv_scans(u):
                link = Chain(dve, wkv_step, u, 4, 2)
                after(dve, dec_exp, u, 3, 3)
                for i in range(KT * BT):
                    c, b = i // BT, i % BT
                    dve.tensor_tensor_scan(PQ[:, 1, i, 1:S + 1], EX[:, 0, c, b * S:(b + 1) * S], VE[:, 0, 1, i, :], 0.0, ALU.mult, ALU.add)
                after(dve, ev_in, u, 2, 1)
                for i in range(KT * BT):
                    c, b = i // BT, i % BT
                    ins = dve.tensor_tensor_scan(PQ[:, 0, i, 1:S + 1], EX[:, 0, c, b * S:(b + 1) * S], VE[:, 0, 0, i, :], 0.0, ALU.mult, ALU.add)
                link(ins)

            def wkv_inverse(u):
                link = Chain(dve, wkv_step, u, 4, 3)
                after(dve, nd_sum, u, 2, 2)
                link(dve.reciprocal(ND[:, 1, :, :], ND[:, 1, :, :]))
                link.end()

            def wkv_out(u):
                dve.tensor_tensor(yy[:, :, :], flat(ND[:, 0, :, :]), flat(ND[:, 1, :, :]), ALU.mult).then_inc(y_in, 1)

            def residual3(u):
                after(dve, yT_mm, u, 1, 1)
                dve.scalar_tensor_tensor(X[:, u, :], bs[1][:, 0:HID], tg[:, 2:3], X[:, u, :], ALU.mult, ALU.add).then_inc(x3_in, 1)
                after(dve, x3_in, u, 1, 1)

            dve.wait_ge(ld_x0, 16)
            ln_stats(0, 0)
            ln_apply(0, 0)
            dve.wait_ge(zeroed, 6)
            for i in range(2):
                dve.memset(Vx[i][0:S, :, :, 0, D:D + 1], 1.0).then_inc(zeroed, 1)
                dve.memset(Vx[i][S:P, :, :, 1, D:D + 1], 1.0).then_inc(zeroed, 1)
            dve.wait_ge(ld_const, 16)
            dve.tensor_tensor(Idup[:, 0:S], CN[:, C_ID:C_ID + S], CN[:, C_ID + S:C_ID + P], ALU.add).then_inc(prep, 1)
            dve.tensor_tensor(Idup[:, S:P], CN[:, C_ID:C_ID + S], CN[:, C_ID + S:C_ID + P], ALU.add).then_inc(prep, 1)
            dve.tensor_copy(Lm[:, :], CN[:, C_ONE:C_ONE + P]).then_inc(prep, 1)
            dve.wait_ge(prep, 3)
            rotate_q(0)
            for b in range(BT):
                rotate_k(0, b)
            low_q(0)
            low_k(0, 0)
            dve.wait_ge(ld_attn, 16 * 3)
            mask_low(0, 0)
            maxima(0, range(2))
            dve.wait_ge(ld_x, 16)
            dve.wait_ge(prep_act, 2)
            dve.wait_ge(ld_ffn, 16 * 8)
            dve.tensor_scalar(nuc[:, :], uc[:, :], -1.0, None, ALU.mult).then_inc(prep, 1)
            dve.wait_ge(prep, 4)

            def tile(t, par, prev2, prev, nxt):
                u, w = t - 1, t - 2
                if nxt:
                    ln_stats(0, t + 1)
                maxima(t, range(2, 3))
                if nxt:
                    ln_apply(0, t + 1)
                if prev:
                    heads(u, 0)
                maxima(t, range(3, 4))
                if prev:
                    heads(u, 1)
                maxima(t, range(4, 6))
                if prev:
                    residual1(u)
                    ln_stats(1, u)
                maxima(t, range(6, 7))
                if prev:
                    ln_apply(1, u)
                maxima(t, range(7, 8))
                if nxt:
                    rotate_q(t + 1)
                shift_low(t)
                if prev:
                    gate(u)
                if prev2:
                    wkv_inverse(w)
                if prev2:
                    wkv_out(w)
                if prev:
                    mix(u, 0)
                if nxt:
                    low_q(t + 1)
                if prev:
                    mix(u, 1)
                if prev2:
                    residual3(w)
                    ln_stats(3, w)
                if prev:
                    mix(u, 2)
                if prev2:
                    ln_apply(3, w, par)
                if prev:
                    mix(u, 3)
                    mix_bias(u)
                    ln_stats(2, u)
                if nxt:
                    rotate_k(t + 1, 0)
                if prev:
                    ln_apply(2, u)
                if nxt:
                    rotate_k(t + 1, 1)
                    mask_low(t + 1, 1 - par)
                if prev:
                    wkv_args(u)
                if nxt:
                    low_k(t + 1, 1 - par)
                if prev:
                    wkv_scans(u)
                if prev2:
                    after(dve, h4_out, w, 16, 16)
                if nxt:
                    maxima(t + 1, range(2))

            over_tiles(dve, tile)
            u, w = NT - 1, NT - 2
            wkv_inverse(w)
            wkv_out(w)
            residual3(w)
            ln_stats(3, w)
            heads(u, 0)
            heads(u, 1)
            ln_apply(3, w, w % 2)
            residual1(u)
            ln_stats(1, u)
            ln_apply(1, u)
            gate(u)
            for n in range(3):
                mix(u, n)
            mix(u, 3)
            mix_bias(u)
            ln_stats(2, u)
            ln_apply(2, u)
            wkv_args(u)
            wkv_products(dve, u)
            wkv_scans(u)
            wkv_sums(dve, u)
            wkv_inverse(u)
            wkv_out(u)
            residual3(u)
            ln_stats(3, u)
            ln_apply(3, u, u % 2)
            dve.wait_ge(rl_in, NT)

            n_r = [0]

            def step(ins):
                n_r[0] += 1
                ins.then_inc(route_step, 1)
                dve.wait_ge(route_step, n_r[0])

            def cols(ap, n, k):
                return ap.rearrange("p (n o) -> p n o", o=1).to_broadcast([P, n, k])

            def rows(ap, n, k):
                return ap.rearrange("p (o k) -> p o k", o=1).to_broadcast([P, n, k])

            step(dve.memset(ones[:, :], 1.0))
            step(dve.tensor_copy(sc[:, :, :], LG[:, :, :]))
            step(dve.tensor_scalar(li[:, :, :], sc[:, :, :], Q_IN, None, ALU.mult))
            step(dve.tensor_copy(sc[:, :, :], li[:, :, :]))
            step(dve.tensor_reduce(small[:, 0, :], sc[:, :, :], AX.X, ALU.max))
            step(dve.tensor_tensor(sc[:, :, :], sc[:, :, :], cols(small[:, 0, :], NT, NE), ALU.subtract))
            step(dve.tensor_scalar(sc[:, :, :], sc[:, :, :], LUT_MIN, None, ALU.max))
            step(dve.scalar_tensor_tensor(key[:, :, :], sc[:, :, :], 8.0, rows(CN[:, C_EV:C_EV + 8], NT, NE), ALU.mult, ALU.add))
            step(dve.tensor_reduce(small[:, 1, :], key[:, :, :], AX.X, ALU.max))
            step(dve.tensor_tensor(oh[:, 0, :, :], key[:, :, :], cols(small[:, 1, :], NT, NE), ALU.is_equal))
            step(dve.scalar_tensor_tensor(key2[:, :, :], oh[:, 0, :, :], -1.0e5, key[:, :, :], ALU.mult, ALU.add))
            step(dve.tensor_reduce(small[:, 2, :], key2[:, :, :], AX.X, ALU.max))
            step(dve.tensor_tensor(oh[:, 1, :, :], key2[:, :, :], cols(small[:, 2, :], NT, NE), ALU.is_equal))
            dve.tensor_tensor(used[:, :, :], oh[:, 0, :, :], oh[:, 1, :, :], ALU.add).then_inc(used_in, 1)
            step(dve.tensor_tensor(tmp[:, 0, :, :], oh[:, 1, :, :], sc[:, :, :], ALU.mult))
            step(dve.tensor_reduce(small[:, 3, :], tmp[:, 0, :, :], AX.X, ALU.add))
            for t in range(NT):
                ins = dve.scalar_tensor_tensor(lutx[:, t, :], CN[:, C_LUTX:C_LUTX + 129], small[:, 3, t:t + 1],
                                               CN[:, C_LUT:C_LUT + 129], ALU.is_equal, ALU.mult, accum_out=small[:, 4, t:t + 1])
            step(ins)
            step(dve.tensor_scalar(small[:, 5, :], small[:, 4, :], Q_OUT, None, ALU.add))
            step(dve.reciprocal(small[:, 6, :], small[:, 5, :]))
            step(dve.tensor_scalar(small[:, 7, :], small[:, 6, :], tg[:, 3:4], None, ALU.mult))
            step(dve.tensor_scalar(wts[:, 0:NT], small[:, 7, :], Q_OUT, None, ALU.mult))
            step(dve.tensor_tensor(wts[:, NT:2 * NT], small[:, 7, :], small[:, 4, :], ALU.mult))
            dve.wait_ge(rk_mm, 1)
            step(dve.memset(cum[:, 0, :], 0.0))
            for t in range(NT):
                step(dve.tensor_tensor(cum[:, t + 1, :], cum[:, t, :], bt[0][:, NT * NE + t * NE:NT * NE + (t + 1) * NE], ALU.add))
            step(dve.tensor_tensor(rank[:, :, :], bt[0][:, 0:NT * NE].rearrange("p (t e) -> p t e", t=NT), cum[:, 0:NT, :], ALU.add))
            step(dve.tensor_tensor(gtj[:, :, :], cols(cum[:, NT, :], NE, NT), rows(CN[:, C_J128:C_J128 + NT], NE, NT), ALU.is_gt))
            step(dve.tensor_reduce(ex[:, 0, :], gtj[:, :, :], AX.X, ALU.add))
            step(dve.memset(ex[:, 3, :], 1.0))
            step(dve.tensor_tensor_scan(ex[:, 1, :], ex[:, 3, :], ex[:, 0, :], 0.0, ALU.mult, ALU.add))
            step(dve.tensor_tensor(ex[:, 2, :], ex[:, 1, :], ex[:, 0, :], ALU.subtract))
            step(dve.scalar_tensor_tensor(rank[:, :, :], rows(ex[:, 2, :], NT, NE), float(P), rank[:, :, :], ALU.mult, ALU.add))
            for k in range(TOPK):
                ins = dve.tensor_tensor(tmp[:, k, :, :], oh[:, k, :, :], rank[:, :, :], ALU.mult)
            step(ins)
            step(dve.tensor_reduce(slot[:, :], tmp[:, :, :, :].rearrange("p k t e -> p (k t) e"), AX.X, ALU.add))
            step(dve.tensor_copy(slot_i[:, :], slot[:, :]))
            dve.tensor_scalar(jt_i[:, :], slot_i[:, :], 7, None, ALU.arith_shift_right)
            step(dve.tensor_scalar(pos_i[:, :], slot_i[:, :], P - 1, None, ALU.bitwise_and))
            dve.tensor_copy(jt[:, :], jt_i[:, :])
            step(dve.tensor_copy(pos[:, :], pos_i[:, :]))
            step(dve.tensor_tensor(val[:, :, 2, :], rows(CN[:, C_POS:C_POS + NJ], TOPK * NT, NJ), cols(jt[:, :], TOPK * NT, NJ), ALU.is_equal))
            for k in range(TOPK):
                h = slice(k * NT, (k + 1) * NT)
                dve.tensor_tensor(val[:, h, 0, :], val[:, h, 2, :], cols(CN[:, C_TOK:C_TOK + NT], NT, NJ), ALU.mult)
            dve.tensor_tensor(val[:, :, 1, :], val[:, :, 2, :], cols(wts[:, :], TOPK * NT, NJ), ALU.mult).then_inc(val_in, 1)
            for q in range(4):
                h = slice(4 * q, 4 * q + 4)
                dve.tensor_tensor(ohp[:, h, :], rows(CN[:, C_POS:C_POS + P], 4, P), cols(pos[:, h], 4, P), ALU.is_equal).then_inc(oh_in, 1)
            step(dve.tensor_tensor(ejc[:, :, :], CN[0:1, C_POS:C_POS + NJ].rearrange("p (n o) -> p n o", o=1).to_broadcast([1, NJ, NE]),
                                   ex[0:1, 1, :].rearrange("p (o k) -> p o k", o=1).to_broadcast([1, NJ, NE]), ALU.is_ge))
            step(dve.tensor_reduce(ejs[:, :], ejc[:, :, :], AX.X, ALU.add))
            dve.tensor_scalar(ej[:, :], ejs[:, :], float(NE - 1), None, ALU.min).then_inc(e_of, 1)
            dve.wait_ge(tb_mm, 1)
            step(dve.tensor_copy(tb[:, :, :], bt[1][:, 0:3 * NJ].rearrange("p (k j) -> p k j", k=3)))
            dve.tensor_copy(gi[:, :], tb[:, 0, :]).then_inc(route, 1)
            step(dve.tensor_scalar(so[:, :], tb[:, 2, :], -1.0, 1.0, ALU.mult, ALU.add))
            step(dve.scalar_tensor_tensor(so[:, :], so[:, :], CN[:, C_OWN:C_OWN + 1], tb[:, 0, :], ALU.mult, ALU.add))
            dve.tensor_copy(si[:, :], so[:, :]).then_inc(route, 1)

            def h_turned(j):
                after(dve, hT_mm, j, 2, 2)
                after(dve, y_mm, j - 1, 1, 1)
                dve.tensor_copy(hT[:, 4:IT, :], bc[:, 0:(IT - 4) * P].rearrange("p (i n) -> p i n", i=IT - 4)).then_inc(hT_in_v, 1)

            def gates(j):
                for i in range(2):
                    after(dve, silu, j, 2, i + 1)
                    after(dve, up_mm, j, 4, 2 * i + 2)
                    after(dve, hT_mm, j - 1, 2, 2)
                    dve.tensor_tensor(hh[:, i * IH:(i + 1) * IH], sg[:, i, :], (bs[1], bt[1])[i][:, 0:IH], ALU.mult).then_inc(h_in, 1)

            dve.memset(hh[:, I:IT * P], 0.0).then_inc(zr, 1)
            dve.wait_ge(zr, 2)
            gates(0)

            def slots(j):
                h_turned(j - 1)
                gates(j)

            slots(1)
            with dve.Fori(2, NJ) as j:
                slots(j)
            h_turned(NJ - 1)

        @block.tensor
        def _(pe):
            pe.wait_ge(ld_const, 16)

            def transposed(dst, src, done):
                for c in range(KT):
                    ins = pe.transpose(dst[:, c * P:(c + 1) * P], src[:, c * P:(c + 1) * P], ident)
                ins.then_inc(done, 1)

            def turn_hn(t):
                after(pe, ln_done[0], t, 1, 1)
                after(pe, k_lo, t - 1, BT, BT)
                transposed(ba, hn, hnT)

            def project_q(t):
                after(pe, hc_self, t, 1, 1)
                after(pe, q_lo, t - 1, 1, 1)
                for b in range(BT):
                    for c in range(KT):
                        ins = pe.matmul(bb[b * S:(b + 1) * S, 0:HID], HC[:, c, b, 0:S], wq[:, c, :], start=(c == 0), stop=(c == KT - 1))
                ins.then_inc(q_mm, 1)

            def project_kv(t, b):
                if b == 0:
                    after(pe, hc_ctx, t, KT, KT)
                    after(pe, aoT_in, t - 2, 1, 1)
                else:
                    after(pe, x1_in, t - 2, 1, 1)
                for c in range(KT):
                    ins = pe.matmul((bc, ba)[b][:, :], HC[:, c, b, :], wkv[:, c, :], start=(c == 0), stop=(c == KT - 1))
                ins.then_inc(kv_mm, 1)

            def turn_q(t):
                after(pe, q_rot, t, 1, 1)
                after(pe, q_in, t, 1, 1)
                for g in range(G):
                    ins = pe.transpose(bb[:, g * P:(g + 1) * P],
                                       qr[:, g, :, :].rearrange("p o d -> p (o d)"), ident)
                ins.then_inc(qT, 1)

            def turn_k(t):
                for b in range(BT):
                    after(pe, k_rot, t, BT, b + 1)
                    after(pe, v_in, t, 4, 2 * b + 2)
                    for g in range(G):
                        ins = pe.transpose((bc, ba)[b][:, g * P:(g + 1) * P],
                                           kr[:, b, g, :, :].rearrange("p o d -> p (o d)"), ident)
                    ins.then_inc(kT, 1)

            def row_scores(t, par, units):
                for n in units:
                    g, b = n // BT, n % BT
                    if n == 0:
                        after(pe, mk_in, t, 1, 1)
                        after(pe, k_hi, t, BT, BT)
                    after(pe, qx, t, G, g + 1)
                    if n >= 2:
                        after(pe, s_max, t, 8, n - 1)
                    else:
                        after(pe, s_max, t - 1, 8, 7 + n)
                    if n == 0:
                        after(pe, kk_in, t - 2, 1, 1)
                    if n == 1:
                        after(pe, rl_in, t - 3, 1, 1)
                    o = bs[n % 2]
                    for p in range(NP):
                        pe.matmul(o[:, p * P:(p + 1) * P], Qx[par][:, g, b, 2 * p:2 * p + 2, :], Kh[par][:, b, g, :],
                                  start=(p == 0), stop=False)
                    pe.matmul(o[:, :].rearrange("p (n k) -> p n k", n=NP)[:, :, 0:S], Idup[:, :],
                              mk2[par][:, b, 0:S].rearrange("p (o k) -> p o k", o=1).to_broadcast([P, NP, S]),
                              start=False, stop=True).then_inc(s_mm, 1)

            def turn_maxima(t):
                after(pe, s_max, t, 8, 8)
                pe.sem_inc(held, 1)
                pe.transpose(bs[0][0:2 * H, 0:P], mx[:, :, :, :, :].rearrange("p b s g n -> p (b s g n)"), ident).then_inc(mT, 1)

            def attend(t, par, g, prev):
                for b in range(BT):
                    if g == 0:
                        after(pe, k_lo, t, BT, BT)
                        after(pe, p_exp, t - 1, 8, 8)
                        if prev:
                            after(pe, mix_step, t - 1, 5 + E0, 5 + E0 - 2 * (1 - b))
                    else:
                        after(pe, p_exp, t, 8, 2 * g + b - 1)
                    o = bt[b]
                    q = Qx[par][:, g, b, :, :]
                    pe.matmul(o[:, :], Kl[par][:, b, g, :], q, start=True, stop=False)
                    pe.matmul(o[:, :], Kh[par][:, b, g, :], q, start=False, stop=False)
                    pe.matmul(o[:, :], mk2[par][:, b, :], Idup[:, 0:S].rearrange("p (o q) -> p o q", o=1).to_broadcast([P, HG, S]),
                              start=False, stop=False)
                    if g == 0:
                        after(pe, m_row, t, BT * 64, BT * 64)
                    pe.matmul(o[:, :], Lm[:, :], mrow[:, b, g * 512:(g + 1) * 512], start=False, stop=True).then_inc(t_mm, 1)

            def values(t, par, g, prev):
                after(pe, p_exp, t, 8, 2 * g + 2)
                if g >= 1:
                    after(pe, o_in, t, 8, 2 * g)
                else:
                    after(pe, o_in, t - 1, 8, 8)
                    after(pe, v_in, t, 4, 4)
                    if prev:
                        after(pe, e_add, t - 1, 1, 1)
                for h in range(HG):
                    ins = pe.matmul(bo[:, h * VW:(h + 1) * VW], Pt[:, g % 2, h, :, :],
                                    Vx[par][:, g * HG + h, :, :, :].rearrange("p b s d -> p (b s d)"), start=True, stop=True)
                ins.then_inc(pv_mm, 1)

            def turn_heads(t, following):
                after(pe, ao_in, t, 2, 2)
                if following:
                    after(pe, k_lo, t + 1, BT, BT)
                transposed(bc, ao, aoT_mm)

            def output(t):
                after(pe, aoT_in, t, 1, 1)
                for c in range(KT):
                    ins = pe.matmul(ba[:, 0:HID], aoT[:, c, :], wo[:, c, :], start=(c == 0), stop=(c == KT - 1))
                ins.then_inc(wo_mm, 1)

            def turn_h2(u):
                after(pe, ln_done[1], u, 1, 1)
                after(pe, p_exp, u, 8, 8)
                transposed(bt[0], h2, h2T_mm)

            def gate_logits(u):
                after(pe, h2T_in, u, 1, 1)
                for c in range(KT):
                    ins = pe.matmul(bt[1][:, 0:E0], h2T[:, c, :], wg0[:, c, :], start=(c == 0), stop=(c == KT - 1))
                ins.then_inc(lg_mm, 1)

            def turn_comb(u):
                after(pe, comb_in, u, 1, 1)
                pe.transpose(bt[1][0:E0, P:2 * P], comb[:, :], ident).then_inc(combT_mm, 1)

            def experts0(u, n):
                if n == 1:
                    after(pe, combT_in, u, 1, 1)
                if n >= 2:
                    after(pe, mix_step, u, 5 + E0, 5 + 2 * (n - 1))
                if n == 0:
                    pe.wait_ge(w0_lo, len(w0_raw))
                    after(pe, h2_hi, u, 1, 1)
                for i, (x, w) in enumerate(((h2h, w0h), (h2h, w0l), (h2l, w0h))):
                    if n == 0 and i == 2:
                        after(pe, h2_lo, u, 1, 1)
                    for c in range(KT):
                        ins = pe.matmul(bt[n % 2][:, :], x[:, c, :], w[:, c, 2 * n:2 * n + 2, :].rearrange("p e n -> p (e n)"),
                                        start=(i == 0 and c == 0), stop=(i == 2 and c == KT - 1))
                ins.then_inc(e_mm, 1)

            def bias0(u):
                after(pe, o_in, u, 8, 8)
                pe.matmul(bo[:, 0:HID], combT[:, :], b0[:, :], start=True, stop=True).then_inc(e_mm, 1)

            def turn_h3(u, following):
                after(pe, ln_done[2], u, 1, 1)
                if following:
                    after(pe, m_lo, u + 1, 1, 1)
                transposed(bs[0], h3, h3T_mm)

            def turn_y(u):
                after(pe, y_in, u, 1, 1)
                for c in range(KT):
                    ins = pe.transpose(bs[1][:, c * P:(c + 1) * P], yy[:, c, :], ident)
                ins.then_inc(yT_mm, 1)

            def turn_h4(u, par):
                after(pe, ln_done[3], u, 1, 1)
                transposed(bs[1], h4[par], h4T_mm)

            def router_logits(u):
                after(pe, h4T_in, u, 1, 1)
                for c in range(KT):
                    ins = pe.matmul(bs[1][:, HID:HID + NE], h4T[:, c, :], wg1[:, c, :], start=(c == 0), stop=(c == KT - 1))
                ins.then_inc(rl_mm, 1)

            turn_hn(0)
            pe.wait_ge(ld_proj, 16 * 3)
            project_q(0)
            for b in range(BT):
                project_kv(0, b)
            turn_q(0)
            turn_k(0)
            pe.wait_ge(prep, 3)
            pe.wait_ge(zeroed, 10)
            pe.wait_ge(mrow_zero, 1)
            row_scores(0, 0, range(4))
            pe.wait_ge(ld_attn, 16 * 3)
            pe.wait_ge(ld_ffn, 16 * 8)

            def tile(t, par, prev2, prev, nxt):
                if nxt:
                    turn_hn(t + 1)
                row_scores(t, par, range(4, 5))
                if nxt:
                    project_q(t + 1)
                if prev:
                    turn_heads(t - 1, True)
                row_scores(t, par, range(5, 6))
                if prev:
                    output(t - 1)
                row_scores(t, par, range(6, 8))
                if nxt:
                    project_kv(t + 1, 0)
                if prev:
                    turn_h2(t - 1)
                turn_maxima(t)
                if prev:
                    gate_logits(t - 1)
                if nxt:
                    turn_q(t + 1)
                    project_kv(t + 1, 1)
                if prev:
                    turn_comb(t - 1)
                    experts0(t - 1, 0)
                    experts0(t - 1, 1)
                if prev2:
                    turn_y(t - 2)
                if prev:
                    experts0(t - 1, 2)
                    experts0(t - 1, 3)
                    bias0(t - 1)
                attend(t, par, 0, prev)
                if prev2:
                    turn_h4(t - 2, par)
                attend(t, par, 1, prev)
                values(t, par, 0, prev)
                if prev2:
                    router_logits(t - 2)
                if prev:
                    turn_h3(t - 1, True)
                if nxt:
                    turn_k(t + 1)
                attend(t, par, 2, prev)
                values(t, par, 1, prev)
                if nxt:
                    row_scores(t + 1, 1 - par, range(1))
                attend(t, par, 3, prev)
                if nxt:
                    row_scores(t + 1, 1 - par, range(1, 2))
                values(t, par, 2, prev)
                if nxt:
                    row_scores(t + 1, 1 - par, range(2, 3))
                values(t, par, 3, prev)
                if nxt:
                    row_scores(t + 1, 1 - par, range(3, 4))

            over_tiles(pe, tile)
            u = NT - 1
            after(pe, rl_in, u - 2, 1, 1)
            turn_y(u - 1)
            turn_heads(u, False)
            turn_h4(u - 1, (u - 1) % 2)
            output(u)
            router_logits(u - 1)
            turn_h2(u)
            gate_logits(u)
            turn_comb(u)
            for n in range(E0 // 2):
                experts0(u, n)
            bias0(u)
            turn_h3(u, False)
            after(pe, rl_in, u - 1, 1, 1)
            turn_y(u)
            turn_h4(u, u % 2)
            router_logits(u)

            pe.wait_ge(used_in, 1)
            u = used[:, :, :].rearrange("p t e -> p (t e)")
            pe.matmul(bt[0][:, 0:NT * NE], CN[:, C_TRI:C_TRI + P], u, start=True, stop=True)
            pe.matmul(bt[0][:, NT * NE:2 * NT * NE], ones[:, :], u, start=True, stop=True).then_inc(rk_mm, 1)
            pe.wait_ge(val_in, 1)
            for i in range(TOPK * NT):
                if i % 4 == 0:
                    pe.wait_ge(oh_in, i // 4 + 1)
                ins = pe.matmul(bt[1][:, 0:3 * NJ], ohp[:, i, :], val[:, i, :, :].rearrange("p k j -> p (k j)"),
                                start=(i == 0), stop=(i == TOPK * NT - 1))
            ins.then_inc(tb_mm, 1)

            def turn_rows(j):
                after(pe, gathered, j, 16, 16)
                after(pe, xT_in, j - 1, 1, 1)
                for c in range(KT):
                    ins = pe.transpose(ba[:, c * P:(c + 1) * P], xg[:, c * P:(c + 1) * P], ident)
                ins.then_inc(xT_mm, 1)

            def expert(j):
                return pe.value_load(ej[0:1, bass.ts(j, 1)], min_val=0, max_val=NE - 1)

            def up(j, e):
                after(pe, xT_in, j, 1, 1)
                for q, o in enumerate((bs[0], bs[1], bt[0], bt[1])):
                    if q % 2 == 0:
                        after(pe, silu, j - 1, 2, q // 2 + 1)
                    else:
                        after(pe, h_in, j - 1, 2, q // 2 + 1)
                    for c in range(KT):
                        ins = pe.matmul(o[:, 0:IH], xgT[:, c, :], w13[:, c, bass.ts(e, 1), q, :].rearrange("p o n -> p (o n)"),
                                        start=(c == 0), stop=(c == KT - 1))
                    ins.then_inc(up_mm, 1)

            def turn_h(j):
                after(pe, h_in, j, 2, 2)
                after(pe, hT_in_a, j - 1, 1, 1)
                after(pe, hT_in_v, j - 1, 1, 1)
                for i in range(IT):
                    o = bb if i < 4 else bc
                    ins = pe.transpose(o[:, (i % 4) * P:(i % 4 + 1) * P], hh[:, i * P:(i + 1) * P], ident)
                    if i == 3:
                        ins.then_inc(hT_mm, 1)
                ins.then_inc(hT_mm, 1)

            def down(j, e):
                after(pe, hT_in_a, j, 1, 1)
                after(pe, hT_in_v, j, 1, 1)
                after(pe, y_sc, j - 1, 1, 1)
                for i in range(IT):
                    k = P if i < IT - 1 else I - (IT - 1) * P
                    ins = pe.matmul(bo[:, 0:HID], hT[0:k, i, :], w2[0:k, i, bass.ts(e, 1), :].rearrange("p o n -> p (o n)"),
                                    start=(i == 0), stop=(i == IT - 1))
                ins.then_inc(y_mm, 1)

            pe.wait_ge(e_of, 1)
            turn_rows(0)
            pe.wait_ge(ld_w13, 16 * KT * NE)
            up(0, expert(0))
            turn_rows(1)
            pe.wait_ge(ld_w2, 16 * 2 * NE)

            def slots(j):
                e_last, e = expert(j - 1), expert(j)
                turn_h(j - 1)
                up(j, e)
                turn_rows(j + 1)
                down(j - 1, e_last)

            slots(1)
            with pe.Fori(2, NJ - 1) as j:
                slots(j)
            e_last, e = expert(NJ - 2), expert(NJ - 1)
            turn_h(NJ - 2)
            up(NJ - 1, e)
            down(NJ - 2, e_last)
            turn_h(NJ - 1)
            down(NJ - 1, e)


def constants():
    import numpy as np
    c = np.zeros((P, C_N), np.float32)
    c[:, C_ID:C_ID + P] = np.eye(P)
    inv = 1.0 / 10000.0 ** (np.arange(0, D, 2, dtype=np.float32) / D)
    emb = np.outer(np.arange(S, dtype=np.float32), inv)
    emb = np.concatenate([emb, emb], -1)
    cos, sin = np.cos(emb).astype(np.float32), np.sin(emb).astype(np.float32)
    sin[:, :D // 2] *= -1
    scale = np.float32(1 / math.sqrt(D))
    c[:, C_COSQ:C_COSQ + D] = np.tile(cos * scale, (2, 1))
    c[:, C_SINQ:C_SINQ + D] = np.tile(sin * scale, (2, 1))
    c[:S, C_COSK:C_COSK + D] = cos
    c[S:, C_COSK:C_COSK + D] = 1
    c[:S, C_SINK:C_SINK + D] = sin
    c[np.arange(P), C_HM + np.arange(P) % S // D] = 1
    c[:, C_EV:C_EV + 8] = 8 - np.arange(8)
    for r in range(4):
        c[r, C_ONE + S * (r % 2):C_ONE + S * (r % 2) + S] = 1
    n = np.arange(P)
    c[:, C_TRI:C_TRI + P] = n[:, None] < n[None, :]
    c[:, C_POS:C_POS + P] = n
    c[:, C_TOK:C_TOK + NT] = n[:, None] + P * np.arange(NT)
    c[:, C_OWN] = B * S + n
    c[:, C_J128:C_J128 + NT] = P * np.arange(NT)
    lut = np.arange(LUT_MIN, 1, dtype=np.float32)
    c[:, C_LUTX:C_LUTX + 129] = lut
    c[:, C_LUT:C_LUT + 129] = (np.exp(lut / np.float32(Q_IN)) * np.float32(Q_OUT)).astype(np.int32)
    return c


def kernel(x, ctx_2048, mask_Bx1xSxS_fk0, g_xattn, g_ffn, L0_xattn_Wq, L0_xattn_Wk, L0_xattn_Wv, L0_xattn_Wo,
           L0_xattn_gate, L0_ffn_wg, L0_ffn_W, L0_ffn_b, L1_xattn_w, L1_xattn_u, L1_ffn_w_gate, L1_ffn_w1, L1_ffn_w2,
           L1_ffn_w3):
    import numpy as np
    import concourse.bacc as bacc
    from concourse.bass_utils import run_bass_kernel_spmd as run

    f = lambda a: np.ascontiguousarray(np.asarray(a))
    gx, gf = np.asarray(g_xattn), np.asarray(g_ffn)
    arrays = {
        "x": f(x), "ctxT": f(np.asarray(ctx_2048).reshape(B * S, HID).T), "mask": f(mask_Bx1xSxS_fk0), "const": constants(),
        "Wq": f(L0_xattn_Wq), "Wkv": f(np.concatenate([L0_xattn_Wk, L0_xattn_Wv], 1)), "Wo": f(L0_xattn_Wo),
        "gates": f(np.stack([gx[0], gf[0], gx[1], gf[1]])), "head_gate": f(np.asarray(L0_xattn_gate).reshape(-1)),
        "wg": f(L0_ffn_wg), "WT": f(np.asarray(L0_ffn_W).transpose(0, 2, 1)), "b": f(L0_ffn_b),
        "w": f(np.asarray(L1_xattn_w).reshape(KT, P).T), "u": f(np.asarray(L1_xattn_u).reshape(KT, P).T), "wgateT": f(np.asarray(L1_ffn_w_gate).T),
        "w13": f(np.stack([np.asarray(w).transpose(0, 2, 1).reshape(NE, HID, 2, IH) for w in (L1_ffn_w1, L1_ffn_w3)], 3)
                 .reshape(NE, HID, 4, IH)),
        "w2T": f(np.asarray(L1_ffn_w2).transpose(0, 2, 1)),
    }
    nc = bacc.Bacc("TRN2", target_bir_lowering=False, num_devices=1)
    A = {n: nc.dram_tensor(f"in_{n}", a.shape, mybir.dt.from_np(a.dtype), kind="ExternalInput").ap() for n, a in arrays.items()}
    out = nc.dram_tensor("out_x", (B * S + P, HID), F32, kind="ExternalOutput").ap()
    H4 = nc.dram_tensor("normed", (B * S, HID), F32, kind="Internal").ap()
    build(nc, A, out, H4)
    r = run(nc, [{f"in_{n}": a for n, a in arrays.items()}], core_ids=[0])
    return r.results[0]["out_x"][0:B * S].reshape(B, S, HID)
```
